# Optimizing a Trainium2 kernel written in Bass

```python
import numpy as np
import jax
import jax.numpy as jnp

def _softmax(x, axis=-1):
    return jax.nn.softmax(x, axis=axis)

def _gelu(x):
    return jax.nn.gelu(x, approximate=True)

def _silu(x):
    return jax.nn.silu(x)

def _sigmoid(x):
    return jax.nn.sigmoid(x)

def _layernorm(x, axis=-1, eps=1e-05):
    m = jnp.mean(x, axis=axis, keepdims=True)
    v = jnp.var(x, axis=axis, keepdims=True)
    return (x - m) / jnp.sqrt(v + eps)

def _scatter_add(tgt, idx, src, axis=0):
    return tgt.at[idx].add(src)

def _segment_sum(src, seg, n):
    return jax.ops.segment_sum(src, seg, n)
kernel_name = 'mk_cond_seq_d4_seqx_r8_60dc20'

def setup_inputs(seed: int=0):
    np.random.seed(seed)
    _w = jnp.asarray

    def _rec_inputs():
        import jax
        import jax.numpy as jnp
        _rk = jax.random.key(seed)
        x = -0.0002928 + 1 * jax.random.normal(jax.random.fold_in(_rk, 1), (32, 32, 128), jnp.float32)
        _lenS = 32 - jax.random.randint(jax.random.fold_in(_rk, 7), (32,), 0, max(1, 32 // 4) + 1, jnp.int32)
        _lenS2 = 32 - jax.random.randint(jax.random.fold_in(_rk, 8), (32,), 0, max(1, 32 // 4) + 1, jnp.int32)
        cond_1024 = 0.0061147 + 1.02565 * jax.random.normal(jax.random.fold_in(_rk, 11), (32, 128), jnp.float32)
        return (x, cond_1024)
    x, cond_1024 = _rec_inputs()

    def _L0_cond_setup():
        import jax, jax.numpy as jnp
        import numpy as np
        EPS = 1e-05

        def _sln(h, w, ln_g, ln_b, Wg, bg, Wb, bb):
            mu = jnp.mean(h, axis=-1, keepdims=True)
            var = jnp.mean((h - mu) ** 2, axis=-1, keepdims=True)
            ln = (h - mu) / jnp.sqrt(var + EPS) * ln_g + ln_b
            gamma = (w @ Wg.T + bg)[:, None, :]
            beta = (w @ Wb.T + bb)[:, None, :]
            return gamma * ln + beta
        key = jax.random.key(seed)
        ks = jax.random.split(key, 20)
        B, N, D = (4, 128, 128)
        F = 4 * D
        s = lambda fan: 1.0 / np.sqrt(fan)
        inp = {'hidden': jax.random.normal(ks[0], (B, N, D), jnp.float32), 'w': jax.random.normal(ks[1], (B, D), jnp.float32), 'ln_g': jnp.ones((D,), jnp.float32), 'ln_b': jnp.zeros((D,), jnp.float32), 'Wg': jax.random.normal(ks[2], (D, D), jnp.float32) * s(D), 'bg': jnp.zeros((D,), jnp.float32), 'Wb': jax.random.normal(ks[3], (D, D), jnp.float32) * s(D), 'bb': jnp.zeros((D,), jnp.float32), 'Wqkv': jax.random.normal(ks[4], (3 * D, D), jnp.float32) * s(D), 'bqkv': jnp.zeros((3 * D,), jnp.float32), 'Wp': jax.random.normal(ks[5], (D, D), jnp.float32) * s(D), 'bp': jnp.zeros((D,), jnp.float32), 'W1': jax.random.normal(ks[6], (F, D), jnp.float32) * s(D), 'b1': jnp.zeros((F,), jnp.float32), 'W2': jax.random.normal(ks[7], (D, F), jnp.float32) * s(F), 'b2': jnp.zeros((D,), jnp.float32), 'num_heads': 16}
        return inp
    _L0_cond_all = _L0_cond_setup()
    _L0_cond_in = {k: v for k, v in _L0_cond_all.items() if k in ('ln_g', 'ln_b', 'Wg', 'bg', 'Wb', 'bb', 'Wqkv', 'bqkv', 'Wp', 'bp', 'W1', 'b1', 'W2', 'b2')}
    del _L0_cond_all

    def _L1_cond_setup():
        import jax, jax.numpy as jnp
        import numpy as np
        FEAT = 128
        ADA = 128
        INTER = 128
        RANK = 8
        EPS = 1e-05

        def _layernorm(a, g, b):
            mu = jnp.mean(a, axis=-1, keepdims=True)
            var = jnp.mean(jnp.square(a - mu), axis=-1, keepdims=True)
            return (a - mu) * jax.lax.rsqrt(var + EPS) * g + b
        key = jax.random.key(seed)
        ks = jax.random.split(key, 6)
        B, T = (16, 128)
        x = jax.random.normal(ks[0], (B, T, FEAT), dtype=jnp.float32)
        ada_emb = jax.random.normal(ks[1], (B, ADA), dtype=jnp.float32)
        W1 = jax.random.normal(ks[2], (ADA, INTER), dtype=jnp.float32) / np.sqrt(ADA)
        b1 = jnp.zeros((INTER,), dtype=jnp.float32)
        W2 = jax.random.normal(ks[3], (INTER, FEAT * RANK * 4), dtype=jnp.float32) * (0.1 / np.sqrt(INTER))
        b2 = jnp.zeros((FEAT * RANK * 4,), dtype=jnp.float32)
        ln_g = jnp.ones((ADA,), dtype=jnp.float32)
        ln_b = jnp.zeros((ADA,), dtype=jnp.float32)
        return {'x': x, 'ada_emb': ada_emb, 'ln_g': ln_g, 'ln_b': ln_b, 'W1': W1, 'b1': b1, 'W2': W2, 'b2': b2}
    _L1_cond_all = _L1_cond_setup()
    _L1_cond_in = {k: v for k, v in _L1_cond_all.items() if k in ('ln_g', 'ln_b', 'W1', 'b1', 'W2', 'b2')}
    del _L1_cond_all

    def _L2_cond_setup():
        import jax, jax.numpy as jnp
        import numpy as np
        EPS = 1e-12

        def rmsnorm(x, g, dim):
            n = jnp.maximum(jnp.linalg.norm(x, axis=-1, keepdims=True), EPS)
            return x / n * dim ** 0.5 * g

        def modulate(x, scale, shift):
            return x * (1.0 + scale[:, None, :]) + shift[:, None, :]
        key = jax.random.key(seed)
        ks = jax.random.split(key, 12)
        B, T, D, H = (8, 128, 128, 16)
        Dm = 4 * D
        s = 0.02
        inp = {'x': jax.random.normal(ks[0], (B, T, D), jnp.float32), 'c': jax.random.normal(ks[1], (B, D), jnp.float32), 'g1': jnp.ones((1,), jnp.float32), 'g2': jnp.ones((1,), jnp.float32), 'gq': jnp.ones((1,), jnp.float32), 'gk': jnp.ones((1,), jnp.float32), 'Wqkv': jax.random.normal(ks[2], (3 * D, D), jnp.float32) * s, 'bqkv': jnp.zeros((3 * D,), jnp.float32), 'Wproj': jax.random.normal(ks[3], (D, D), jnp.float32) * s, 'bproj': jnp.zeros((D,), jnp.float32), 'Wfc1': jax.random.normal(ks[4], (Dm, D), jnp.float32) * s, 'bfc1': jnp.zeros((Dm,), jnp.float32), 'Wfc2': jax.random.normal(ks[5], (D, Dm), jnp.float32) * s, 'bfc2': jnp.zeros((D,), jnp.float32), 'Wada': jax.random.normal(ks[6], (6 * D, D), jnp.float32) * s, 'bada': jnp.zeros((6 * D,), jnp.float32)}
        return inp
    _L2_cond_all = _L2_cond_setup()
    _L2_cond_in = {k: v for k, v in _L2_cond_all.items() if k in ('g1', 'g2', 'gq', 'gk', 'Wqkv', 'bqkv', 'Wproj', 'bproj', 'Wfc1', 'bfc1', 'Wfc2', 'bfc2', 'Wada', 'bada')}
    del _L2_cond_all

    def _L3_cond_setup():
        import jax, jax.numpy as jnp
        import numpy as np
        B, N, D = (2, 256, 128)
        H, HD = (16, 64)
        E, DD = (8, 512)
        EPS = 1e-05

        def _ln(x, g, b):
            m = jnp.mean(x, axis=-1, keepdims=True)
            v = jnp.var(x, axis=-1, keepdims=True)
            return (x - m) * jax.lax.rsqrt(v + EPS) * g + b
        key = jax.random.key(seed)
        ks = jax.random.split(key, 16)
        s = 0.02
        return {'x': jax.random.normal(ks[0], (B, N, D), jnp.float32), 't': jax.random.normal(ks[1], (B, 1, D), jnp.float32), 'W_ada': jax.random.normal(ks[2], (D, D), jnp.float32) * s, 'b_ada': jnp.zeros((D,), jnp.float32), 'ln1_g': jnp.ones((D,), jnp.float32), 'ln1_b': jnp.zeros((D,), jnp.float32), 'Wqkv': jax.random.normal(ks[3], (3 * H * HD, D), jnp.float32) * s, 'qn_g': jnp.ones((HD,), jnp.float32), 'qn_b': jnp.zeros((HD,), jnp.float32), 'kn_g': jnp.ones((HD,), jnp.float32), 'kn_b': jnp.zeros((HD,), jnp.float32), 'Wout': jax.random.normal(ks[4], (D, H * HD), jnp.float32) * s, 'mlp_g': jnp.ones((D,), jnp.float32), 'mlp_b': jnp.zeros((D,), jnp.float32), 'Wgate': jax.random.normal(ks[5], (E, D), jnp.float32) * s, 'fc1s': jax.random.normal(ks[6], (E, DD, D), jnp.float32) * s, 'b1s': jnp.zeros((E, DD), jnp.float32), 'fc2s': jax.random.normal(ks[7], (E, D, DD), jnp.float32) * s, 'b2s': jnp.zeros((E, D), jnp.float32)}
    _L3_cond_all = _L3_cond_setup()
    _L3_cond_in = {k: v for k, v in _L3_cond_all.items() if k in ('W_ada', 'b_ada', 'ln1_g', 'ln1_b', 'Wqkv', 'qn_g', 'qn_b', 'kn_g', 'kn_b', 'Wout', 'mlp_g', 'mlp_b', 'Wgate', 'fc1s', 'b1s', 'fc2s', 'b2s')}
    del _L3_cond_all
    return {'x': x, 'cond_1024': cond_1024, 'L0_cond_ln_g': _L0_cond_in['ln_g'], 'L0_cond_ln_b': _L0_cond_in['ln_b'], 'L0_cond_Wg': _L0_cond_in['Wg'], 'L0_cond_bg': _L0_cond_in['bg'], 'L0_cond_Wb': _L0_cond_in['Wb'], 'L0_cond_bb': _L0_cond_in['bb'], 'L0_cond_Wqkv': _L0_cond_in['Wqkv'], 'L0_cond_bqkv': _L0_cond_in['bqkv'], 'L0_cond_Wp': _L0_cond_in['Wp'], 'L0_cond_bp': _L0_cond_in['bp'], 'L0_cond_W1': _L0_cond_in['W1'], 'L0_cond_b1': _L0_cond_in['b1'], 'L0_cond_W2': _L0_cond_in['W2'], 'L0_cond_b2': _L0_cond_in['b2'], 'L1_cond_ln_g': _L1_cond_in['ln_g'], 'L1_cond_ln_b': _L1_cond_in['ln_b'], 'L1_cond_W1': _L1_cond_in['W1'], 'L1_cond_b1': _L1_cond_in['b1'], 'L1_cond_W2': _L1_cond_in['W2'], 'L1_cond_b2': _L1_cond_in['b2'], 'L2_cond_g1': _L2_cond_in['g1'], 'L2_cond_g2': _L2_cond_in['g2'], 'L2_cond_gq': _L2_cond_in['gq'], 'L2_cond_gk': _L2_cond_in['gk'], 'L2_cond_Wqkv': _L2_cond_in['Wqkv'], 'L2_cond_bqkv': _L2_cond_in['bqkv'], 'L2_cond_Wproj': _L2_cond_in['Wproj'], 'L2_cond_bproj': _L2_cond_in['bproj'], 'L2_cond_Wfc1': _L2_cond_in['Wfc1'], 'L2_cond_bfc1': _L2_cond_in['bfc1'], 'L2_cond_Wfc2': _L2_cond_in['Wfc2'], 'L2_cond_bfc2': _L2_cond_in['bfc2'], 'L2_cond_Wada': _L2_cond_in['Wada'], 'L2_cond_bada': _L2_cond_in['bada'], 'L3_cond_W_ada': _L3_cond_in['W_ada'], 'L3_cond_b_ada': _L3_cond_in['b_ada'], 'L3_cond_ln1_g': _L3_cond_in['ln1_g'], 'L3_cond_ln1_b': _L3_cond_in['ln1_b'], 'L3_cond_Wqkv': _L3_cond_in['Wqkv'], 'L3_cond_qn_g': _L3_cond_in['qn_g'], 'L3_cond_qn_b': _L3_cond_in['qn_b'], 'L3_cond_kn_g': _L3_cond_in['kn_g'], 'L3_cond_kn_b': _L3_cond_in['kn_b'], 'L3_cond_Wout': _L3_cond_in['Wout'], 'L3_cond_mlp_g': _L3_cond_in['mlp_g'], 'L3_cond_mlp_b': _L3_cond_in['mlp_b'], 'L3_cond_Wgate': _L3_cond_in['Wgate'], 'L3_cond_fc1s': _L3_cond_in['fc1s'], 'L3_cond_b1s': _L3_cond_in['b1s'], 'L3_cond_fc2s': _L3_cond_in['fc2s'], 'L3_cond_b2s': _L3_cond_in['b2s']}

def reference(x, cond_1024, L0_cond_ln_g, L0_cond_ln_b, L0_cond_Wg, L0_cond_bg, L0_cond_Wb, L0_cond_bb, L0_cond_Wqkv, L0_cond_bqkv, L0_cond_Wp, L0_cond_bp, L0_cond_W1, L0_cond_b1, L0_cond_W2, L0_cond_b2, L1_cond_ln_g, L1_cond_ln_b, L1_cond_W1, L1_cond_b1, L1_cond_W2, L1_cond_b2, L2_cond_g1, L2_cond_g2, L2_cond_gq, L2_cond_gk, L2_cond_Wqkv, L2_cond_bqkv, L2_cond_Wproj, L2_cond_bproj, L2_cond_Wfc1, L2_cond_bfc1, L2_cond_Wfc2, L2_cond_bfc2, L2_cond_Wada, L2_cond_bada, L3_cond_W_ada, L3_cond_b_ada, L3_cond_ln1_g, L3_cond_ln1_b, L3_cond_Wqkv, L3_cond_qn_g, L3_cond_qn_b, L3_cond_kn_g, L3_cond_kn_b, L3_cond_Wout, L3_cond_mlp_g, L3_cond_mlp_b, L3_cond_Wgate, L3_cond_fc1s, L3_cond_b1s, L3_cond_fc2s, L3_cond_b2s):
    import jax
    import jax.numpy as jnp

    def _L0_cond_ref(hidden, w, ln_g, ln_b, Wg, bg, Wb, bb, Wqkv, bqkv, Wp, bp, W1, b1, W2, b2, num_heads):
        import jax, jax.numpy as jnp
        import numpy as np
        EPS = 1e-05

        def _sln(h, w, ln_g, ln_b, Wg, bg, Wb, bb):
            mu = jnp.mean(h, axis=-1, keepdims=True)
            var = jnp.mean((h - mu) ** 2, axis=-1, keepdims=True)
            ln = (h - mu) / jnp.sqrt(var + EPS) * ln_g + ln_b
            gamma = (w @ Wg.T + bg)[:, None, :]
            beta = (w @ Wb.T + bb)[:, None, :]
            return gamma * ln + beta
        B, N, D = hidden.shape
        hd = D // num_heads
        h = _sln(hidden, w, ln_g, ln_b, Wg, bg, Wb, bb)
        qkv = (h @ Wqkv.T + bqkv).reshape(B, N, num_heads, hd, 3)
        q = jnp.moveaxis(qkv[..., 0], 2, 1)
        k = jnp.moveaxis(qkv[..., 1], 2, 1)
        v = jnp.moveaxis(qkv[..., 2], 2, 1)
        energy = jnp.einsum('bhqd,bhkd->bhqk', q, k)
        att = jax.nn.softmax(energy, axis=-1) / D ** 0.5
        out = jnp.einsum('bhqk,bhkd->bhqd', att, v)
        out = jnp.moveaxis(out, 1, 2).reshape(B, N, D)
        out = out @ Wp.T + bp
        h1 = out + hidden
        h2 = _sln(h1, w, ln_g, ln_b, Wg, bg, Wb, bb)
        return h2 + h1

    def _L1_cond_ref(x, ada_emb, ln_g, ln_b, W1, b1, W2, b2):
        import jax, jax.numpy as jnp
        import numpy as np
        FEAT = 128
        ADA = 128
        INTER = 128
        RANK = 8
        EPS = 1e-05

        def _layernorm(a, g, b):
            mu = jnp.mean(a, axis=-1, keepdims=True)
            var = jnp.mean(jnp.square(a - mu), axis=-1, keepdims=True)
            return (a - mu) * jax.lax.rsqrt(var + EPS) * g + b
        B, T, D = x.shape
        h = jax.nn.gelu(_layernorm(ada_emb, ln_g, ln_b) @ W1 + b1, approximate=False)
        w = h @ W2 + b2
        a1, bb1, a2, bb2 = jnp.split(w, 4, axis=-1)
        a1 = a1.reshape(B, D, RANK)
        bb1 = bb1.reshape(B, D, RANK)
        a2 = a2.reshape(B, D, RANK)
        bb2 = bb2.reshape(B, D, RANK)
        y = jnp.einsum('btd,bdr->btr', x, a1)
        y = jnp.einsum('btr,bdr->btd', y, bb1)
        y = jax.nn.gelu(y, approximate=False)
        y = jnp.einsum('btd,bdr->btr', y, a2)
        y = jnp.einsum('btr,bdr->btd', y, bb2)
        return y + x

    def _L2_cond_ref(x, c, g1, g2, gq, gk, Wqkv, bqkv, Wproj, bproj, Wfc1, bfc1, Wfc2, bfc2, Wada, bada):
        import jax, jax.numpy as jnp
        import numpy as np
        EPS = 1e-12

        def rmsnorm(x, g, dim):
            n = jnp.maximum(jnp.linalg.norm(x, axis=-1, keepdims=True), EPS)
            return x / n * dim ** 0.5 * g

        def modulate(x, scale, shift):
            return x * (1.0 + scale[:, None, :]) + shift[:, None, :]
        B, T, D = x.shape
        H = 16
        hd = D // H
        ada = jax.nn.silu(c) @ Wada.T + bada
        shift_msa, scale_msa, gate_msa, shift_mlp, scale_mlp, gate_mlp = jnp.split(ada, 6, axis=-1)
        h = modulate(rmsnorm(x, g1, D), scale_msa, shift_msa)
        qkv = h @ Wqkv.T + bqkv
        qkv = qkv.reshape(B, T, 3, H, hd).transpose(2, 0, 3, 1, 4)
        q, k, v = (qkv[0], qkv[1], qkv[2])
        q = rmsnorm(q, gq, hd) * hd ** (-0.5)
        k = rmsnorm(k, gk, hd)
        attn = jax.nn.softmax(jnp.einsum('bhqd,bhkd->bhqk', q, k), axis=-1)
        o = jnp.einsum('bhqk,bhkd->bhqd', attn, v)
        o = o.transpose(0, 2, 1, 3).reshape(B, T, D)
        o = o @ Wproj.T + bproj
        x = x + gate_msa[:, None, :] * o
        h = modulate(rmsnorm(x, g2, D), scale_mlp, shift_mlp)
        h = jax.nn.gelu(h @ Wfc1.T + bfc1, approximate=True)
        h = h @ Wfc2.T + bfc2
        x = x + gate_mlp[:, None, :] * h
        return x

    def _L3_cond_ref(x, t, W_ada, b_ada, ln1_g, ln1_b, Wqkv, qn_g, qn_b, kn_g, kn_b, Wout, mlp_g, mlp_b, Wgate, fc1s, b1s, fc2s, b2s):
        import jax, jax.numpy as jnp
        import numpy as np
        B, N, D = (2, 256, 128)
        H, HD = (16, 64)
        E, DD = (8, 512)
        EPS = 1e-05

        def _ln(x, g, b):
            m = jnp.mean(x, axis=-1, keepdims=True)
            v = jnp.var(x, axis=-1, keepdims=True)
            return (x - m) * jax.lax.rsqrt(v + EPS) * g + b
        b, n, d = x.shape
        shift = jax.nn.silu(t) @ W_ada.T + b_ada
        h = _ln(x, ln1_g, ln1_b) + shift
        qkv = (h @ Wqkv.T).reshape(b, n, 3, H, HD)
        q = _ln(qkv[:, :, 0].transpose(0, 2, 1, 3), qn_g, qn_b)
        k = _ln(qkv[:, :, 1].transpose(0, 2, 1, 3), kn_g, kn_b)
        v = qkv[:, :, 2].transpose(0, 2, 1, 3)
        scores = jnp.einsum('bhnd,bhmd->bhnm', q, k) / jnp.sqrt(jnp.float32(HD))
        attn = jax.nn.softmax(scores, axis=-1)
        o = jnp.einsum('bhnm,bhmd->bhnd', attn, v)
        o = o.transpose(0, 2, 1, 3).reshape(b, n, H * HD)
        x = x + o @ Wout.T
        tok = x.reshape(-1, d)
        bs = tok.shape[0]
        gate = jax.nn.softmax(tok @ Wgate.T, axis=-1)
        k_cap = bs // E
        vals, idx = jax.lax.top_k(gate.T, k_cap)
        idx_flat = idx.T.reshape(-1)
        w = vals.T
        g = _ln(tok[idx_flat], mlp_g, mlp_b).reshape(k_cap, E, d)
        y = jnp.einsum('ked,ehd->keh', g, fc1s) + b1s
        y = jax.nn.gelu(y, approximate=True)
        y = jnp.einsum('keh,edh->ked', y, fc2s) + b2s
        y = y * w[..., None]
        tok = tok.at[idx_flat].add(y.reshape(-1, d))
        return tok.reshape(x.shape)
    x = _L0_cond_ref(x, cond_1024, L0_cond_ln_g, L0_cond_ln_b, L0_cond_Wg, L0_cond_bg, L0_cond_Wb, L0_cond_bb, L0_cond_Wqkv, L0_cond_bqkv, L0_cond_Wp, L0_cond_bp, L0_cond_W1, L0_cond_b1, L0_cond_W2, L0_cond_b2, 16)
    x = _L1_cond_ref(x, cond_1024, L1_cond_ln_g, L1_cond_ln_b, L1_cond_W1, L1_cond_b1, L1_cond_W2, L1_cond_b2)
    x = _L2_cond_ref(x, cond_1024, L2_cond_g1, L2_cond_g2, L2_cond_gq, L2_cond_gk, L2_cond_Wqkv, L2_cond_bqkv, L2_cond_Wproj, L2_cond_bproj, L2_cond_Wfc1, L2_cond_bfc1, L2_cond_Wfc2, L2_cond_bfc2, L2_cond_Wada, L2_cond_bada)
    x = _L3_cond_ref(x, cond_1024[:, None, :], L3_cond_W_ada, L3_cond_b_ada, L3_cond_ln1_g, L3_cond_ln1_b, L3_cond_Wqkv, L3_cond_qn_g, L3_cond_qn_b, L3_cond_kn_g, L3_cond_kn_b, L3_cond_Wout, L3_cond_mlp_g, L3_cond_mlp_b, L3_cond_Wgate, L3_cond_fc1s, L3_cond_b1s, L3_cond_fc2s, L3_cond_b2s)
    return x

_drawn_inputs = setup_inputs


def setup_inputs(seed=0):
    import zlib

    import numpy as np

    out = dict(_drawn_inputs(seed))
    spreads = {'L0_cond_ln_g': (1.0, 0.2),
     'L0_cond_ln_b': (0.0, 0.1),
     'L0_cond_bg': (0.0, 0.1),
     'L0_cond_bb': (0.0, 0.1),
     'L0_cond_bqkv': (0.0, 0.8),
     'L0_cond_bp': (0.0, 0.1),
     'L0_cond_b1': (0.0, 0.1),
     'L0_cond_b2': (0.0, 0.1),
     'L1_cond_ln_g': (1.0, 0.2),
     'L1_cond_ln_b': (0.0, 0.583),
     'L1_cond_b1': (0.0, 0.478),
     'L1_cond_b2': (0.0, 0.1),
     'L2_cond_bqkv': (0.0, 0.8),
     'L2_cond_bproj': (0.0, 0.774),
     'L2_cond_bfc1': (0.0, 0.8),
     'L2_cond_bfc2': (0.0, 0.8),
     'L2_cond_bada': (0.0, 0.8),
     'L3_cond_b_ada': (0.0, 0.8),
     'L3_cond_ln1_g': (1.0, 0.6),
     'L3_cond_ln1_b': (0.0, 0.8),
     'L3_cond_qn_g': (1.0, 0.6),
     'L3_cond_qn_b': (0.0, 0.8),
     'L3_cond_kn_g': (1.0, 0.6),
     'L3_cond_kn_b': (0.0, 0.8),
     'L3_cond_mlp_g': (1.0, 0.6),
     'L3_cond_mlp_b': (0.0, 0.8),
     'L3_cond_b1s': (0.0, 0.8),
     'L3_cond_b2s': (0.0, 0.641)}
    factors = {'L2_cond_Wqkv': 8.0,
     'L2_cond_Wproj': 8.0,
     'L2_cond_Wfc1': 8.0,
     'L2_cond_Wfc2': 8.0,
     'L2_cond_Wada': 4.534,
     'L3_cond_W_ada': 4.888,
     'L3_cond_Wgate': 4.122,
     'L3_cond_fc1s': 8.0,
     'L3_cond_fc2s': 7.424}
    for name, (base, spread) in spreads.items():
        noise = np.random.default_rng([zlib.crc32(name.encode()), seed]).standard_normal(out[name].shape)
        drawn = base * np.exp(spread * noise) if base else spread * noise
        out[name] = jnp.asarray(drawn.astype(out[name].dtype))
    for name, factor in factors.items():
        out[name] = (out[name] * factor).astype(out[name].dtype)
    return out
```

```python
import math
from contextlib import ExitStack

import numpy as np

import concourse.bass as bass
from concourse import mybir

F32 = mybir.dt.float32
BF16 = mybir.dt.bfloat16
I32 = mybir.dt.int32
ALU = mybir.AluOpType
ACT = mybir.ActivationFunctionType
AX_X = mybir.AxisListType.X

P = 128
B, N, D = 32, 32, 128
TOK = B * N
HALF = TOK // 2
NT = TOK // P
TH = NT // 2
BT = P // N
BH = B // 2
NH, HD = 16, 8
NG = 4
VW = HD + 1
RANK = 8
FF = 512
NC = FF // P
NU = NT
H3, HD3 = 16, 64
C3 = H3 * HD3 // P
W3 = H3 * HD3
E = 8
CAP = TOK // E
TE = NT * E
EPS = 1e-5
EPS_N = 1e-12
LN_SCALE = 2.0 ** 24
BITS = 30

VEC = ["l0_bg", "l0_bb", "l0_lng", "l0_lnb", "l0_bq", "l0_bk", "l0_bv", "l0_bp",
       "l1_lng", "l1_lnb", "l1_b1",
       "l2_g1", "l2_g2", "l2_gq", "l2_gk", "l2_bq", "l2_bk", "l2_bv", "l2_bproj", "l2_bfc2",
       "l2_bfc1_0", "l2_bfc1_1", "l2_bfc1_2", "l2_bfc1_3",
       "l2_bada_0", "l2_bada_1", "l2_bada_2", "l2_bada_3", "l2_bada_4", "l2_bada_5",
       "l3_bada", "l3_ln1g", "l3_ln1b", "l3_qg", "l3_qb", "l3_kg", "l3_kb", "l3_mg", "l3_mb",
       "mask_0", "mask_1", "mask_2", "mask_3"]
VCOL = {n: i for i, n in enumerate(VEC)}
NV = len(VEC)


def build(nc, xT, condT, vec, w0, consts, w1, w2, w3, wm1, wm2, b1s, b2s, l1b2, bits, tril, out, layers=4):
    ctx = ExitStack()
    with ctx:
        def sb(name, cols, dt=F32, parts=P):
            return ctx.enter_context(nc.sbuf_tensor(name, [parts, cols], dt))

        sems = {}

        def sem(name):
            if name not in sems:
                sems[name] = ctx.enter_context(nc.semaphore(name))
            return sems[name]

        PS = ctx.enter_context(nc.psum_tensor("PS", [P, 8, 512], F32))

        XA = sb("XA", TOK)
        XB = sb("XB", TOK)
        CD = sb("CD", P)
        V = sb("V", NV)
        W0 = sb("W0", 6 * P)
        CO = sb("CO", 6 * P + BH)
        W1 = sb("W1", P + 4 * RANK * P)
        W1B = sb("W1B", 4 * RANK)
        W2 = sb("W2", 3 * P + P + FF + FF + 6 * P)
        W3S = sb("W3S", P + 3 * W3 + W3 + E)
        FC1 = W1[:, P:P + E * FF]
        FC2 = sb("FC2", E * FF)
        B1 = sb("B1", E * NC)
        B2 = sb("B2", E * P)
        BIT = sb("BIT", BITS, I32, TE)
        TRI = sb("TRI", 2 * TE, F32, TE)

        ident = CO[:, 0:P]
        centre = CO[:, P:2 * P]
        mean_m = CO[:, 2 * P:3 * P]
        mean8 = CO[:, 3 * P:4 * P]
        iota1 = CO[:, 4 * P:5 * P]
        bmask = CO[:, 6 * P:6 * P + BH]

        def vcol(name, a=0, b=P):
            return V[a:b, VCOL[name]:VCOL[name] + 1]

        WK = sb("WK", 4 * TOK)
        T_, SQ, RS, HN = (WK[:, i * TOK:(i + 1) * TOK] for i in range(4))
        QT = sb("QT", TOK)
        AR1 = sb("AR1", 8 * TOK)
        AR2 = sb("AR2", 8 * TOK)
        KBD = AR1[:, 0:4 * TOK].rearrange("p (h n) -> p h n", h=NG)
        HID = AR1[:, 4 * TOK:8 * TOK].rearrange("p (c n) -> p c n", c=NC)
        QK3 = AR1[:, 4 * TOK:8 * TOK].rearrange("p (b s c n) -> p b s c n", b=2, s=2, c=C3)
        VBD = AR2[:, 0:NT * NH * BT * VW].rearrange("p (t h b d) -> p t h b d", t=NT, h=NH, b=BT)
        V3 = AR2[:, 5120:5120 + 2 * W3].rearrange("p (b n) -> p b n", b=2)
        OH = AR1[:, :].rearrange("p (t n) -> p t n", t=NT)
        OT = AR2[:, :].rearrange("p (e t n) -> p e t n", e=E, t=NT)
        PTB = sb("PTB", 2 * H3 * P)
        PTB3 = PTB[:, :].rearrange("p (b h n) -> p b h n", b=2, h=H3)
        EX = sb("EX", 2 * 512)
        EXB = EX[:, :].rearrange("p (b n) -> p b n", b=2)
        PT = sb("PT", 2 * 512)
        PTt = PT[:, :].rearrange("p (b n) -> p b n", b=2)
        MX = sb("MX", 2 * NH)
        REC = sb("REC", 2 * NH)
        ON = sb("ON", 2 * P)
        OA = sb("OA", TOK)
        O3 = OA[:, :].rearrange("p (c n) -> p c n", c=C3)
        ST = sb("ST", 4 * 2 * H3)
        EPSC = sb("EPSC", 4)

        CN = sb("CN", 6 * P)
        HC = sb("HC", P)
        GG = sb("GG", B)
        GB = sb("GB", B)
        GM = sb("GM", B)
        AW = sb("AW", 4 * B * RANK)
        AW4 = AW[:, :].rearrange("p (w b r) -> p w b r", w=4, b=B)
        BTT = sb("BTT", 4 * P)
        SC = sb("SC", P)
        ADA = sb("ADA", 6 * B)
        ADA6 = ADA[:, :].rearrange("p (s b) -> p s b", s=6)
        SH3 = sb("SH3", B)
        BP = sb("BP", 8)
        KM = sb("KM", 16)

        XT = T_.rearrange("p (t d) -> p t d", t=NT)
        XN = HN.rearrange("p (t d) -> p t d", t=NT)
        XG = SQ
        Y = RS.rearrange("p (e d) -> p e d", e=E)
        HS = EX[:, :]
        GT = sb("GT", 3 * TE)
        GE = QT[0:TE, 0:6 * P]
        JK = QT[0:TE, 6 * P:7 * P]
        CT = sb("CT", 16, F32, TE)
        CI = sb("CI", 4, I32, TE)
        SM = sb("SM", TE)
        MS = sb("MS", 64)
        OUT = XB[:, :]

        def half(ap, hf):
            return ap[:, hf * HALF:(hf + 1) * HALF]

        def bview(ap):
            return ap.rearrange("p (b n) -> p b n", b=BH)

        def bb(ap, hf):
            return ap[:, hf * BH:(hf + 1) * BH].unsqueeze(2).broadcast_to([P, BH, N])

        def bank(i):
            return PS[:, i, :]

        NORM_BANKS = {(0, 0): (0, 2), (0, 1): (1, 3), (1, 0): (2, 4), (1, 1): (3, 5),
                      (2, 0): (None, 2), (2, 1): (None, 3), (3, 0): (None, 2), (3, 1): (None, 3),
                      (4, 0): (2, 4), (4, 1): (3, 5)}

        def av_out(u):
            return PS[:, u % 2, 0:2 * BT * 2 * VW].rearrange("p (i b g d) -> p i b g d", i=2, b=BT, g=2)

        block = ctx.enter_context(nc.Block())

        @block.sync
        def _(sp):
            sp.dma_start(CD[:, :], condT).then_inc(sem("ld_first"), 16)
            sp.dma_start(V[:, :], vec).then_inc(sem("ld_first"), 16)
            sp.dma_start(CO[:, :], consts).then_inc(sem("ld_first"), 16)
            sp.dma_start(XA[:, :], xT).then_inc(sem("ld_x"), 16)
            sp.dma_start(W0[:, :], w0).then_inc(sem("ld_w0"), 16)
            sp.dma_start(W2[:, :], w2).then_inc(sem("ld_w2"), 16)
            sp.dma_start(W1[:, :], w1).then_inc(sem("ld_w1"), 16)
            sp.dma_start(W1B[:, :], l1b2).then_inc(sem("ld_w1"), 16)
            sp.dma_start(W3S[:, :], w3).then_inc(sem("ld_w3"), 16)
            sp.dma_start(FC2[:, :], wm2).then_inc(sem("ld_m"), 16)
            sp.dma_start(B1[:, :], b1s).then_inc(sem("ld_m"), 16)
            sp.dma_start(B2[:, :], b2s.partition_broadcast(P)).then_inc(sem("ld_m"), 16)
            sp.dma_start(BIT[:, :], bits).then_inc(sem("ld_m"), 16)
            sp.dma_start(TRI[:, :], tril).then_inc(sem("ld_m"), 16)
            sp.wait_ge(sem("w_low"), 4)
            sp.dma_start(FC1, wm1).then_inc(sem("ld_m"), 16)
            if layers < 4:
                sp.wait_ge(sem("x_done"), 2 * layers)
                sp.dma_start(out, (XB if layers % 2 else XA)[:, :]).then_inc(sem("stored"), 16)
                sp.wait_ge(sem("stored"), 16)
                sp.wait_ge(sem("ld_m"), 96)
            else:
                for t in range(NT):
                    sp.wait_ge(sem("out_tile"), t + 1)
                    sp.dma_start(out[t * P:(t + 1) * P, :], OUT[:, t * P:(t + 1) * P]).then_inc(sem("stored"), 16)
                sp.wait_ge(sem("stored"), 16 * NT)

        @block.gpsimd
        def _(pool):
            nc.gpsimd.memset(EPSC[:, 0:1], EPS).then_inc(sem("eps_set"), 1)
            nc.gpsimd.memset(EPSC[:, 1:2], 0.5 * math.log(LN_SCALE)).then_inc(sem("eps_set"), 1)
            nc.gpsimd.memset(EPSC[:, 2:3], 0.0).then_inc(sem("eps_set"), 1)
            nc.gpsimd.memset(AR2[:, 0:NT * NH * BT * VW], 0.0).then_inc(sem("vbd_zero"), 1)
            pool.wait_ge(sem("vbd_zero"), 1)
            for b in range(BT):
                nc.gpsimd.memset(VBD[32 * b:32 * b + 32, :, :, b, HD:VW].rearrange("p t h d -> p (t h) d"), 1.0).then_inc(sem("vbd_ones"), 1)
                pool.wait_ge(sem("vbd_ones"), b + 1)
            nc.gpsimd.memset(PTB[:, :], 0.0).then_inc(sem("ptb_zero"), 1)

        def second(pe, e):
            pe.wait_ge(sem("e_h"), e + 1)
            if e >= 2:
                pe.wait_ge(sem("e_y"), e - 1)
            for c in range(NC):
                m = pe.matmul(PS[:, 6 + e % 2, 0:P], HS[:, (e % 2) * FF + c * P:(e % 2) * FF + (c + 1) * P],
                              FC2[:, e * FF + c * P:e * FF + (c + 1) * P], start=(c == 0), stop=(c == NC - 1))
            m.then_inc(sem("e_fc2"), 1)

        @block.tensor
        def _(pe):
            mm = pe.matmul

            def norm(k, hf, x):
                cb, vb = NORM_BANKS[(k, hf)]
                n = 2 * k + hf + 1
                if k == 1:
                    pe.wait_ge(sem("shifted"), NU)
                if cb is not None:
                    mm(bank(cb), centre, half(x, hf), start=True, stop=True).then_inc(sem("centred"), 1)
                pe.wait_ge(sem("squared"), n)
                mm(bank(vb), mean_m, half(SQ, hf), start=True, stop=True).then_inc(sem("meansq"), 1)

            def conditioning():
                pe.wait_ge(sem("ld_first"), 48)
                pe.wait_ge(sem("ld_w0"), 16)
                mm(PS[:, 4, 0:P], W0[:, 0:P], CD[:, :], start=True, stop=True)
                mm(PS[:, 4, P:2 * P], W0[:, P:2 * P], CD[:, :], start=True, stop=True).then_inc(sem("c_gb"), 1)
                mm(PS[:, 5, 0:P], centre, CD[:, :], start=True, stop=True).then_inc(sem("c_cen"), 1)

            def conditioning2():
                pe.wait_ge(sem("c_sq"), 1)
                mm(PS[:, 5, P:2 * P], mean_m, CN[:, 0:P], start=True, stop=True).then_inc(sem("c_var"), 1)
                pe.wait_ge(sem("c_ln"), 1)
                pe.wait_ge(sem("ld_w1"), 32)
                mm(PS[:, 5, 2 * P:3 * P], W1[:, 0:P], CN[:, 4 * P:5 * P], start=True, stop=True).then_inc(sem("c_h"), 1)
                pe.wait_ge(sem("c_silu"), 1)
                pe.wait_ge(sem("ld_w2"), 16)
                pe.wait_ge(sem("c_gb_used"), 1)
                for s in range(6):
                    m = mm(PS[:, 4 if s < 4 else 6, (s % 4) * P:(s % 4 + 1) * P],
                           W2[:, 4 * P + 2 * FF + s * P:4 * P + 2 * FF + (s + 1) * P], SC[:, :], start=True, stop=True)
                    if s == 3:
                        m.then_inc(sem("c_ada"), 1)
                pe.wait_ge(sem("ld_w3"), 16)
                mm(PS[:, 6, 2 * P:3 * P], W3S[:, 0:P], SC[:, :], start=True, stop=True).then_inc(sem("c_ada"), 1)
                mm(PS[:, 7, 0:1], W0[:, 5 * P:6 * P], vcol("l0_bv"), start=True, stop=True)
                mm(PS[:, 7, 1:2], W2[:, 3 * P:4 * P], vcol("l2_bv"), start=True, stop=True).then_inc(sem("c_bv"), 1)
                pe.wait_ge(sem("c_gelu"), 1)
                pe.wait_ge(sem("c_low_free"), 1)
                for w in range(4):
                    for r in range(RANK):
                        c = P + (w * RANK + r) * P
                        m = mm(PS[:, 4 + w, r * B:r * B + P], W1[:, c:c + P], HC[:, :], start=True, stop=True)
                    m.then_inc(sem("w_low"), 1)
                pe.wait_ge(sem("low_sb"), 4)
                for i, w in enumerate((1, 3)):
                    for hf in range(2):
                        pe.transpose(PS[:, 4, (2 * i + hf) * P:(2 * i + hf + 1) * P],
                                     AW[:, (w * 2 + hf) * P:(w * 2 + hf + 1) * P], ident).then_inc(sem("low_t"), 1)

            def attention_in(l, Wt, qk_banks, v_bank):
                for hf in range(2):
                    pe.wait_ge(sem("hn"), 2 * l + hf + 1)
                    mm(bank(qk_banks[0] + hf), Wt[:, 0:P], half(HN, hf), start=True, stop=True).then_inc(sem("q_ps"), 1)
                    mm(bank(qk_banks[1] + hf), Wt[:, P:2 * P], half(HN, hf), start=True, stop=True).then_inc(sem("k_ps"), 1)

            def values(l, Wt, v_bank):
                for hf in range(2):
                    if l == 1:
                        pe.wait_ge(sem("qb"), hf + 1)
                    for i in range(TH):
                        t = hf * TH + i
                        m = mm(PS[:, v_bank + hf, i * P:(i + 1) * P], HN[:, t * P:(t + 1) * P], Wt[:, 2 * P:3 * P],
                               start=True, stop=True)
                    m.then_inc(sem("v_ps"), 1)

            def attention(l, Wp):
                for s in range(NU + 2):
                    if s < NU:
                        tp, gp = s // 2, s % 2
                        if s == 0:
                            pe.wait_ge(sem("q_sb"), 2 * l + 2)
                            pe.wait_ge(sem("kbd"), 8 * l + 8)
                            pe.wait_ge(sem("vbd"), 8 * l + 8)
                        if s >= 2:
                            pe.wait_ge(sem("shifted"), NU * l + s - 1)
                        for t in (2 * tp, 2 * tp + 1):
                            for g in (2 * gp, 2 * gp + 1):
                                for b in range(BT):
                                    c = t * P + 32 * b
                                    m = mm(PS[32 * b:32 * b + 32, 4 + g, (t % 2) * P:(t % 2 + 1) * P],
                                           QT[32 * g:32 * g + 32, c:c + 32], KBD[32 * g:32 * g + 32, :, c:c + 32],
                                           start=True, stop=True)
                        m.then_inc(sem("scores"), 1)
                    if s >= 2:
                        u = s - 2
                        tp, gp = u // 2, u % 2
                        pe.wait_ge(sem("pt"), NU * l + u + 1)
                        if u >= 2:
                            pe.wait_ge(sem("normed"), NU * l + u - 1)
                        for g in range(2):
                            for i in range(2):
                                for hh in range(NG):
                                    m = mm(av_out(u)[32 * hh:32 * hh + 32, i, :, g, :],
                                           PTt[:, u % 2, ((g * 2 + i) * NG + hh) * 32:((g * 2 + i) * NG + hh + 1) * 32],
                                           VBD[:, 2 * tp + i, NG * (2 * gp + g) + hh, :, :], start=True, stop=True)
                        m.then_inc(sem("av"), 1)
                    if s in (NU // 2 + 3, NU + 1):
                        project(l, 0 if s < NU else 1, Wp)

            def project(l, hf, Wp):
                pe.wait_ge(sem("oT"), NT // 2 * l + 2 * (hf + 1))
                mm(bank(2 + hf), Wp, half(OA, hf), start=True, stop=True).then_inc(sem("proj"), 1)

            conditioning()
            pe.wait_ge(sem("ld_x"), 16)
            mm(bank(0), centre, half(XA, 0), start=True, stop=True).then_inc(sem("centred"), 1)
            mm(bank(1), centre, half(XA, 1), start=True, stop=True).then_inc(sem("centred"), 1)
            for hf in range(2):
                pe.wait_ge(sem("squared"), hf + 1)
                mm(bank(2 + hf), mean_m, half(SQ, hf), start=True, stop=True).then_inc(sem("meansq"), 1)
            conditioning2()
            pe.wait_ge(sem("low_tsb"), 2)
            attention_in(0, W0[:, 2 * P:5 * P], (4, 6), 2)
            values(0, W0[:, 2 * P:5 * P], 2)
            attention(0, W0[:, 5 * P:6 * P])
            for hf in range(2):
                pe.wait_ge(sem("h1"), hf + 1)
                norm(1, hf, XB)
            if layers >= 2:
                for hf in range(2):
                    cols = slice(hf * BH * RANK, (hf + 1) * BH * RANK)
                    a1 = AW4[:, 0, hf * BH:(hf + 1) * BH, :].rearrange("p b r -> p (b r)")
                    a2 = AW4[:, 2, hf * BH:(hf + 1) * BH, :].rearrange("p b r -> p (b r)")
                    u, w = 4 + 2 * hf, 5 + 2 * hf
                    pe.wait_ge(sem("x_done"), hf + 1)
                    mm(bank(u), a1, half(XB, hf), start=True, stop=True).then_inc(sem("y1"), 1)
                    pe.wait_ge(sem("y1m"), hf + 1)
                    mm(bank(w), BTT[:, hf * P:(hf + 1) * P], half(T_, hf), start=True, stop=True).then_inc(sem("y2"), 1)
                    pe.wait_ge(sem("y2g"), hf + 1)
                    mm(bank(u), a2, half(RS, hf), start=True, stop=True).then_inc(sem("y3"), 1)
                    pe.wait_ge(sem("y3m"), hf + 1)
                    mm(bank(w), BTT[:, (2 + hf) * P:(3 + hf) * P], half(T_, hf), start=True, stop=True).then_inc(sem("y4"), 1)
            if layers >= 3:
                for hf in range(2):
                    norm(2, hf, XA)
                attention_in(1, W2[:, 0:3 * P], (4, 6), 4)
                for hf in range(2):
                    pe.wait_ge(sem("q_sq"), hf + 1)
                    mm(bank(0 + hf), mean8, half(SQ, hf), start=True, stop=True).then_inc(sem("qk_ms"), 1)
                    pe.wait_ge(sem("k_sq"), hf + 1)
                    mm(bank(2 + hf), mean8, half(T_, hf), start=True, stop=True).then_inc(sem("qk_ms"), 1)
                values(1, W2[:, 0:3 * P], 4)
                attention(1, W2[:, 3 * P:4 * P])
                for hf in range(2):
                    norm(3, hf, XB)
                for hf in range(2):
                    pe.wait_ge(sem("hn"), 4 + hf + 1)
                    for c in range(NC):
                        if hf == 1:
                            pe.wait_ge(sem("hid"), c + 1)
                        mm(bank(4 + c), W2[:, 4 * P + c * P:4 * P + (c + 1) * P], half(HN, hf),
                           start=True, stop=True).then_inc(sem("fc1_ps"), 1)
                for hf in range(2):
                    for c in range(NC):
                        pe.wait_ge(sem("hid"), NC * hf + c + 1)
                        m = mm(bank(hf), W2[:, 4 * P + FF + c * P:4 * P + FF + (c + 1) * P], half(HID[:, c, :], hf),
                               start=(c == 0), stop=(c == NC - 1))
                    m.then_inc(sem("fc2_ps"), 1)
            if layers >= 4:
                WQ3 = W3S[:, P:P + W3]
                WK3 = W3S[:, P + W3:P + 2 * W3]
                WV3 = W3S[:, P + 2 * W3:P + 3 * W3]
                WO3 = W3S[:, P + 3 * W3:P + 4 * W3]
                for hf in range(2):
                    pe.wait_ge(sem("x_done"), 4 + hf + 1)
                    norm(4, hf, XB)
                pe.wait_ge(sem("w3c"), 2)

                def front_a(t):
                    pe.wait_ge(sem("hn"), 6 + (1 if t < TH else 2))
                    if t >= 1:
                        pe.wait_ge(sem("q3n"), t)
                    for i in range(2):
                        mm(bank(i), HN[:, t * P:(t + 1) * P], WQ3[:, i * 512:(i + 1) * 512],
                           start=True, stop=True).then_inc(sem("q3"), 1)

                def front_b(t):
                    if t == 0:
                        pe.wait_ge(sem("hn"), 8)
                    if t >= 1:
                        pe.wait_ge(sem("k3n"), t)
                    for i in range(2):
                        mm(bank(2 + i), HN[:, t * P:(t + 1) * P], WK3[:, i * 512:(i + 1) * 512],
                           start=True, stop=True).then_inc(sem("k3"), 1)

                def front_v(t):
                    if t >= 1:
                        pe.wait_ge(sem("k3t"), t)
                    for i in range(2):
                        m = mm(bank(4 + i), HN[:, t * P:(t + 1) * P], WV3[:, i * 512:(i + 1) * 512],
                               start=True, stop=True)
                    m.then_inc(sem("v3"), 1)

                def turn(t, src, ready, free, n_free, done):
                    pe.wait_ge(sem(ready), t + 1)
                    pe.wait_ge(sem(free), n_free)
                    for c in range(C3):
                        m = pe.transpose(PS[:, 4 + c // 4, (c % 4) * P:(c % 4 + 1) * P], src[:, c * P:(c + 1) * P], ident)
                    m.then_inc(sem(done), 1)

                def scores3(t):
                    pe.wait_ge(sem("k3t"), t + 1)
                    if t >= 1:
                        pe.wait_ge(sem("shifted3"), t)
                        pe.wait_ge(sem("x3"), t)
                    for c in range(C3):
                        for u in range(2):
                            for b in range(BT):
                                r = slice(64 * u, 64 * u + 64)
                                n = slice(32 * b, 32 * b + 32)
                                m = mm(PS[32 * b:32 * b + 32, 6 + u, c * 32:c * 32 + 32], QK3[r, t % 2, 0, c, n],
                                       QK3[r, t % 2, 1, c, n], start=True, stop=True)
                    m.then_inc(sem("scores3"), 1)

                def av3(t, rnd):
                    pe.wait_ge(sem("pt3"), t + 1)
                    if 2 * t + rnd >= 1:
                        pe.wait_ge(sem("o3"), 2 * t + rnd)
                    for c in range(4 * rnd, 4 * rnd + 4):
                        for u in range(2):
                            h = 2 * c + u
                            m = mm(PS[64 * u:64 * u + 64, 6 + (c % 4) // 2, 256 + (c % 2) * P:256 + (c % 2 + 1) * P],
                                   V3[:, t % 2, h * HD3:(h + 1) * HD3], PTB3[:, t % 2, h, :], start=True, stop=True)
                    m.then_inc(sem("av3"), 1)

                def out3(t):
                    pe.wait_ge(sem("o3"), 2 * t + 2)
                    for c in range(C3):
                        m = mm(PS[:, 7, 256:256 + P], WO3[:, c * P:(c + 1) * P], O3[:, c, :], start=(c == 0), stop=(c == C3 - 1))
                    m.then_inc(sem("out3"), 1)

                for t in range(NT + 1):
                    if t < NT:
                        front_a(t)
                    if t >= 1:
                        scores3(t - 1)
                    if t < NT:
                        front_b(t)
                        front_v(t)
                    if t >= 1:
                        av3(t - 1, 0)
                    if t < NT:
                        turn(t, T_, "q3n", "v3s", t + 1, "q3tp")
                    if t >= 1:
                        av3(t - 1, 1)
                    if t < NT:
                        turn(t, RS, "k3n", "q3t", t + 1, "k3tp")
                    if t >= 1:
                        out3(t - 1)
                for t in range(NT):
                    pe.wait_ge(sem("x3"), t + 1)
                    m = mm(PS[:, 0, t * E:(t + 1) * E], XA[:, t * P:(t + 1) * P], W3S[:, P + 4 * W3:P + 4 * W3 + E],
                           start=True, stop=True)
                m.then_inc(sem("logits"), 1)
                for t in range(NT):
                    m = pe.transpose(PS[:, 4 + t // 4, (t % 4) * P:(t % 4 + 1) * P], XA[:, t * P:(t + 1) * P], ident)
                m.then_inc(sem("xt_ps"), 1)
                pe.wait_ge(sem("gate"), 1)
                pe.transpose(PS[0:TE, 1, 0:P], GT[:, 0:TE], ident).then_inc(sem("gate_t"), 1)
                pe.wait_ge(sem("ld_m"), 96)
                for i in range(BITS):
                    pe.wait_ge(sem("counted"), i + 1)
                    mm(PS[0:TE, 2, 0:1], TRI[:, TE:2 * TE], CT[:, 0:1], start=True, stop=True).then_inc(sem("total"), 1)
                pe.wait_ge(sem("prefix"), 2)
                mm(PS[0:TE, 3, 0:2], TRI[:, 0:TE], CT[:, 2:4], start=True, stop=True)
                mm(PS[0:TE, 3, 2:4], TRI[:, TE:2 * TE], CT[:, 2:4], start=True, stop=True).then_inc(sem("offsets"), 1)
                pe.wait_ge(sem("slots"), 1)
                pe.transpose(PS[:, 1, 0:TE], GE[:, 4 * P:5 * P], ident[0:TE, 0:TE]).then_inc(sem("slots_t"), 1)
                pe.wait_ge(sem("xn"), NT)
                for t in range(NT):
                    pe.wait_ge(sem("onehot"), t + 1)
                    for i in range(2):
                        m = mm(bank(2 + i), XN[:, t, :], OH[:, t, i * 512:(i + 1) * 512], start=(t == 0), stop=(t == NT - 1))
                    m.then_inc(sem("gathered"), 1)
                for e in range(E):
                    pe.wait_ge(sem("xg"), 2 if e >= 4 else 1)
                    if e >= 2:
                        pe.wait_ge(sem("e_b1"), e - 1)
                    for c in range(NC):
                        m = mm(PS[:, 4 + e % 2, c * P:(c + 1) * P], FC1[:, e * FF + c * P:e * FF + (c + 1) * P],
                               XG[:, e * P:(e + 1) * P], start=True, stop=True)
                    m.then_inc(sem("e_fc1"), 1)
                    if e >= 1:
                        second(pe, e - 1)
                second(pe, E - 1)
                n = 0
                for e in range(E):
                    for i in range(2):
                        if e == 0:
                            pe.wait_ge(sem("gated"), TH * (i + 1))
                        if n >= 2:
                            pe.wait_ge(sem("ot"), n - 1)
                        for t in range(4 * i, 4 * i + 4):
                            m = pe.transpose(PS[:, 2 + i, (t % 4) * P:(t % 4 + 1) * P], OH[:, t, e * P:(e + 1) * P], ident)
                        m.then_inc(sem("ot_ps"), 1)
                        n += 1
                pe.wait_ge(sem("ot"), 2 * E)
                pe.wait_ge(sem("e_y"), E)
                for t in range(NT):
                    if t >= 2:
                        pe.wait_ge(sem("out_tile"), t - 1)
                    for e in range(E):
                        m = mm(PS[:, 4 + t % 2, 0:P], OT[:, e, t, :], Y[:, e, :], start=(e == 0), stop=(e == E - 1))
                    m.then_inc(sem("scattered"), 1)

        @block.scalar
        def _(act):
            A = nc.scalar.activation
            eps, half_ln, zero = (EPSC[:, i:i + 1] for i in range(3))

            def rsqrt(out_, in_, w_in, n_in, scale, bias, out_bias, tag, n):
                act.wait_ge(sem(w_in), n_in)
                A(out_, in_, ACT.Ln, bias=bias, scale=scale).then_inc(sem(tag + "_ln"), 1)
                act.wait_ge(sem(tag + "_ln"), n)
                A(out_, out_, ACT.Exp, bias=out_bias, scale=-0.5).then_inc(sem(tag), 1)

            def norm_sq(k, hf, x=None, w=None, n_w=None):
                n = 2 * k + hf + 1
                if x is None:
                    cb = NORM_BANKS[(k, hf)][0]
                    act.wait_ge(sem("centred"), {0: 0, 1: 2, 4: 4}[k] + hf + 1)
                    A(half(SQ, hf), bank(cb), ACT.Square).then_inc(sem("squared"), 1)
                else:
                    act.wait_ge(sem(w), n_w)
                    A(half(SQ, hf), half(x, hf), ACT.Square).then_inc(sem("squared"), 1)

            def norm_rs(k, hf):
                n = 2 * k + hf + 1
                vb = NORM_BANKS[(k, hf)][1]
                if k in (2, 3):
                    rsqrt(half(RS, hf), half(RS, hf), "floored", 2 * (k - 2) + hf + 1, LN_SCALE, zero, half_ln, "rstd", n)
                else:
                    rsqrt(half(RS, hf), bank(vb), "meansq", n, 1.0, eps, zero, "rstd", n)

            def exp_rows(l):
                for u in range(NU):
                    act.wait_ge(sem("shifted"), NU * l + u + 1)
                    A(EXB[:, u % 2, :], EXB[:, u % 2, :], ACT.Exp).then_inc(sem("exped"), 1)

            nc.scalar.preload_act_table_set("natural_log_exp_and_others")
            act.wait_ge(sem("ld_first"), 48)
            act.wait_ge(sem("eps_set"), 3)
            act.wait_ge(sem("c_cen"), 1)
            A(CN[:, 0:P], PS[:, 5, 0:P], ACT.Square).then_inc(sem("c_sq"), 1)
            A(CN[:, 5 * P:6 * P], CD[:, :], ACT.Exp, scale=-1.0).then_inc(sem("c_exp"), 1)
            norm_sq(0, 0)
            norm_sq(0, 1)
            rsqrt(CN[:, P:2 * P], PS[:, 5, P:2 * P], "c_var", 1, 1.0, eps, zero, "c_rs", 1)
            norm_rs(0, 0)
            norm_rs(0, 1)
            act.wait_ge(sem("c_h"), 1)
            A(HC[:, :], PS[:, 5, 2 * P:3 * P], ACT.Gelu, bias=vcol("l1_b1")).then_inc(sem("c_gelu"), 1)
            nc.scalar.preload_act_table_set("natural_log_exp_and_others")
            act.wait_ge(sem("low_t"), 4)
            for i in range(2):
                A(BTT[:, i * 256:(i + 1) * 256], PS[:, 4, i * 256:(i + 1) * 256], ACT.Identity).then_inc(sem("low_tsb"), 1)
            for hf in range(2):
                act.wait_ge(sem("q_ps"), hf + 1)
                A(half(QT, hf), bank(4 + hf), ACT.Identity, bias=vcol("l0_bq")).then_inc(sem("q_sb"), 1)
                act.wait_ge(sem("k_ps"), hf + 1)
                A(half(SQ, hf), bank(6 + hf), ACT.Identity, bias=vcol("l0_bk")).then_inc(sem("k_sb"), 1)

            def values_out(l, v_bank):
                if l == 0:
                    act.wait_ge(sem("vbd_ones"), 4)
                for hf in range(2):
                    act.wait_ge(sem("v_ps"), 2 * l + hf + 1)
                    for b in range(BT):
                        r = slice(32 * b, 32 * b + 32)
                        A(VBD[r, hf * TH:(hf + 1) * TH, :, b, 0:HD],
                          PS[r, v_bank + hf, :].rearrange("p (t h d) -> p t h d", t=TH, h=NH),
                          ACT.Identity).then_inc(sem("vbd"), 1)

            values_out(0, 2)
            exp_rows(0)
            norm_sq(1, 0)
            norm_rs(1, 0)
            norm_sq(1, 1)
            norm_rs(1, 1)
            if layers >= 2:
                for hf in range(2):
                    act.wait_ge(sem("y2"), hf + 1)
                    A(half(RS, hf), bank(5 + 2 * hf), ACT.Gelu).then_inc(sem("y2g"), 1)
                nc.scalar.preload_act_table_set("natural_log_exp_and_others")
            if layers >= 3:
                for hf in range(2):
                    norm_sq(2, hf, XA, "x_done", 2 + hf + 1)
                for hf in range(2):
                    norm_rs(2, hf)
                for hf in range(2):
                    act.wait_ge(sem("q_ps"), 2 + hf + 1)
                    A(half(QT, hf), bank(4 + hf), ACT.Identity, bias=vcol("l2_bq")).then_inc(sem("qb"), 1)
                    act.wait_ge(sem("qb"), hf + 1)
                    A(half(SQ, hf), half(QT, hf), ACT.Square).then_inc(sem("q_sq"), 1)
                    act.wait_ge(sem("k_ps"), 2 + hf + 1)
                    A(half(T_, hf), bank(6 + hf), ACT.Square, bias=vcol("l2_bk")).then_inc(sem("k_sq"), 1)
                values_out(1, 4)
                for i in range(4):
                    hf, s = i // 2, i % 2
                    buf = half(RS, hf) if s == 0 else half(SQ, hf)
                    rsqrt(buf, buf, "qk_floor", i + 1, LN_SCALE, zero, half_ln, "qk_rs", i + 1)
                exp_rows(1)
                for hf in range(2):
                    norm_sq(3, hf, XB, "h1", 2 + hf + 1)
                    norm_rs(3, hf)
                for hf in range(2):
                    for c in range(NC):
                        act.wait_ge(sem("fc1_ps"), NC * hf + c + 1)
                        A(half(HID[:, c, :], hf), bank(4 + c), ACT.Gelu_apprx_tanh,
                          bias=vcol(f"l2_bfc1_{c}")).then_inc(sem("hid"), 1)
                nc.scalar.preload_act_table_set("natural_log_exp_and_others")
            if layers >= 4:
                for hf in range(2):
                    norm_sq(4, hf)
                    norm_rs(4, hf)
                st = [ST[:, i * H3:(i + 1) * H3] for i in range(4)]

                def square3(t, s, nm, w_in, n_in):
                    act.wait_ge(sem(nm), 2 * t + 2)
                    if n_in:
                        act.wait_ge(sem(w_in), n_in)
                    A(SQ.rearrange("p (k n) -> p k n", k=2), PS[:, 2 * s:2 * s + 2, :], ACT.Square).then_inc(sem(nm + "sq"), 1)

                def turned3(t, s, g, b_, nm):
                    act.wait_ge(sem(nm + "p"), t + 1)
                    A(QK3[:, t % 2, s, :, :].rearrange("p (k c) n -> p k (c n)", k=2), PS[:, 4:6, :],
                      ACT.Identity, bias=vcol(b_), scale=vcol(g)).then_inc(sem(nm), 1)

                def exp3(t):
                    act.wait_ge(sem("shifted3"), t + 1)
                    A(EXB[:, 0, :], EXB[:, 0, :], ACT.Exp, scale=1.0 / math.sqrt(HD3)).then_inc(sem("exped3"), 1)

                def out3(t, rnd):
                    act.wait_ge(sem("av3"), 2 * t + rnd + 1)
                    if t >= 1:
                        act.wait_ge(sem("out3"), t)
                    A(O3[:, 4 * rnd:4 * rnd + 4, :].rearrange("p (k c) n -> p k (c n)", k=2), PS[:, 6:8, 256:512],
                      ACT.Identity).then_inc(sem("o3"), 1)

                for t in range(NT + 1):
                    if t < NT:
                        square3(t, 0, "q3", "k3sum", t)
                        rsqrt(st[2], st[0], "q3sum", t + 1, 1.0 / HD3, eps, zero, "q3rs", t + 1)
                        square3(t, 1, "k3", "q3sum", t + 1)
                    if t >= 1:
                        exp3(t - 1)
                    if t < NT:
                        act.wait_ge(sem("v3"), t + 1)
                        if t >= 2:
                            act.wait_ge(sem("av3"), 2 * (t - 1))
                        A(V3[:, t % 2, :].rearrange("p (k n) -> p k n", k=2), PS[:, 4:6, :], ACT.Identity).then_inc(sem("v3s"), 1)
                        rsqrt(st[3], st[1], "k3sum", t + 1, 1.0 / HD3, eps, zero, "k3rs", t + 1)
                    if t >= 1:
                        out3(t - 1, 0)
                    if t < NT:
                        turned3(t, 0, "l3_qg", "l3_qb", "q3t")
                    if t >= 1:
                        out3(t - 1, 1)
                    if t < NT:
                        turned3(t, 1, "l3_kg", "l3_kb", "k3t")
                act.wait_ge(sem("g_shift"), 1)
                A(GT[:, 0:TE], GT[:, 0:TE], ACT.Exp).then_inc(sem("g_exp"), 1)
                rsqrt(MS[:, 40:48], MS[:, 8:24].rearrange("p (t s) -> p t s", s=2)[:, :, 1], "mv", NT, 1.0, eps, zero, "m_rs", 1)
                for i in range(2):
                    act.wait_ge(sem("gathered"), NT)
                    A(half(XG, i), bank(2 + i), ACT.Identity, bias=vcol("l3_mb"), scale=vcol("l3_mg")).then_inc(sem("xg"), 1)
                for e in range(E):
                    act.wait_ge(sem("e_b1"), e + 1)
                    h = HS[:, (e % 2) * FF:(e % 2 + 1) * FF]
                    A(h, h, ACT.Gelu_apprx_tanh).then_inc(sem("e_h"), 1)
                for n in range(2 * E):
                    e, i = n // 2, n % 2
                    act.wait_ge(sem("ot_ps"), n + 1)
                    A(OT[:, e, 4 * i:4 * i + 4, :].rearrange("p t n -> p (t n)"), bank(2 + i), ACT.Identity).then_inc(sem("ot"), 1)

        def back3(dve, then, t):
            v = nc.vector
            dve.wait_ge(sem("scores3"), t + 1)
            sc = PS[:, 6:8, 0:256].rearrange("p u (c n) -> p u c n", c=C3)
            mx = MX[:, 0:H3]
            ex = EXB[:, 0, :].rearrange("p (u c n) -> p u c n", u=2, c=C3)
            ex3 = EXB[:, 0, :].rearrange("p (h n) -> p h n", h=H3)
            then(v.tensor_reduce(mx, sc, AX_X, ALU.max))
            v.tensor_tensor(ex, sc, mx.rearrange("p (u c) -> p u c", u=2).unsqueeze(3).broadcast_to([P, 2, C3, N]),
                            ALU.subtract).then_inc(sem("shifted3"), 1)
            dve.wait_ge(sem("exped3"), t + 1)
            rec = REC[:, 0:H3]
            then(v.tensor_reduce(rec, ex3, AX_X, ALU.add))
            then(v.reciprocal(rec, rec))
            then(v.tensor_tensor(EXB[:, 1, :].rearrange("p (h n) -> p h n", h=H3), ex3,
                                 rec.unsqueeze(2).broadcast_to([P, H3, N]), ALU.mult))
            if t >= 2:
                dve.wait_ge(sem("av3"), 2 * (t - 1))
            for b in range(BT):
                r = slice(32 * b, 32 * b + 32)
                m = v.transpose(PTB3[r, t % 2, :, r].rearrange("p (c u) n -> p u c n", u=2),
                                EXB[r, 1, :].rearrange("p (u c n) -> p u c n", u=2, c=C3))
            m.then_inc(sem("pt3"), 1)

        def resid3(dve, t):
            dve.wait_ge(sem("out3"), t + 1)
            nc.vector.tensor_tensor(XA[:, t * P:(t + 1) * P], PS[:, 7, 256:256 + P], XB[:, t * P:(t + 1) * P],
                                    ALU.add).then_inc(sem("x3"), 1)

        @block.vector
        def _(dve):
            v = nc.vector
            TT, TS, STT = v.tensor_tensor, v.tensor_scalar, v.scalar_tensor_tensor
            step = [0]

            def then(ins):
                step[0] += 1
                ins.then_inc(sem("dve_step"), 1)
                dve.wait_ge(sem("dve_step"), step[0])

            def centred_times(k, hf):
                dve.wait_ge(sem("rstd"), 2 * k + hf + 1)
                then(TT(half(T_, hf), bank(NORM_BANKS[(k, hf)][0]), half(RS, hf), ALU.mult))

            dve.wait_ge(sem("ld_first"), 48)
            dve.wait_ge(sem("c_gb"), 1)
            then(TS(GM[:, :], PS[:, 4, 0:B], vcol("l0_bg"), None, ALU.add))
            then(TS(GB[:, :], PS[:, 4, P:P + B], vcol("l0_bb"), None, ALU.add))
            TS(GG[:, :], GM[:, :], vcol("l0_lng"), None, ALU.mult).then_inc(sem("c_gb_used"), 1)
            then(STT(GB[:, :], GM[:, :], vcol("l0_lnb"), GB[:, :], ALU.mult, ALU.add))
            then(TT(KM[:, 8:9], vcol("l2_gq"), vcol("l2_gk"), ALU.mult))
            then(TS(KM[:, 8:9], KM[:, 8:9], 1.0 / math.sqrt(HD), None, ALU.mult))
            for h in range(4):
                m = TT(KM[:, 4 + h:5 + h], KM[:, 8:9], vcol(f"mask_{h}"), ALU.mult)
            then(m)
            dve.wait_ge(sem("c_exp"), 1)
            then(TS(CN[:, 5 * P:6 * P], CN[:, 5 * P:6 * P], 1.0, None, ALU.add))
            then(v.reciprocal(CN[:, 5 * P:6 * P], CN[:, 5 * P:6 * P]))
            TT(SC[:, :], CD[:, :], CN[:, 5 * P:6 * P], ALU.mult).then_inc(sem("c_silu"), 1)
            dve.wait_ge(sem("c_rs"), 1)
            then(TT(CN[:, 4 * P:5 * P], PS[:, 5, 0:P], CN[:, P:2 * P], ALU.mult))
            TS(CN[:, 4 * P:5 * P], CN[:, 4 * P:5 * P], vcol("l1_lng"), vcol("l1_lnb"), ALU.mult, ALU.add).then_inc(sem("c_ln"), 1)
            for hf in range(2):
                centred_times(0, hf)
                then(TT(bview(half(T_, hf)), bview(half(T_, hf)), bb(GG, hf), ALU.mult))
                TT(bview(half(HN, hf)), bview(half(T_, hf)), bb(GB, hf), ALU.add).then_inc(sem("hn"), 1)
            dve.wait_ge(sem("c_ada"), 1)
            bada = V[:, VCOL["l2_bada_0"]:VCOL["l2_bada_0"] + 6]
            TT(ADA6[:, 0:4, :], PS[:, 4, :].rearrange("p (s b) -> p s b", s=4)[:, :, 0:B],
               bada[:, 0:4].unsqueeze(2).broadcast_to([P, 4, B]), ALU.add)
            dve.wait_ge(sem("c_ada"), 2)
            then(TT(ADA6[:, 4:6, :], PS[:, 6, 0:2 * P].rearrange("p (s b) -> p s b", s=2)[:, :, 0:B],
                    bada[:, 4:6].unsqueeze(2).broadcast_to([P, 2, B]), ALU.add))
            TS(ADA6[:, 1, :], ADA6[:, 1, :], 1.0, vcol("l2_g1"), ALU.add, ALU.mult)
            TS(ADA6[:, 4, :], ADA6[:, 4, :], 1.0, vcol("l2_g2"), ALU.add, ALU.mult)
            TS(SH3[:, :], PS[:, 6, 2 * P:2 * P + B], vcol("l3_bada"), vcol("l3_ln1b"), ALU.add, ALU.add)
            dve.wait_ge(sem("c_bv"), 1)
            then(TS(BP[:, 0:1], PS[:, 7, 0:1], 1.0 / math.sqrt(D), vcol("l0_bp"), ALU.mult, ALU.add))
            TS(BP[:, 1:2], PS[:, 7, 1:2], vcol("l2_bproj"), None, ALU.add).then_inc(sem("c_low_free"), 1)
            for w in range(4):
                dve.wait_ge(sem("w_low"), w + 1)
                TT(AW4[:, w, :, :].rearrange("p b r -> p r b"), PS[:, 4 + w, 0:RANK * B].rearrange("p (r b) -> p r b", r=RANK),
                   W1B[:, w * RANK:(w + 1) * RANK].unsqueeze(2).broadcast_to([P, RANK, B]), ALU.add).then_inc(sem("low_sb"), 1)
            for hf in range(2):
                dve.wait_ge(sem("k_sb"), hf + 1)
                for h in range(NG):
                    TS(half(KBD[:, h, :], hf), half(SQ, hf), vcol(f"mask_{h}"), None, ALU.mult).then_inc(sem("kbd"), 1)

            def attention(l, att_scale, residual):
                for s in range(NU + 3):
                    if s < NU:
                        u, gp = s, s % 2
                        dve.wait_ge(sem("scores"), NU * l + u + 1)
                        sc = PS[:, 4 + 2 * gp:6 + 2 * gp, 0:2 * P].rearrange("p g (x n) -> p g x n", n=N)
                        mx = MX[:, (u % 2) * NH:(u % 2 + 1) * NH]
                        then(v.tensor_reduce(mx, sc, AX_X, ALU.max))
                        TT(EXB[:, u % 2, :].rearrange("p (g x n) -> p g x n", g=2, n=N), sc,
                           mx.rearrange("p (g x) -> p g x", g=2).unsqueeze(3).broadcast_to([P, 2, NH // 2, N]),
                           ALU.subtract).then_inc(sem("shifted"), 1)
                    if 1 <= s <= NU:
                        u = s - 1
                        dve.wait_ge(sem("exped"), NU * l + u + 1)
                        if u >= 2:
                            dve.wait_ge(sem("av"), NU * l + u - 1)
                        v.transpose(PTt[:, u % 2, :], EXB[:, u % 2, :]).then_inc(sem("pt"), 1)
                    if s >= 3:
                        u = s - 3
                        tp, gp = u // 2, u % 2
                        dve.wait_ge(sem("av"), NU * l + u + 1)
                        av = av_out(u).rearrange("p i b g d -> p (i b) g d")
                        rec = REC[:, (u % 2) * NH:(u % 2 + 1) * NH]
                        then(v.reciprocal(rec, PS[:, u % 2, HD:NH * VW:VW]))
                        on = ON[:, :].rearrange("p (x g d) -> p x g d", g=NG, d=HD)
                        STT(on[:, :, 2 * gp:2 * gp + 2, :], av[:, :, :, 0:HD], att_scale,
                            rec.rearrange("p (x g) -> p x g", g=2).unsqueeze(3).broadcast_to([P, 2 * BT, 2, HD]),
                            ALU.mult, ALU.mult).then_inc(sem("normed"), 1)
                        if gp == 1:
                            dve.wait_ge(sem("normed"), NU * l + u + 1)
                            v.transpose(OA[:, tp * 2 * P:(tp + 1) * 2 * P], ON[:, :]).then_inc(sem("oT"), 1)
                    if s in (NU // 2 + 3, NU + 2):
                        residual(0 if s < NU else 1)

            def residual0(hf):
                dve.wait_ge(sem("proj"), hf + 1)
                STT(half(XB, hf), bank(2 + hf), BP[:, 0:1], half(XA, hf), ALU.add, ALU.add).then_inc(sem("h1"), 1)

            dve.wait_ge(sem("ld_x"), 16)
            attention(0, 1.0 / math.sqrt(D), residual0)
            for hf in range(2):
                centred_times(1, hf)
                then(TT(bview(half(T_, hf)), bview(half(T_, hf)), bb(GG, hf), ALU.mult))
                then(TT(bview(half(T_, hf)), bview(half(T_, hf)), bb(GB, hf), ALU.add))
                TT(half(XB, hf), half(XB, hf), half(T_, hf), ALU.add).then_inc(sem("x_done"), 1)
            if layers >= 2:
                mk = bmask.unsqueeze(2).broadcast_to([P, BH, N])
                for hf in range(2):
                    dve.wait_ge(sem("y1"), hf + 1)
                    TT(bview(half(T_, hf)), bview(bank(4 + 2 * hf)), mk, ALU.mult).then_inc(sem("y1m"), 1)
                    dve.wait_ge(sem("y3"), hf + 1)
                    TT(bview(half(T_, hf)), bview(bank(4 + 2 * hf)), mk, ALU.mult).then_inc(sem("y3m"), 1)
                    dve.wait_ge(sem("y4"), hf + 1)
                    TT(half(XA, hf), bank(5 + 2 * hf), half(XB, hf), ALU.add).then_inc(sem("x_done"), 1)
            if layers >= 3:
                FLOOR = EPS_N * EPS_N

                def floor_norm(k, hf):
                    dve.wait_ge(sem("meansq"), 2 * k + hf + 1)
                    TS(half(RS, hf), bank(NORM_BANKS[(k, hf)][1]), FLOOR / D, None, ALU.max).then_inc(sem("floored"), 1)

                def modulate(k, hf, x, scale, shift):
                    dve.wait_ge(sem("rstd"), 2 * k + hf + 1)
                    then(TT(half(HN, hf), half(x, hf), half(RS, hf), ALU.mult))
                    then(TT(bview(half(HN, hf)), bview(half(HN, hf)), bb(ADA6[:, scale, :], hf), ALU.mult))
                    TT(bview(half(HN, hf)), bview(half(HN, hf)), bb(ADA6[:, shift, :], hf), ALU.add).then_inc(sem("hn"), 1)

                for hf in range(2):
                    floor_norm(2, hf)
                for hf in range(2):
                    modulate(2, hf, XA, 1, 0)
                for i in range(4):
                    hf, s = i // 2, i % 2
                    dve.wait_ge(sem("qk_ms"), i + 1)
                    if s == 0:
                        TS(half(RS, hf), bank(hf), FLOOR / HD, None, ALU.max).then_inc(sem("qk_floor"), 1)
                    else:
                        TS(half(SQ, hf), bank(2 + hf), FLOOR / HD, None, ALU.max).then_inc(sem("qk_floor"), 1)
                for hf in range(2):
                    dve.wait_ge(sem("qk_rs"), 2 * hf + 1)
                    TT(half(QT, hf), half(QT, hf), half(RS, hf), ALU.mult).then_inc(sem("q_sb"), 1)
                    dve.wait_ge(sem("qk_rs"), 2 * hf + 2)
                    then(STT(half(SQ, hf), bank(6 + hf), vcol("l2_bk"), half(SQ, hf), ALU.add, ALU.mult))
                    for h in range(4):
                        TS(half(KBD[:, h, :], hf), half(SQ, hf), KM[:, 4 + h:5 + h], None, ALU.mult).then_inc(sem("kbd"), 1)

                def residual2(hf):
                    dve.wait_ge(sem("proj"), 2 + hf + 1)
                    then(STT(bview(half(T_, hf)), bview(bank(2 + hf)), BP[:, 1:2], bb(ADA6[:, 2, :], hf), ALU.add, ALU.mult))
                    TT(half(XB, hf), half(XA, hf), half(T_, hf), ALU.add).then_inc(sem("h1"), 1)

                attention(1, 1.0, residual2)
                for hf in range(2):
                    floor_norm(3, hf)
                    modulate(3, hf, XB, 4, 3)
                for hf in range(2):
                    dve.wait_ge(sem("fc2_ps"), hf + 1)
                    then(STT(bview(half(T_, hf)), bview(bank(hf)), vcol("l2_bfc2"), bb(ADA6[:, 5, :], hf), ALU.add, ALU.mult))
                    TT(half(XB, hf), half(XB, hf), half(T_, hf), ALU.add).then_inc(sem("x_done"), 1)
            if layers >= 4:
                dve.wait_ge(sem("ld_w3"), 16)
                for s in range(2):
                    w = W3S[:, P + s * W3:P + (s + 1) * W3].rearrange("p (h d) -> p h d", h=H3)
                    mean = ST[:, s * H3:(s + 1) * H3]
                    then(v.tensor_reduce(mean, w, AX_X, ALU.add))
                    then(TS(mean, mean, 1.0 / HD3, None, ALU.mult))
                    TT(w, w, mean.unsqueeze(2).broadcast_to([P, H3, HD3]), ALU.subtract).then_inc(sem("w3c"), 1)
                for hf in range(2):
                    centred_times(4, hf)
                    then(TS(half(T_, hf), half(T_, hf), vcol("l3_ln1g"), None, ALU.mult))
                    TT(bview(half(HN, hf)), bview(half(T_, hf)), bb(SH3, hf), ALU.add).then_inc(sem("hn"), 1)
                st = [ST[:, i * H3:(i + 1) * H3] for i in range(4)]
                dve.wait_ge(sem("w3c"), 2)
                dve.wait_ge(sem("ptb_zero"), 1)
                for t in range(NT + 1):
                    if t < NT:
                        for s, nm in enumerate(("q3", "k3")):
                            dve.wait_ge(sem(nm + "sq"), t + 1)
                            v.tensor_reduce(st[s], SQ.rearrange("p (h d) -> p h d", h=H3), AX_X, ALU.add).then_inc(sem(nm + "sum"), 1)
                            dve.wait_ge(sem(nm + "rs"), t + 1)
                            if t >= 1:
                                dve.wait_ge(sem(nm + "tp"), t)
                            dst = T_ if s == 0 else RS
                            TT(dst.rearrange("p (h d) -> p h d", h=H3),
                               PS[:, 2 * s:2 * s + 2, :].rearrange("p k (h d) -> p (k h) d", d=HD3),
                               st[2 + s].unsqueeze(2).broadcast_to([P, H3, HD3]), ALU.mult).then_inc(sem(nm + "n"), 1)
                            if s == 0 and t >= 1:
                                back3(dve, then, t - 1)
                            if s == 1 and t >= 1:
                                resid3(dve, t - 1)
                    else:
                        back3(dve, then, t - 1)
                        resid3(dve, t - 1)
                dve.wait_ge(sem("logits"), 1)
                lg = PS[:, 0, 0:TE].rearrange("p (t e) -> p t e", e=E)
                g3 = GT[:, 0:TE].rearrange("p (t e) -> p t e", e=E)
                then(v.tensor_reduce(MS[:, 0:NT], lg, AX_X, ALU.max))
                TT(g3, lg, MS[:, 0:NT].unsqueeze(2).broadcast_to([P, NT, E]), ALU.subtract).then_inc(sem("g_shift"), 1)
                dve.wait_ge(sem("xt_ps"), 1)
                then(v.tensor_copy(T_.rearrange("p (k n) -> p k n", k=2), PS[:, 4:6, :]))
                dve.wait_ge(sem("g_exp"), 1)
                then(v.tensor_reduce(MS[:, 24:32], g3, AX_X, ALU.add))
                then(v.reciprocal(MS[:, 32:40], MS[:, 24:32]))
                TT(g3, g3, MS[:, 32:40].unsqueeze(2).broadcast_to([P, NT, E]), ALU.mult).then_inc(sem("gate"), 1)
                for t in range(NT):
                    m = v.bn_stats(CN[:, 6 * t:6 * t + 6], XT[:, t, :])
                then(m)
                for t in range(NT):
                    v.bn_aggr(MS[:, 8 + 2 * t:10 + 2 * t], CN[:, 6 * t:6 * t + 6]).then_inc(sem("mv"), 1)
                dve.wait_ge(sem("m_rs"), 1)
                for t in range(NT):
                    TS(XN[:, t, :], XT[:, t, :], MS[:, 8 + 2 * t:9 + 2 * t], MS[:, 40 + t:41 + t], ALU.subtract, ALU.mult).then_inc(sem("xn"), 1)
                dve.wait_ge(sem("gate_t"), 1)
                ge = GE[:, 0:P]
                then(v.tensor_copy(ge, PS[0:TE, 1, 0:P]))
                dve.wait_ge(sem("ld_m"), 96)
                thr, cand, add = CI[:, 0:1], CI[:, 1:2], CI[:, 2:3]
                then(v.memset(thr, 0))
                for i in range(BITS):
                    then(TT(cand, thr, BIT[:, i:i + 1], ALU.bitwise_or))
                    TS(JK[:, :], ge, cand.bitcast(F32), None, ALU.is_ge, ALU.add, accum_out=CT[:, 0:1]).then_inc(sem("counted"), 1)
                    dve.wait_ge(sem("total"), i + 1)
                    then(STT(add, PS[0:TE, 2, 0:1], float(CAP), BIT[:, i:i + 1], ALU.is_ge, ALU.mult))
                    then(TT(thr, thr, add, ALU.bitwise_or))
                gt, eq, pg, pq = (GE[:, i * P:(i + 1) * P] for i in (1, 2, 3, 5))
                sl = GE[:, 4 * P:5 * P]
                then(v.memset(JK[:, :], 1.0))
                then(TS(gt, ge, thr.bitcast(F32), None, ALU.is_gt))
                then(TS(eq, ge, thr.bitcast(F32), None, ALU.is_equal))
                then(v.tensor_tensor_scan(pg, JK[:, :], gt, 0.0, ALU.mult, ALU.add))
                then(v.tensor_tensor_scan(pq, JK[:, :], eq, 0.0, ALU.mult, ALU.add))
                v.tensor_copy(CT[:, 2:3], pg[:, P - 1:P]).then_inc(sem("prefix"), 1)
                v.tensor_copy(CT[:, 3:4], pq[:, P - 1:P]).then_inc(sem("prefix"), 1)
                dve.wait_ge(sem("offsets"), 1)
                then(v.tensor_copy(CT[:, 4:8], PS[0:TE, 3, 0:4]))
                then(TT(CT[:, 5:6], CT[:, 5:6], CT[:, 6:7], ALU.add))
                then(STT(gt, pg, CT[:, 4:5], gt, ALU.add, ALU.mult))
                then(STT(eq, pq, CT[:, 5:6], eq, ALU.add, ALU.mult))
                TT(sl, gt, eq, ALU.add).then_inc(sem("slots"), 1)
                dve.wait_ge(sem("slots_t"), 1)
                then(v.tensor_copy(SM[:, :], PS[:, 1, 0:TE]))
                for t in range(NT):
                    for e in range(E):
                        m = TS(OH[:, t, e * P:(e + 1) * P], iota1, SM[:, t * E + e:t * E + e + 1], None, ALU.is_equal)
                    m.then_inc(sem("onehot"), 1)
                dve.wait_ge(sem("gathered"), NT)

                def gated(t):
                    for e in range(E):
                        k = t * E + e
                        m = TS(OH[:, t, e * P:(e + 1) * P], iota1, SM[:, k:k + 1], GT[:, k:k + 1], ALU.is_equal, ALU.mult)
                    m.then_inc(sem("gated"), 1)

                for e in range(E + 1):
                    if e < E:
                        dve.wait_ge(sem("e_fc1"), e + 1)
                        if e >= 2:
                            dve.wait_ge(sem("e_fc2"), e - 1)
                        TT(HS[:, (e % 2) * FF:(e % 2 + 1) * FF].rearrange("p (c n) -> p c n", c=NC),
                           bank(4 + e % 2).rearrange("p (c n) -> p c n", c=NC),
                           B1[:, e * NC:(e + 1) * NC].unsqueeze(2).broadcast_to([P, NC, P]), ALU.add).then_inc(sem("e_b1"), 1)
                        gated(e)
                    if e >= 1:
                        dve.wait_ge(sem("e_fc2"), e)
                        TT(Y[:, e - 1, :], PS[:, 6 + (e - 1) % 2, 0:P], B2[:, (e - 1) * P:e * P], ALU.add).then_inc(sem("e_y"), 1)
                for t in range(NT):
                    dve.wait_ge(sem("scattered"), t + 1)
                    TT(OUT[:, t * P:(t + 1) * P], PS[:, 4 + t % 2, 0:P], XT[:, t, :], ALU.add).then_inc(sem("out_tile"), 1)


def _pack(inp):
    f = np.float32
    a = {k: np.asarray(v) for k, v in inp.items()}
    L0 = {k[8:]: v for k, v in a.items() if k.startswith("L0_cond_")}
    L1 = {k[8:]: v for k, v in a.items() if k.startswith("L1_cond_")}
    L2 = {k[8:]: v for k, v in a.items() if k.startswith("L2_cond_")}
    L3 = {k[8:]: v for k, v in a.items() if k.startswith("L3_cond_")}
    ones = np.ones(P, f)

    def rows(w):
        return w.reshape(NG, NG, HD, -1).transpose(1, 0, 2, 3).reshape(w.shape)

    wqkv0 = L0["Wqkv"].reshape(NH * HD, 3, D)
    bqkv0 = L0["bqkv"].reshape(NH * HD, 3)
    feat = lambda b: rows(b.reshape(P, 1)).reshape(P)
    col = {
        "l0_bg": L0["bg"], "l0_bb": L0["bb"], "l0_lng": L0["ln_g"], "l0_lnb": L0["ln_b"],
        "l0_bq": bqkv0[:, 0], "l0_bk": bqkv0[:, 1], "l0_bv": feat(bqkv0[:, 2]), "l0_bp": L0["bp"],
        "l1_lng": L1["ln_g"], "l1_lnb": L1["ln_b"], "l1_b1": L1["b1"],
        "l2_g1": np.broadcast_to(L2["g1"], P), "l2_g2": np.broadcast_to(L2["g2"], P),
        "l2_gq": np.broadcast_to(L2["gq"], P), "l2_gk": np.broadcast_to(L2["gk"], P),
        "l2_bq": L2["bqkv"][0:P], "l2_bk": L2["bqkv"][P:2 * P], "l2_bv": feat(L2["bqkv"][2 * P:3 * P]),
        "l2_bproj": L2["bproj"], "l2_bfc2": L2["bfc2"],
        "l3_bada": L3["b_ada"], "l3_ln1g": L3["ln1_g"], "l3_ln1b": L3["ln1_b"],
        "l3_qg": np.tile(L3["qn_g"], 2), "l3_qb": np.tile(L3["qn_b"], 2),
        "l3_kg": np.tile(L3["kn_g"], 2), "l3_kb": np.tile(L3["kn_b"], 2),
        "l3_mg": L3["mlp_g"], "l3_mb": L3["mlp_b"],
    }
    for c in range(NC):
        col[f"l2_bfc1_{c}"] = L2["bfc1"][c * P:(c + 1) * P]
    for s in range(6):
        col[f"l2_bada_{s}"] = L2["bada"][s * P:(s + 1) * P]
    part = np.arange(P)
    for h in range(4):
        col[f"mask_{h}"] = ((part // HD) % NG == h).astype(f)
    vec = np.stack([col[n] for n in VEC], axis=1)
    eye = np.eye(P, dtype=f)
    j8 = (part[:, None] // HD == part[None, :] // HD).astype(f) / f(HD)
    bm = (part[:, None] // RANK == np.arange(BH)[None, :]).astype(f)
    consts = np.concatenate([eye, eye - f(1 / P), np.full((P, P), 1 / P, f), j8,
                             np.broadcast_to(np.arange(1, P + 1, dtype=f), (P, P)), np.ones((P, P), f), bm], axis=1)
    cond = np.concatenate([a["cond_1024"].T, np.zeros((D, P - B), f)], axis=1)
    w0 = np.concatenate([L0["Wg"].T, L0["Wb"].T, wqkv0[:, 0].T, wqkv0[:, 1].T, wqkv0[:, 2].T, rows(L0["Wp"].T)], axis=1)
    w1 = np.concatenate([L1["W1"], L1["W2"].reshape(P, 4, D, RANK).transpose(0, 1, 3, 2).reshape(P, -1)], axis=1)
    l1b2 = L1["b2"].reshape(4, D, RANK).transpose(1, 0, 2).reshape(P, -1)
    w2 = np.concatenate([L2["Wqkv"].T, rows(L2["Wproj"].T), L2["Wfc1"].T,
                         L2["Wfc2"].T.reshape(NC, P, P).transpose(1, 0, 2).reshape(P, -1), L2["Wada"].T], axis=1)
    w3 = np.concatenate([L3["W_ada"].T, L3["Wqkv"].T,
                         L3["Wout"].T.reshape(C3, P, P).transpose(1, 0, 2).reshape(P, -1), L3["Wgate"].T], axis=1)
    wm1 = L3["fc1s"].transpose(2, 0, 1).reshape(P, -1)
    wm2 = L3["fc2s"].transpose(2, 0, 1).reshape(NC, P, E, P).transpose(1, 2, 0, 3).reshape(P, -1)
    b1s = L3["b1s"].reshape(E, NC, P).transpose(2, 0, 1).reshape(P, -1)
    b2s = L3["b2s"].reshape(-1)
    bits = np.broadcast_to(np.array([1 << (BITS - 1 - i) for i in range(BITS)], np.int32), (TE, BITS))
    te = np.arange(TE)
    same = te[:, None] % E == te[None, :] % E
    before = same & (te[:, None] // E < te[None, :] // E)
    tril = np.concatenate([before, same], axis=1).astype(f)
    return {"xT": a["x"].reshape(TOK, D).T, "condT": cond, "vec": vec, "w0": w0, "consts": consts, "w1": w1,
            "w2": w2, "w3": w3, "wm1": wm1, "wm2": wm2, "b1s": b1s, "b2s": b2s, "l1b2": l1b2,
            "bits": bits, "tril": tril}


def kernel(**inputs):
    import concourse.bacc as _bacc
    from concourse.bass_utils import run_bass_kernel_spmd as _run

    nc = _bacc.Bacc("TRN2", target_bir_lowering=False, num_devices=1)
    arrays, args = {}, []
    for name, a in _pack(inputs).items():
        a = np.ascontiguousarray(a)
        arrays[f"in_{name}"] = a
        args.append(nc.dram_tensor(f"in_{name}", a.shape, mybir.dt.from_np(a.dtype), kind="ExternalInput").ap())
    args.append(nc.dram_tensor("out_0", (TOK, D), F32, kind="ExternalOutput").ap())
    build(nc, *args)
    r = _run(nc, [arrays], core_ids=[0])
    return r.results[0]["out_0"].reshape(B, N, D)
```

```python
import math
from contextlib import ExitStack

import numpy as np

import concourse.bass as bass
from concourse import mybir

F32 = mybir.dt.float32
BF16 = mybir.dt.bfloat16
I32 = mybir.dt.int32
ALU = mybir.AluOpType
ACT = mybir.ActivationFunctionType
AX_X = mybir.AxisListType.X

P = 128
B, N, D = 32, 32, 128
TOK = B * N
HALF = TOK // 2
NT = TOK // P
TH = NT // 2
BT = P // N
BH = B // 2
NH, HD = 16, 8
NG = 4
VW = HD + 1
RANK = 8
FF = 512
NC = FF // P
NU = NT
H3, HD3 = 16, 64
C3 = H3 * HD3 // P
W3 = H3 * HD3
E = 8
CAP = TOK // E
TE = NT * E
EPS = 1e-5
EPS_N = 1e-12
LN_SCALE = 2.0 ** 24
DIG = 8
NCAND = P // E
XW = D + E

VEC = ["l0_bg", "l0_bb", "l0_lng", "l0_lnb", "l0_bq", "l0_bk", "l0_bv", "l0_bp",
       "l1_lng", "l1_lnb", "l1_b1",
       "l2_g1", "l2_g2", "l2_gq", "l2_gk", "l2_bq", "l2_bk", "l2_bv", "l2_bproj", "l2_bfc2",
       "l2_bfc1_0", "l2_bfc1_1", "l2_bfc1_2", "l2_bfc1_3",
       "l2_bada_0", "l2_bada_1", "l2_bada_2", "l2_bada_3", "l2_bada_4", "l2_bada_5",
       "l3_bada", "l3_ln1g", "l3_ln1b", "l3_qg", "l3_qb", "l3_kg", "l3_kb", "l3_mg", "l3_mb",
       "mask_0", "mask_1", "mask_2", "mask_3"]
VCOL = {n: i for i, n in enumerate(VEC)}
NV = len(VEC)


def build(nc, xT, condT, vec, w0, consts, w1, w2, w3, wm1, wm2, b1s, b2s, l1b2, cands, tril, out, layers=4):
    ctx = ExitStack()
    with ctx:
        def sb(name, cols, dt=F32, parts=P):
            return ctx.enter_context(nc.sbuf_tensor(name, [parts, cols], dt))

        sems = {}

        def sem(name):
            if name not in sems:
                sems[name] = ctx.enter_context(nc.semaphore(name))
            return sems[name]

        PS = ctx.enter_context(nc.psum_tensor("PS", [P, 8, 512], F32))

        XA = sb("XA", TOK)
        XB = sb("XB", TOK)
        CD = sb("CD", P)
        V = sb("V", NV)
        W0 = sb("W0", 6 * P)
        CO = sb("CO", 6 * P + BH)
        W1 = sb("W1", P + 4 * RANK * P)
        W1B = sb("W1B", 4 * RANK)
        W2 = sb("W2", 3 * P + P + FF + FF + 6 * P)
        W3S = sb("W3S", P + 3 * W3 + W3 + E)
        FC1 = W1[:, P:P + E * FF]
        FC2 = sb("FC2", E * FF)
        B1 = sb("B1", E * NC)
        B2 = sb("B2", E * P)
        CU = sb("CU", DIG, I32)
        TRI = sb("TRI", 2 * TE + P)

        ident = CO[:, 0:P]
        centre = CO[:, P:2 * P]
        mean_m = CO[:, 2 * P:3 * P]
        mean8 = CO[:, 3 * P:4 * P]
        iota1 = CO[:, 4 * P:5 * P]
        bmask = CO[:, 6 * P:6 * P + BH]

        def vcol(name, a=0, b=P):
            return V[a:b, VCOL[name]:VCOL[name] + 1]

        WK = sb("WK", 4 * TOK)
        T_, SQ, RS, HN = (WK[:, i * TOK:(i + 1) * TOK] for i in range(4))
        QT = sb("QT", TOK)
        AR1 = sb("AR1", 8 * TOK)
        AR2 = sb("AR2", 8 * TOK)
        KBD = AR1[:, 0:4 * TOK].rearrange("p (h n) -> p h n", h=NG)
        HID = AR1[:, 4 * TOK:8 * TOK].rearrange("p (c n) -> p c n", c=NC)
        QK3 = AR1[:, 4 * TOK:8 * TOK].rearrange("p (b s c n) -> p b s c n", b=2, s=2, c=C3)
        VBD = AR2[:, 0:NT * NH * BT * VW].rearrange("p (t h b d) -> p t h b d", t=NT, h=NH, b=BT)
        V3 = AR2[:, 5 * TOK:5 * TOK + 3 * W3].rearrange("p (b n) -> p b n", b=3)
        PTB = sb("PTB", 2 * H3 * P)
        PTB3 = PTB[:, :].rearrange("p (b h n) -> p b h n", b=2, h=H3)
        EX = sb("EX", 2 * 512)
        EXB = EX[:, :].rearrange("p (b n) -> p b n", b=2)
        PT = sb("PT", 2 * 512)
        PTt = PT[:, :].rearrange("p (b n) -> p b n", b=2)
        MX = sb("MX", 2 * NH)
        REC = sb("REC", 2 * NH)
        ON = sb("ON", 2 * P)
        OA = sb("OA", TOK)
        O3 = OA[:, :].rearrange("p (c n) -> p c n", c=C3)
        ST = sb("ST", 4 * 2 * H3)
        EPSC = sb("EPSC", 4)

        CN = sb("CN", 6 * P)
        HC = sb("HC", P)
        GG = sb("GG", B)
        GB = sb("GB", B)
        GM = sb("GM", B)
        AW = sb("AW", 4 * B * RANK)
        AW4 = AW[:, :].rearrange("p (w b r) -> p w b r", w=4, b=B)
        BTT = sb("BTT", 4 * P)
        SC = sb("SC", P)
        ADA = sb("ADA", 6 * B)
        ADA6 = ADA[:, :].rearrange("p (s b) -> p s b", s=6)
        SH3 = sb("SH3", B)
        BP = sb("BP", 8)
        KM = sb("KM", 16)

        XT = PT[:, :].rearrange("p (t d) -> p t d", t=NT)
        XN = HN.rearrange("p (t d) -> p t d", t=NT)
        RX = T_.rearrange("p (t d) -> p t d", t=NT)
        HS = EX[:, :]
        GT = sb("GT", TE)
        LG = sb("LG", TE)
        G16 = PTB[:, 0:TOK]
        JK = PTB[:, TOK:TOK + TOK // 2].bitcast(BF16)
        GE = QT[0:TE, 0:6 * P]
        ONE = QT[0:TE, 6 * P:7 * P]
        SM = sb("SM", TE)
        CT = sb("CT", 8)
        CI = sb("CI", 4, I32)
        MS = sb("MS", 80)
        PRED = sb("PRED", 2, BF16)
        CB = sb("CB", 3 * P, BF16)
        OHB = AR1[:, 0:4 * TOK].bitcast(BF16).rearrange("p (t e n) -> p t e n", t=NT, e=E)
        OTB = AR2[:, 0:4 * TOK].bitcast(BF16).rearrange("p (e t n) -> p e t n", e=E, t=NT)
        XS = AR1[:, 4 * TOK:4 * TOK + 3 * NT * XW // 2].bitcast(BF16).rearrange("p (w t n) -> p w t n", w=3, t=NT)
        GR = AR1[:, 6 * TOK:6 * TOK + E * XW].rearrange("p (e n) -> p e n", e=E)
        YS = AR2[:, 4 * TOK:4 * TOK + 3 * TOK // 2].bitcast(BF16).rearrange("p (w e n) -> p w e n", w=3, e=E)
        YF = RS.rearrange("p (e n) -> p e n", e=E)
        YR = SQ.rearrange("p (e n) -> p e n", e=E)
        XG = OA[:, :]

        def gates(hf):
            return GT[:, hf * TH * E:(hf + 1) * TH * E].rearrange("p (t e) -> p t e", e=E).unsqueeze(2).broadcast_to([P, TH, NCAND, E])

        def gx(hf):
            return RS[:, hf * HALF:(hf + 1) * HALF].rearrange("p (t c e) -> p t c e", c=NCAND, e=E)

        OUT = XB[:, :]

        def half(ap, hf):
            return ap[:, hf * HALF:(hf + 1) * HALF]

        def bview(ap):
            return ap.rearrange("p (b n) -> p b n", b=BH)

        def bb(ap, hf):
            return ap[:, hf * BH:(hf + 1) * BH].unsqueeze(2).broadcast_to([P, BH, N])

        def bank(i):
            return PS[:, i, :]

        NORM_BANKS = {(0, 0): (0, 2), (0, 1): (1, 3), (1, 0): (2, 4), (1, 1): (3, 5),
                      (2, 0): (None, 2), (2, 1): (None, 3), (3, 0): (None, 2), (3, 1): (None, 3),
                      (4, 0): (2, 4), (4, 1): (3, 5)}

        def av_out(u):
            return PS[:, u % 2, 0:2 * BT * 2 * VW].rearrange("p (i b g d) -> p i b g d", i=2, b=BT, g=2)

        block = ctx.enter_context(nc.Block())

        @block.sync
        def _(sp):
            sp.dma_start(CD[:, :], condT).then_inc(sem("ld_first"), 16)
            sp.dma_start(V[:, :], vec).then_inc(sem("ld_first"), 16)
            sp.dma_start(CO[:, :], consts).then_inc(sem("ld_first"), 16)
            sp.dma_start(XA[:, :], xT).then_inc(sem("ld_x"), 16)
            sp.dma_start(W0[:, :], w0).then_inc(sem("ld_w0"), 16)
            sp.dma_start(W2[:, :], w2).then_inc(sem("ld_w2"), 16)
            sp.dma_start(W1[:, :], w1).then_inc(sem("ld_w1"), 16)
            sp.dma_start(W1B[:, :], l1b2).then_inc(sem("ld_w1"), 16)
            sp.dma_start(W3S[:, :], w3).then_inc(sem("ld_w3"), 16)
            sp.dma_start(FC2[:, :], wm2).then_inc(sem("ld_m"), 16)
            sp.dma_start(B1[:, :], b1s).then_inc(sem("ld_m"), 16)
            sp.dma_start(B2[:, :], b2s.partition_broadcast(P)).then_inc(sem("ld_m"), 16)
            sp.dma_start(CU[:, :], cands).then_inc(sem("ld_m"), 16)
            sp.dma_start(TRI[:, :], tril).then_inc(sem("ld_m"), 16)
            sp.wait_ge(sem("w_low"), 4)
            sp.dma_start(FC1, wm1).then_inc(sem("ld_m"), 16)
            if layers < 4:
                sp.wait_ge(sem("x_done"), 2 * layers)
                sp.dma_start(out, (XB if layers % 2 else XA)[:, :]).then_inc(sem("stored"), 16)
                sp.wait_ge(sem("stored"), 16)
                sp.wait_ge(sem("ld_m"), 96)
            else:
                for t in range(NT):
                    sp.wait_ge(sem("out_tile"), t + 1)
                    sp.dma_start(out[t * P:(t + 1) * P, :], OUT[:, t * P:(t + 1) * P]).then_inc(sem("stored"), 16)
                sp.wait_ge(sem("stored"), 16 * NT)

        @block.gpsimd
        def _(pool):
            nc.gpsimd.memset(EPSC[:, 0:1], EPS).then_inc(sem("eps_set"), 1)
            nc.gpsimd.memset(EPSC[:, 1:2], 0.5 * math.log(LN_SCALE)).then_inc(sem("eps_set"), 1)
            nc.gpsimd.memset(EPSC[:, 2:3], 0.0).then_inc(sem("eps_set"), 1)
            nc.gpsimd.memset(AR2[:, 0:NT * NH * BT * VW], 0.0).then_inc(sem("vbd_zero"), 1)
            pool.wait_ge(sem("vbd_zero"), 1)
            for b in range(BT):
                nc.gpsimd.memset(VBD[32 * b:32 * b + 32, :, :, b, HD:VW].rearrange("p t h d -> p (t h) d"), 1.0).then_inc(sem("vbd_ones"), 1)
                pool.wait_ge(sem("vbd_ones"), b + 1)
            nc.gpsimd.memset(PTB[:, :], 0.0).then_inc(sem("ptb_zero"), 1)
            if layers >= 4:
                g = nc.gpsimd

                def split(src, rest, parts, tag, n):
                    if len(parts) == 3:
                        g.tensor_copy(parts[0], src).then_inc(sem(tag + "_a"), 1)
                        pool.wait_ge(sem(tag + "_a"), n)
                    g.tensor_tensor(rest, src, parts[0], ALU.subtract).then_inc(sem(tag + "_b"), 1)
                    pool.wait_ge(sem(tag + "_b"), n)
                    g.tensor_copy(parts[-2], rest).then_inc(sem(tag + "_c"), 1)
                    pool.wait_ge(sem(tag + "_c"), n)
                    return g.tensor_tensor(parts[-1], rest, parts[-2], ALU.subtract)

                pool.wait_ge(sem("gate"), 1)
                g3 = GT[:, :].rearrange("p (t e) -> p t e", e=E)
                split(g3, LG[:, :].rearrange("p (t e) -> p t e", e=E), [XS[:, w, :, D:XW] for w in range(3)], "gs", 1).then_inc(sem("xs"), 2)
                pool.wait_ge(sem("xs"), 2)
                pool.wait_ge(sem("xn"), NT)
                split(XN, RX, [XS[:, w, :, 0:D] for w in range(3)], "xsp", 1).then_inc(sem("xs"), 2)
                for e in range(E):
                    pool.wait_ge(sem("yw"), 2 * e + 2)
                    g.tensor_tensor(YF[:, e, :], YR[:, e, :], YS[:, 0, e, :], ALU.subtract).then_inc(sem("yr"), 1)
                    pool.wait_ge(sem("yr"), e + 1)
                    g.tensor_copy(YS[:, 1, e, :], YF[:, e, :]).then_inc(sem("ym"), 1)
                    pool.wait_ge(sem("ym"), e + 1)
                    g.tensor_tensor(YS[:, 2, e, :], YF[:, e, :], YS[:, 1, e, :], ALU.subtract).then_inc(sem("ys"), 1)

        def second(pe, e):
            pe.wait_ge(sem("e_h"), e + 1)
            if e >= 2:
                pe.wait_ge(sem("e_y"), e - 1)
            for c in range(NC):
                m = pe.matmul(PS[:, 6 + e % 2, 0:P], HS[:, (e % 2) * FF + c * P:(e % 2) * FF + (c + 1) * P],
                              FC2[:, e * FF + c * P:e * FF + (c + 1) * P], start=(c == 0), stop=(c == NC - 1))
            m.then_inc(sem("e_fc2"), 1)

        @block.tensor
        def _(pe):
            mm = pe.matmul

            def norm(k, hf, x):
                cb, vb = NORM_BANKS[(k, hf)]
                n = 2 * k + hf + 1
                if k == 1:
                    pe.wait_ge(sem("shifted"), NU)
                if cb is not None:
                    mm(bank(cb), centre, half(x, hf), start=True, stop=True).then_inc(sem("centred"), 1)
                pe.wait_ge(sem("squared"), n)
                mm(bank(vb), mean_m, half(SQ, hf), start=True, stop=True).then_inc(sem("meansq"), 1)

            def conditioning():
                pe.wait_ge(sem("ld_first"), 48)
                pe.wait_ge(sem("ld_w0"), 16)
                mm(PS[:, 4, 0:P], W0[:, 0:P], CD[:, :], start=True, stop=True)
                mm(PS[:, 4, P:2 * P], W0[:, P:2 * P], CD[:, :], start=True, stop=True).then_inc(sem("c_gb"), 1)
                mm(PS[:, 5, 0:P], centre, CD[:, :], start=True, stop=True).then_inc(sem("c_cen"), 1)

            def conditioning2():
                pe.wait_ge(sem("c_sq"), 1)
                mm(PS[:, 5, P:2 * P], mean_m, CN[:, 0:P], start=True, stop=True).then_inc(sem("c_var"), 1)
                pe.wait_ge(sem("c_ln"), 1)
                pe.wait_ge(sem("ld_w1"), 32)
                mm(PS[:, 5, 2 * P:3 * P], W1[:, 0:P], CN[:, 4 * P:5 * P], start=True, stop=True).then_inc(sem("c_h"), 1)
                pe.wait_ge(sem("c_silu"), 1)
                pe.wait_ge(sem("ld_w2"), 16)
                pe.wait_ge(sem("c_gb_used"), 1)
                for s in range(6):
                    m = mm(PS[:, 4 if s < 4 else 6, (s % 4) * P:(s % 4 + 1) * P],
                           W2[:, 4 * P + 2 * FF + s * P:4 * P + 2 * FF + (s + 1) * P], SC[:, :], start=True, stop=True)
                    if s == 3:
                        m.then_inc(sem("c_ada"), 1)
                pe.wait_ge(sem("ld_w3"), 16)
                mm(PS[:, 6, 2 * P:3 * P], W3S[:, 0:P], SC[:, :], start=True, stop=True).then_inc(sem("c_ada"), 1)
                mm(PS[:, 7, 0:1], W0[:, 5 * P:6 * P], vcol("l0_bv"), start=True, stop=True)
                mm(PS[:, 7, 1:2], W2[:, 3 * P:4 * P], vcol("l2_bv"), start=True, stop=True).then_inc(sem("c_bv"), 1)
                pe.wait_ge(sem("c_gelu"), 1)
                pe.wait_ge(sem("c_low_free"), 1)
                for w in range(4):
                    for r in range(RANK):
                        c = P + (w * RANK + r) * P
                        m = mm(PS[:, 4 + w, r * B:r * B + P], W1[:, c:c + P], HC[:, :], start=True, stop=True)
                    m.then_inc(sem("w_low"), 1)
                pe.wait_ge(sem("low_sb"), 4)
                for i, w in enumerate((1, 3)):
                    for hf in range(2):
                        pe.transpose(PS[:, 4, (2 * i + hf) * P:(2 * i + hf + 1) * P],
                                     AW[:, (w * 2 + hf) * P:(w * 2 + hf + 1) * P], ident).then_inc(sem("low_t"), 1)

            def attention_in(l, Wt, qk_banks, v_bank):
                for hf in range(2):
                    pe.wait_ge(sem("hn"), 2 * l + hf + 1)
                    mm(bank(qk_banks[0] + hf), Wt[:, 0:P], half(HN, hf), start=True, stop=True).then_inc(sem("q_ps"), 1)
                    mm(bank(qk_banks[1] + hf), Wt[:, P:2 * P], half(HN, hf), start=True, stop=True).then_inc(sem("k_ps"), 1)

            def values(l, Wt, v_bank):
                for hf in range(2):
                    if l == 1:
                        pe.wait_ge(sem("qb"), hf + 1)
                    for i in range(TH):
                        t = hf * TH + i
                        m = mm(PS[:, v_bank + hf, i * P:(i + 1) * P], HN[:, t * P:(t + 1) * P], Wt[:, 2 * P:3 * P],
                               start=True, stop=True)
                    m.then_inc(sem("v_ps"), 1)

            def attention(l, Wp):
                for s in range(NU + 2):
                    if s < NU:
                        tp, gp = s // 2, s % 2
                        if s == 0:
                            pe.wait_ge(sem("q_sb"), 2 * l + 2)
                            pe.wait_ge(sem("kbd"), 8 * l + 8)
                            pe.wait_ge(sem("vbd"), 8 * l + 8)
                        if s >= 2:
                            pe.wait_ge(sem("shifted"), NU * l + s - 1)
                        for t in (2 * tp, 2 * tp + 1):
                            for g in (2 * gp, 2 * gp + 1):
                                for b in range(BT):
                                    c = t * P + 32 * b
                                    m = mm(PS[32 * b:32 * b + 32, 4 + g, (t % 2) * P:(t % 2 + 1) * P],
                                           QT[32 * g:32 * g + 32, c:c + 32], KBD[32 * g:32 * g + 32, :, c:c + 32],
                                           start=True, stop=True)
                        m.then_inc(sem("scores"), 1)
                    if s >= 2:
                        u = s - 2
                        tp, gp = u // 2, u % 2
                        pe.wait_ge(sem("pt"), NU * l + u + 1)
                        if u >= 2:
                            pe.wait_ge(sem("normed"), NU * l + u - 1)
                        for g in range(2):
                            for i in range(2):
                                for hh in range(NG):
                                    m = mm(av_out(u)[32 * hh:32 * hh + 32, i, :, g, :],
                                           PTt[:, u % 2, ((g * 2 + i) * NG + hh) * 32:((g * 2 + i) * NG + hh + 1) * 32],
                                           VBD[:, 2 * tp + i, NG * (2 * gp + g) + hh, :, :], start=True, stop=True)
                        m.then_inc(sem("av"), 1)
                    if s in (NU // 2 + 3, NU + 1):
                        project(l, 0 if s < NU else 1, Wp)

            def project(l, hf, Wp):
                pe.wait_ge(sem("oT"), NT // 2 * l + 2 * (hf + 1))
                mm(bank(2 + hf), Wp, half(OA, hf), start=True, stop=True).then_inc(sem("proj"), 1)

            conditioning()
            pe.wait_ge(sem("ld_x"), 16)
            mm(bank(0), centre, half(XA, 0), start=True, stop=True).then_inc(sem("centred"), 1)
            mm(bank(1), centre, half(XA, 1), start=True, stop=True).then_inc(sem("centred"), 1)
            for hf in range(2):
                pe.wait_ge(sem("squared"), hf + 1)
                mm(bank(2 + hf), mean_m, half(SQ, hf), start=True, stop=True).then_inc(sem("meansq"), 1)
            conditioning2()
            pe.wait_ge(sem("low_tsb"), 2)
            attention_in(0, W0[:, 2 * P:5 * P], (4, 6), 2)
            values(0, W0[:, 2 * P:5 * P], 2)
            attention(0, W0[:, 5 * P:6 * P])
            for hf in range(2):
                pe.wait_ge(sem("h1"), hf + 1)
                norm(1, hf, XB)
            if layers >= 2:
                for hf in range(2):
                    cols = slice(hf * BH * RANK, (hf + 1) * BH * RANK)
                    a1 = AW4[:, 0, hf * BH:(hf + 1) * BH, :].rearrange("p b r -> p (b r)")
                    a2 = AW4[:, 2, hf * BH:(hf + 1) * BH, :].rearrange("p b r -> p (b r)")
                    u, w = 4 + 2 * hf, 5 + 2 * hf
                    pe.wait_ge(sem("x_done"), hf + 1)
                    mm(bank(u), a1, half(XB, hf), start=True, stop=True).then_inc(sem("y1"), 1)
                    pe.wait_ge(sem("y1m"), hf + 1)
                    mm(bank(w), BTT[:, hf * P:(hf + 1) * P], half(T_, hf), start=True, stop=True).then_inc(sem("y2"), 1)
                    pe.wait_ge(sem("y2g"), hf + 1)
                    mm(bank(u), a2, half(RS, hf), start=True, stop=True).then_inc(sem("y3"), 1)
                    pe.wait_ge(sem("y3m"), hf + 1)
                    mm(bank(w), BTT[:, (2 + hf) * P:(3 + hf) * P], half(T_, hf), start=True, stop=True).then_inc(sem("y4"), 1)
            if layers >= 3:
                for hf in range(2):
                    norm(2, hf, XA)
                attention_in(1, W2[:, 0:3 * P], (4, 6), 4)
                for hf in range(2):
                    pe.wait_ge(sem("q_sq"), hf + 1)
                    mm(bank(0 + hf), mean8, half(SQ, hf), start=True, stop=True).then_inc(sem("qk_ms"), 1)
                    pe.wait_ge(sem("k_sq"), hf + 1)
                    mm(bank(2 + hf), mean8, half(T_, hf), start=True, stop=True).then_inc(sem("qk_ms"), 1)
                values(1, W2[:, 0:3 * P], 4)
                attention(1, W2[:, 3 * P:4 * P])
                for hf in range(2):
                    norm(3, hf, XB)
                for hf in range(2):
                    pe.wait_ge(sem("hn"), 4 + hf + 1)
                    for c in range(NC):
                        if hf == 1:
                            pe.wait_ge(sem("hid"), c + 1)
                        mm(bank(4 + c), W2[:, 4 * P + c * P:4 * P + (c + 1) * P], half(HN, hf),
                           start=True, stop=True).then_inc(sem("fc1_ps"), 1)
                for hf in range(2):
                    for c in range(NC):
                        pe.wait_ge(sem("hid"), NC * hf + c + 1)
                        m = mm(bank(hf), W2[:, 4 * P + FF + c * P:4 * P + FF + (c + 1) * P], half(HID[:, c, :], hf),
                               start=(c == 0), stop=(c == NC - 1))
                    m.then_inc(sem("fc2_ps"), 1)
            if layers >= 4:
                WQ3 = W3S[:, P:P + W3]
                WK3 = W3S[:, P + W3:P + 2 * W3]
                WV3 = W3S[:, P + 2 * W3:P + 3 * W3]
                WO3 = W3S[:, P + 3 * W3:P + 4 * W3]
                for hf in range(2):
                    pe.wait_ge(sem("x_done"), 4 + hf + 1)
                    norm(4, hf, XB)
                pe.wait_ge(sem("w3c"), 2)

                def queries(t):
                    pe.wait_ge(sem("hn"), 6 + (1 if t < TH else 2))
                    if t >= 1:
                        pe.wait_ge(sem("q3n"), t)
                    for i in range(2):
                        m = mm(bank(i), HN[:, t * P:(t + 1) * P], WQ3[:, i * 512:(i + 1) * 512], start=True, stop=True)
                    m.then_inc(sem("q3"), 1)

                def keys(t):
                    if t == 0:
                        pe.wait_ge(sem("hn"), 8)
                    if t >= 1:
                        pe.wait_ge(sem("k3n"), t)
                    for i in range(2):
                        m = mm(bank(2 + i), HN[:, t * P:(t + 1) * P], WK3[:, i * 512:(i + 1) * 512], start=True, stop=True)
                    m.then_inc(sem("k3"), 1)

                def values3(t):
                    if t >= 1:
                        pe.wait_ge(sem("k3t"), 2 * t)
                    for i in range(2):
                        m = mm(bank(4 + i), HN[:, t * P:(t + 1) * P], WV3[:, i * 512:(i + 1) * 512], start=True, stop=True)
                    m.then_inc(sem("v3"), 1)

                def turn(t, src, ready, n_ready, free, n_free, done):
                    pe.wait_ge(sem(ready), n_ready)
                    for k in range(2):
                        pe.wait_ge(sem(free), n_free[k])
                        for c in range(4 * k, 4 * k + 4):
                            m = pe.transpose(PS[:, 4 + k, (c % 4) * P:(c % 4 + 1) * P], src[:, c * P:(c + 1) * P], ident)
                        m.then_inc(sem(done), 1)

                def scores3(t):
                    if t >= 2:
                        pe.wait_ge(sem("x3"), t - 1)
                    if t >= 3:
                        pe.wait_ge(sem("tail_read"), t - 2)
                    for c in range(C3):
                        if c % 4 == 0:
                            pe.wait_ge(sem("k3t"), 2 * t + c // 4 + 1)
                        for u in range(2):
                            for b in range(BT):
                                r = slice(64 * u, 64 * u + 64)
                                n = slice(32 * b, 32 * b + 32)
                                m = mm(PS[32 * b:32 * b + 32, 6 + u, c * 32:c * 32 + 32], QK3[r, t % 2, 0, c, n],
                                       QK3[r, t % 2, 1, c, n], start=True, stop=True)
                    m.then_inc(sem("scores3"), 1)

                def av3(t, rnd):
                    if rnd == 0:
                        pe.wait_ge(sem("pt3"), t + 1)
                        if t + 1 < NT:
                            pe.wait_ge(sem("shifted3"), t + 2)
                        else:
                            pe.wait_ge(sem("x3"), t)
                            pe.wait_ge(sem("tail_read"), t - 1)
                    else:
                        pe.wait_ge(sem("o3"), 2 * t + 1)
                    for c in range(4 * rnd, 4 * rnd + 4):
                        for u in range(2):
                            h = 2 * c + u
                            m = mm(PS[64 * u:64 * u + 64, 6 + (c % 4) // 2, 256 + (c % 2) * P:256 + (c % 2 + 1) * P],
                                   V3[:, t % 3, h * HD3:(h + 1) * HD3], PTB3[:, t % 2, h, :], start=True, stop=True)
                    m.then_inc(sem("av3"), 1)

                def out3(t):
                    pe.wait_ge(sem("o3"), 2 * t + 2)
                    for c in range(C3):
                        m = mm(PS[:, 7, 256:256 + P], WO3[:, c * P:(c + 1) * P], O3[:, c, :], start=(c == 0), stop=(c == C3 - 1))
                    m.then_inc(sem("out3"), 1)

                def tail(t):
                    pe.wait_ge(sem("x3"), t + 1)
                    mm(PS[:, 6, 256:256 + E], XA[:, t * P:(t + 1) * P], W3S[:, P + 4 * W3:P + 4 * W3 + E], start=True, stop=True)
                    pe.transpose(PS[:, 6, 384:512], XA[:, t * P:(t + 1) * P], ident).then_inc(sem("tail"), 1)

                queries(0)
                keys(0)
                values3(0)
                turn(0, T_, "q3n", 1, "v3s", (1, 1), "q3tp")
                turn(0, RS, "k3n", 1, "q3t", (1, 2), "k3tp")
                for t in range(NT + 1):
                    if t < NT:
                        scores3(t)
                    if t + 1 < NT:
                        queries(t + 1)
                        values3(t + 1)
                    if t >= 1:
                        av3(t - 1, 0)
                    if t + 1 < NT:
                        keys(t + 1)
                    if t >= 1:
                        av3(t - 1, 1)
                    if t + 1 < NT:
                        turn(t + 1, T_, "q3n", t + 2, "v3s", (t + 2, t + 2), "q3tp")
                    if t >= 1:
                        out3(t - 1)
                    if t >= 2:
                        tail(t - 2)
                    if t + 1 < NT:
                        turn(t + 1, RS, "k3n", t + 2, "q3t", (2 * t + 3, 2 * t + 4), "k3tp")
                pe.wait_ge(sem("tail_read"), NT - 1)
                tail(NT - 1)
                pe.wait_ge(sem("gate"), 1)
                for t in range(NT):
                    if t % TH == 0:
                        pe.wait_ge(sem("gate_x"), t // TH + 1)
                    m = pe.transpose(PS[:, t // 4, (t % 4) * P:(t % 4 + 1) * P], RS[:, t * P:(t + 1) * P], ident)
                m.then_inc(sem("gate_t"), 1)
                pe.transpose(PS[0:TE, 2, 0:P], GT[:, :], ident).then_inc(sem("gate_t"), 1)
                pe.wait_ge(sem("cb"), 3)
                for i in range(DIG):
                    pe.wait_ge(sem("pred"), i + 1)
                    mm(PS[:, 3, 0:1], CB[:, 2 * P:3 * P], PRED[:, 0:1], start=True, stop=True).then_inc(sem("digit"), 1)
                pe.wait_ge(sem("prefix"), 2)
                ends = GE[:, 3 * P - 1:4 * P:P]
                mm(PS[0:TE, 3, 0:2], TRI[0:TE, 0:TE], ends, start=True, stop=True)
                mm(PS[0:TE, 3, 2:4], TRI[0:TE, TE:2 * TE], ends, start=True, stop=True).then_inc(sem("offsets"), 1)
                pe.wait_ge(sem("slots"), 1)
                pe.transpose(PS[:, 3, 0:TE], GE[:, 4 * P:5 * P], ident[0:TE, 0:TE]).then_inc(sem("slots_t"), 1)
                pe.wait_ge(sem("xs"), 4)
                otp = PS[:, 1, :].bitcast(BF16)
                for s in range(E + 3):
                    if s < E:
                        e = s
                        pe.wait_ge(sem("onehot"), e + 1)
                        if e >= 1:
                            pe.wait_ge(sem("gr"), e)
                        for t in range(NT):
                            for w in range(3):
                                m = mm(PS[:, 0, 0:XW], OHB[:, t, e, :], XS[:, w, t, :], start=(t == 0 and w == 0),
                                       stop=(t == NT - 1 and w == 2))
                        m.then_inc(sem("gathered"), 1)
                        if e >= 1:
                            pe.wait_ge(sem("ot"), e)
                        for t in range(NT):
                            m = pe.transpose(otp[:, t * P:(t + 1) * P], OHB[:, t, e, :], CB[:, 0:P])
                        m.then_inc(sem("ot_ps"), 1)
                        pe.wait_ge(sem("gr"), e + 1)
                        if e >= 1:
                            pe.wait_ge(sem("xg"), e)
                        pe.transpose(PS[:, 2, 0:P], GR[:, e, 0:P], ident).then_inc(sem("xgt"), 1)
                    if 1 <= s <= E:
                        e = s - 1
                        pe.wait_ge(sem("xg"), e + 1)
                        if e >= 2:
                            pe.wait_ge(sem("e_b1"), e - 1)
                        if e == 0:
                            pe.wait_ge(sem("ld_m"), 96)
                        for c in range(NC):
                            m = mm(PS[:, 3 + e % 2, c * P:(c + 1) * P], FC1[:, e * FF + c * P:e * FF + (c + 1) * P],
                                   XG[:, e * P:(e + 1) * P], start=True, stop=True)
                        m.then_inc(sem("e_fc1"), 1)
                    if 2 <= s <= E + 1:
                        e = s - 2
                        pe.wait_ge(sem("e_h"), e + 1)
                        if e >= 1:
                            pe.wait_ge(sem("e_y"), e)
                        for c in range(NC):
                            m = mm(PS[:, 5, 0:P], HS[:, (e % 2) * FF + c * P:(e % 2) * FF + (c + 1) * P],
                                   FC2[:, e * FF + c * P:e * FF + (c + 1) * P], start=(c == 0), stop=(c == NC - 1))
                        m.then_inc(sem("e_fc2"), 1)
                    if s >= 3:
                        e = s - 3
                        pe.wait_ge(sem("ys"), e + 1)
                        if e == 0:
                            pe.wait_ge(sem("tail_read"), NT)
                        for t in range(NT):
                            for w in range(3):
                                m = mm(PS[:, 6 + t // 4, (t % 4) * P:(t % 4 + 1) * P], OTB[:, e, t, :], YS[:, w, e, :],
                                       start=(e == 0 and w == 0 and t % 4 == 0), stop=(e == E - 1 and w == 2),
                                       skip_group_check=True)
                            if t % 4 == 3:
                                m.then_inc(sem("scattered"), 1)

        @block.scalar
        def _(act):
            A = nc.scalar.activation
            eps, half_ln, zero = (EPSC[:, i:i + 1] for i in range(3))

            def rsqrt(out_, in_, w_in, n_in, scale, bias, out_bias, tag, n):
                act.wait_ge(sem(w_in), n_in)
                A(out_, in_, ACT.Ln, bias=bias, scale=scale).then_inc(sem(tag + "_ln"), 1)
                act.wait_ge(sem(tag + "_ln"), n)
                A(out_, out_, ACT.Exp, bias=out_bias, scale=-0.5).then_inc(sem(tag), 1)

            def norm_sq(k, hf, x=None, w=None, n_w=None):
                n = 2 * k + hf + 1
                if x is None:
                    cb = NORM_BANKS[(k, hf)][0]
                    act.wait_ge(sem("centred"), {0: 0, 1: 2, 4: 4}[k] + hf + 1)
                    A(half(SQ, hf), bank(cb), ACT.Square).then_inc(sem("squared"), 1)
                else:
                    act.wait_ge(sem(w), n_w)
                    A(half(SQ, hf), half(x, hf), ACT.Square).then_inc(sem("squared"), 1)

            def norm_rs(k, hf):
                n = 2 * k + hf + 1
                vb = NORM_BANKS[(k, hf)][1]
                if k in (2, 3):
                    rsqrt(half(RS, hf), half(RS, hf), "floored", 2 * (k - 2) + hf + 1, LN_SCALE, zero, half_ln, "rstd", n)
                else:
                    rsqrt(half(RS, hf), bank(vb), "meansq", n, 1.0, eps, zero, "rstd", n)

            def exp_rows(l):
                for u in range(NU):
                    act.wait_ge(sem("shifted"), NU * l + u + 1)
                    A(EXB[:, u % 2, :], EXB[:, u % 2, :], ACT.Exp).then_inc(sem("exped"), 1)

            nc.scalar.preload_act_table_set("natural_log_exp_and_others")
            act.wait_ge(sem("ld_first"), 48)
            act.wait_ge(sem("eps_set"), 3)
            act.wait_ge(sem("c_cen"), 1)
            A(CN[:, 0:P], PS[:, 5, 0:P], ACT.Square).then_inc(sem("c_sq"), 1)
            A(CN[:, 5 * P:6 * P], CD[:, :], ACT.Exp, scale=-1.0).then_inc(sem("c_exp"), 1)
            norm_sq(0, 0)
            norm_sq(0, 1)
            rsqrt(CN[:, P:2 * P], PS[:, 5, P:2 * P], "c_var", 1, 1.0, eps, zero, "c_rs", 1)
            norm_rs(0, 0)
            norm_rs(0, 1)
            act.wait_ge(sem("c_h"), 1)
            A(HC[:, :], PS[:, 5, 2 * P:3 * P], ACT.Gelu, bias=vcol("l1_b1")).then_inc(sem("c_gelu"), 1)
            nc.scalar.preload_act_table_set("natural_log_exp_and_others")
            act.wait_ge(sem("low_t"), 4)
            for i in range(2):
                A(BTT[:, i * 256:(i + 1) * 256], PS[:, 4, i * 256:(i + 1) * 256], ACT.Identity).then_inc(sem("low_tsb"), 1)
            for hf in range(2):
                act.wait_ge(sem("q_ps"), hf + 1)
                A(half(QT, hf), bank(4 + hf), ACT.Identity, bias=vcol("l0_bq")).then_inc(sem("q_sb"), 1)
                act.wait_ge(sem("k_ps"), hf + 1)
                A(half(SQ, hf), bank(6 + hf), ACT.Identity, bias=vcol("l0_bk")).then_inc(sem("k_sb"), 1)

            def values_out(l, v_bank):
                if l == 0:
                    act.wait_ge(sem("vbd_ones"), 4)
                for hf in range(2):
                    act.wait_ge(sem("v_ps"), 2 * l + hf + 1)
                    for b in range(BT):
                        r = slice(32 * b, 32 * b + 32)
                        A(VBD[r, hf * TH:(hf + 1) * TH, :, b, 0:HD],
                          PS[r, v_bank + hf, :].rearrange("p (t h d) -> p t h d", t=TH, h=NH),
                          ACT.Identity).then_inc(sem("vbd"), 1)

            values_out(0, 2)
            exp_rows(0)
            norm_sq(1, 0)
            norm_rs(1, 0)
            norm_sq(1, 1)
            norm_rs(1, 1)
            if layers >= 2:
                for hf in range(2):
                    act.wait_ge(sem("y2"), hf + 1)
                    A(half(RS, hf), bank(5 + 2 * hf), ACT.Gelu).then_inc(sem("y2g"), 1)
                nc.scalar.preload_act_table_set("natural_log_exp_and_others")
            if layers >= 3:
                for hf in range(2):
                    norm_sq(2, hf, XA, "x_done", 2 + hf + 1)
                for hf in range(2):
                    norm_rs(2, hf)
                for hf in range(2):
                    act.wait_ge(sem("q_ps"), 2 + hf + 1)
                    A(half(QT, hf), bank(4 + hf), ACT.Identity, bias=vcol("l2_bq")).then_inc(sem("qb"), 1)
                    act.wait_ge(sem("qb"), hf + 1)
                    A(half(SQ, hf), half(QT, hf), ACT.Square).then_inc(sem("q_sq"), 1)
                    act.wait_ge(sem("k_ps"), 2 + hf + 1)
                    A(half(T_, hf), bank(6 + hf), ACT.Square, bias=vcol("l2_bk")).then_inc(sem("k_sq"), 1)
                values_out(1, 4)
                for i in range(4):
                    hf, s = i // 2, i % 2
                    buf = half(RS, hf) if s == 0 else half(SQ, hf)
                    rsqrt(buf, buf, "qk_floor", i + 1, LN_SCALE, zero, half_ln, "qk_rs", i + 1)
                exp_rows(1)
                for hf in range(2):
                    norm_sq(3, hf, XB, "h1", 2 + hf + 1)
                    norm_rs(3, hf)
                for hf in range(2):
                    for c in range(NC):
                        act.wait_ge(sem("fc1_ps"), NC * hf + c + 1)
                        A(half(HID[:, c, :], hf), bank(4 + c), ACT.Gelu_apprx_tanh,
                          bias=vcol(f"l2_bfc1_{c}")).then_inc(sem("hid"), 1)
                nc.scalar.preload_act_table_set("natural_log_exp_and_others")
            if layers >= 4:
                for hf in range(2):
                    norm_sq(4, hf)
                    norm_rs(4, hf)
                st = [ST[:, i * H3:(i + 1) * H3] for i in range(4)]

                def square3(t, s, nm, w_in, n_in):
                    act.wait_ge(sem(nm), t + 1)
                    if n_in:
                        act.wait_ge(sem(w_in), n_in)
                    A(SQ.rearrange("p (k n) -> p k n", k=2), PS[:, 2 * s:2 * s + 2, :], ACT.Square).then_inc(sem(nm + "sq"), 1)

                def turned3(t, s, g, b_, nm):
                    for k in range(2):
                        act.wait_ge(sem(nm + "p"), 2 * t + k + 1)
                        A(QK3[:, t % 2, s, 4 * k:4 * k + 4, :].rearrange("p c n -> p (c n)"), bank(4 + k),
                          ACT.Identity, bias=vcol(b_), scale=vcol(g)).then_inc(sem(nm), 1)

                def exp3(t):
                    act.wait_ge(sem("shifted3"), t + 1)
                    A(EXB[:, 0, :], EXB[:, 0, :], ACT.Exp, scale=1.0 / math.sqrt(HD3)).then_inc(sem("exped3"), 1)

                def out3(t, rnd):
                    act.wait_ge(sem("av3"), 2 * t + rnd + 1)
                    if t >= 1:
                        act.wait_ge(sem("out3"), t)
                    A(O3[:, 4 * rnd:4 * rnd + 4, :].rearrange("p (k c) n -> p k (c n)", k=2), PS[:, 6:8, 256:512],
                      ACT.Identity).then_inc(sem("o3"), 1)

                for t in range(-1, NT + 1):
                    if 0 <= t < NT:
                        exp3(t)
                    if t + 1 < NT:
                        square3(t + 1, 0, "q3", "k3sum", t + 1)
                        act.wait_ge(sem("v3"), t + 2)
                        if t >= 2:
                            act.wait_ge(sem("av3"), 2 * (t - 1))
                        A(V3[:, (t + 1) % 3, :].rearrange("p (k n) -> p k n", k=2), PS[:, 4:6, :],
                          ACT.Identity).then_inc(sem("v3s"), 1)
                        rsqrt(st[2], st[0], "q3sum", t + 2, 1.0 / HD3, eps, zero, "q3rs", t + 2)
                    if t >= 1:
                        out3(t - 1, 0)
                    if t + 1 < NT:
                        square3(t + 1, 1, "k3", "q3sum", t + 2)
                        rsqrt(st[3], st[1], "k3sum", t + 2, 1.0 / HD3, eps, zero, "k3rs", t + 2)
                    if t >= 1:
                        out3(t - 1, 1)
                    if t + 1 < NT:
                        turned3(t + 1, 0, "l3_qg", "l3_qb", "q3t")
                        turned3(t + 1, 1, "l3_kg", "l3_kb", "k3t")
                act.wait_ge(sem("g_shift"), 1)
                A(GT[:, :], GT[:, :], ACT.Exp).then_inc(sem("g_exp"), 1)
                rsqrt(MS[:, 40:48], MS[:, 8:24].rearrange("p (t s) -> p t s", s=2)[:, :, 1], "mv", NT, 1.0, eps, zero, "m_rs", 1)
                act.wait_ge(sem("gate"), 1)
                act.wait_ge(sem("gate_x"), 1)
                A(gx(1), gates(1), ACT.Identity).then_inc(sem("gate_x"), 1)
                act.wait_ge(sem("gate_t"), 1)
                A(G16.rearrange("p (k n) -> p k n", k=2), PS[:, 0:2, :], ACT.Identity).then_inc(sem("g16"), 1)
                act.wait_ge(sem("m_nb"), 1)
                for t in range(NT):
                    A(XN[:, t, :], XT[:, t, :], ACT.Identity, bias=MS[:, 48 + t:49 + t], scale=MS[:, 40 + t:41 + t]).then_inc(sem("xn"), 1)
                for s in range(E + 1):
                    if s < E:
                        e = s
                        act.wait_ge(sem("gathered"), e + 1)
                        A(GR[:, e, :], PS[:, 0, 0:XW], ACT.Identity).then_inc(sem("gr"), 1)
                    if s >= 1:
                        e = s - 1
                        act.wait_ge(sem("e_b1"), e + 1)
                        h = HS[:, (e % 2) * FF:(e % 2 + 1) * FF]
                        A(h, h, ACT.Gelu_apprx_tanh).then_inc(sem("e_h"), 1)
                    if s < E:
                        e = s
                        act.wait_ge(sem("xgt"), e + 1)
                        A(XG[:, e * P:(e + 1) * P], PS[:, 2, 0:P], ACT.Identity, bias=vcol("l3_mb"),
                          scale=vcol("l3_mg")).then_inc(sem("xg"), 1)
                        act.wait_ge(sem("ot_ps"), e + 1)
                        A(OTB[:, e, :, :].rearrange("p t n -> p (t n)"), PS[:, 1, :].bitcast(BF16), ACT.Identity).then_inc(sem("ot"), 1)

        @block.vector
        def _(dve):
            v = nc.vector
            TT, TS, STT = v.tensor_tensor, v.tensor_scalar, v.scalar_tensor_tensor
            step = [0]

            def then(ins):
                step[0] += 1
                ins.then_inc(sem("dve_step"), 1)
                dve.wait_ge(sem("dve_step"), step[0])

            def centred_times(k, hf):
                dve.wait_ge(sem("rstd"), 2 * k + hf + 1)
                then(TT(half(T_, hf), bank(NORM_BANKS[(k, hf)][0]), half(RS, hf), ALU.mult))

            dve.wait_ge(sem("ld_first"), 48)
            dve.wait_ge(sem("c_gb"), 1)
            then(TS(GM[:, :], PS[:, 4, 0:B], vcol("l0_bg"), None, ALU.add))
            then(TS(GB[:, :], PS[:, 4, P:P + B], vcol("l0_bb"), None, ALU.add))
            TS(GG[:, :], GM[:, :], vcol("l0_lng"), None, ALU.mult).then_inc(sem("c_gb_used"), 1)
            then(STT(GB[:, :], GM[:, :], vcol("l0_lnb"), GB[:, :], ALU.mult, ALU.add))
            then(TT(KM[:, 8:9], vcol("l2_gq"), vcol("l2_gk"), ALU.mult))
            then(TS(KM[:, 8:9], KM[:, 8:9], 1.0 / math.sqrt(HD), None, ALU.mult))
            for h in range(4):
                m = TT(KM[:, 4 + h:5 + h], KM[:, 8:9], vcol(f"mask_{h}"), ALU.mult)
            then(m)
            dve.wait_ge(sem("c_exp"), 1)
            then(TS(CN[:, 5 * P:6 * P], CN[:, 5 * P:6 * P], 1.0, None, ALU.add))
            then(v.reciprocal(CN[:, 5 * P:6 * P], CN[:, 5 * P:6 * P]))
            TT(SC[:, :], CD[:, :], CN[:, 5 * P:6 * P], ALU.mult).then_inc(sem("c_silu"), 1)
            dve.wait_ge(sem("c_rs"), 1)
            then(TT(CN[:, 4 * P:5 * P], PS[:, 5, 0:P], CN[:, P:2 * P], ALU.mult))
            TS(CN[:, 4 * P:5 * P], CN[:, 4 * P:5 * P], vcol("l1_lng"), vcol("l1_lnb"), ALU.mult, ALU.add).then_inc(sem("c_ln"), 1)
            for hf in range(2):
                centred_times(0, hf)
                then(TT(bview(half(T_, hf)), bview(half(T_, hf)), bb(GG, hf), ALU.mult))
                TT(bview(half(HN, hf)), bview(half(T_, hf)), bb(GB, hf), ALU.add).then_inc(sem("hn"), 1)
            dve.wait_ge(sem("c_ada"), 1)
            bada = V[:, VCOL["l2_bada_0"]:VCOL["l2_bada_0"] + 6]
            TT(ADA6[:, 0:4, :], PS[:, 4, :].rearrange("p (s b) -> p s b", s=4)[:, :, 0:B],
               bada[:, 0:4].unsqueeze(2).broadcast_to([P, 4, B]), ALU.add)
            dve.wait_ge(sem("c_ada"), 2)
            then(TT(ADA6[:, 4:6, :], PS[:, 6, 0:2 * P].rearrange("p (s b) -> p s b", s=2)[:, :, 0:B],
                    bada[:, 4:6].unsqueeze(2).broadcast_to([P, 2, B]), ALU.add))
            TS(ADA6[:, 1, :], ADA6[:, 1, :], 1.0, vcol("l2_g1"), ALU.add, ALU.mult)
            TS(ADA6[:, 4, :], ADA6[:, 4, :], 1.0, vcol("l2_g2"), ALU.add, ALU.mult)
            TS(SH3[:, :], PS[:, 6, 2 * P:2 * P + B], vcol("l3_bada"), vcol("l3_ln1b"), ALU.add, ALU.add)
            dve.wait_ge(sem("c_bv"), 1)
            then(TS(BP[:, 0:1], PS[:, 7, 0:1], 1.0 / math.sqrt(D), vcol("l0_bp"), ALU.mult, ALU.add))
            TS(BP[:, 1:2], PS[:, 7, 1:2], vcol("l2_bproj"), None, ALU.add).then_inc(sem("c_low_free"), 1)
            for w in range(4):
                dve.wait_ge(sem("w_low"), w + 1)
                TT(AW4[:, w, :, :].rearrange("p b r -> p r b"), PS[:, 4 + w, 0:RANK * B].rearrange("p (r b) -> p r b", r=RANK),
                   W1B[:, w * RANK:(w + 1) * RANK].unsqueeze(2).broadcast_to([P, RANK, B]), ALU.add).then_inc(sem("low_sb"), 1)
            for hf in range(2):
                dve.wait_ge(sem("k_sb"), hf + 1)
                for h in range(NG):
                    TS(half(KBD[:, h, :], hf), half(SQ, hf), vcol(f"mask_{h}"), None, ALU.mult).then_inc(sem("kbd"), 1)

            def attention(l, att_scale, residual):
                for s in range(NU + 3):
                    if s < NU:
                        u, gp = s, s % 2
                        dve.wait_ge(sem("scores"), NU * l + u + 1)
                        sc = PS[:, 4 + 2 * gp:6 + 2 * gp, 0:2 * P].rearrange("p g (x n) -> p g x n", n=N)
                        mx = MX[:, (u % 2) * NH:(u % 2 + 1) * NH]
                        then(v.tensor_reduce(mx, sc, AX_X, ALU.max))
                        TT(EXB[:, u % 2, :].rearrange("p (g x n) -> p g x n", g=2, n=N), sc,
                           mx.rearrange("p (g x) -> p g x", g=2).unsqueeze(3).broadcast_to([P, 2, NH // 2, N]),
                           ALU.subtract).then_inc(sem("shifted"), 1)
                    if 1 <= s <= NU:
                        u = s - 1
                        dve.wait_ge(sem("exped"), NU * l + u + 1)
                        if u >= 2:
                            dve.wait_ge(sem("av"), NU * l + u - 1)
                        v.transpose(PTt[:, u % 2, :], EXB[:, u % 2, :]).then_inc(sem("pt"), 1)
                    if s >= 3:
                        u = s - 3
                        tp, gp = u // 2, u % 2
                        dve.wait_ge(sem("av"), NU * l + u + 1)
                        av = av_out(u).rearrange("p i b g d -> p (i b) g d")
                        rec = REC[:, (u % 2) * NH:(u % 2 + 1) * NH]
                        then(v.reciprocal(rec, PS[:, u % 2, HD:NH * VW:VW]))
                        on = ON[:, :].rearrange("p (x g d) -> p x g d", g=NG, d=HD)
                        STT(on[:, :, 2 * gp:2 * gp + 2, :], av[:, :, :, 0:HD], att_scale,
                            rec.rearrange("p (x g) -> p x g", g=2).unsqueeze(3).broadcast_to([P, 2 * BT, 2, HD]),
                            ALU.mult, ALU.mult).then_inc(sem("normed"), 1)
                        if gp == 1:
                            dve.wait_ge(sem("normed"), NU * l + u + 1)
                            v.transpose(OA[:, tp * 2 * P:(tp + 1) * 2 * P], ON[:, :]).then_inc(sem("oT"), 1)
                    if s in (NU // 2 + 3, NU + 2):
                        residual(0 if s < NU else 1)

            def residual0(hf):
                dve.wait_ge(sem("proj"), hf + 1)
                STT(half(XB, hf), bank(2 + hf), BP[:, 0:1], half(XA, hf), ALU.add, ALU.add).then_inc(sem("h1"), 1)

            dve.wait_ge(sem("ld_x"), 16)
            attention(0, 1.0 / math.sqrt(D), residual0)
            for hf in range(2):
                centred_times(1, hf)
                then(TT(bview(half(T_, hf)), bview(half(T_, hf)), bb(GG, hf), ALU.mult))
                then(TT(bview(half(T_, hf)), bview(half(T_, hf)), bb(GB, hf), ALU.add))
                TT(half(XB, hf), half(XB, hf), half(T_, hf), ALU.add).then_inc(sem("x_done"), 1)
            if layers >= 2:
                mk = bmask.unsqueeze(2).broadcast_to([P, BH, N])
                for hf in range(2):
                    dve.wait_ge(sem("y1"), hf + 1)
                    TT(bview(half(T_, hf)), bview(bank(4 + 2 * hf)), mk, ALU.mult).then_inc(sem("y1m"), 1)
                    dve.wait_ge(sem("y3"), hf + 1)
                    TT(bview(half(T_, hf)), bview(bank(4 + 2 * hf)), mk, ALU.mult).then_inc(sem("y3m"), 1)
                    dve.wait_ge(sem("y4"), hf + 1)
                    TT(half(XA, hf), bank(5 + 2 * hf), half(XB, hf), ALU.add).then_inc(sem("x_done"), 1)
            if layers >= 3:
                FLOOR = EPS_N * EPS_N

                def floor_norm(k, hf):
                    dve.wait_ge(sem("meansq"), 2 * k + hf + 1)
                    TS(half(RS, hf), bank(NORM_BANKS[(k, hf)][1]), FLOOR / D, None, ALU.max).then_inc(sem("floored"), 1)

                def modulate(k, hf, x, scale, shift):
                    dve.wait_ge(sem("rstd"), 2 * k + hf + 1)
                    then(TT(half(HN, hf), half(x, hf), half(RS, hf), ALU.mult))
                    then(TT(bview(half(HN, hf)), bview(half(HN, hf)), bb(ADA6[:, scale, :], hf), ALU.mult))
                    TT(bview(half(HN, hf)), bview(half(HN, hf)), bb(ADA6[:, shift, :], hf), ALU.add).then_inc(sem("hn"), 1)

                for hf in range(2):
                    floor_norm(2, hf)
                for hf in range(2):
                    modulate(2, hf, XA, 1, 0)
                for i in range(4):
                    hf, s = i // 2, i % 2
                    dve.wait_ge(sem("qk_ms"), i + 1)
                    if s == 0:
                        TS(half(RS, hf), bank(hf), FLOOR / HD, None, ALU.max).then_inc(sem("qk_floor"), 1)
                    else:
                        TS(half(SQ, hf), bank(2 + hf), FLOOR / HD, None, ALU.max).then_inc(sem("qk_floor"), 1)
                for hf in range(2):
                    dve.wait_ge(sem("qk_rs"), 2 * hf + 1)
                    TT(half(QT, hf), half(QT, hf), half(RS, hf), ALU.mult).then_inc(sem("q_sb"), 1)
                    dve.wait_ge(sem("qk_rs"), 2 * hf + 2)
                    then(STT(half(SQ, hf), bank(6 + hf), vcol("l2_bk"), half(SQ, hf), ALU.add, ALU.mult))
                    for h in range(4):
                        TS(half(KBD[:, h, :], hf), half(SQ, hf), KM[:, 4 + h:5 + h], None, ALU.mult).then_inc(sem("kbd"), 1)

                def residual2(hf):
                    dve.wait_ge(sem("proj"), 2 + hf + 1)
                    then(STT(bview(half(T_, hf)), bview(bank(2 + hf)), BP[:, 1:2], bb(ADA6[:, 2, :], hf), ALU.add, ALU.mult))
                    TT(half(XB, hf), half(XA, hf), half(T_, hf), ALU.add).then_inc(sem("h1"), 1)

                attention(1, 1.0, residual2)
                for hf in range(2):
                    floor_norm(3, hf)
                    modulate(3, hf, XB, 4, 3)
                for hf in range(2):
                    dve.wait_ge(sem("fc2_ps"), hf + 1)
                    then(STT(bview(half(T_, hf)), bview(bank(hf)), vcol("l2_bfc2"), bb(ADA6[:, 5, :], hf), ALU.add, ALU.mult))
                    TT(half(XB, hf), half(XB, hf), half(T_, hf), ALU.add).then_inc(sem("x_done"), 1)
            if layers >= 4:
                dve.wait_ge(sem("ld_w3"), 16)
                for s in range(2):
                    w = W3S[:, P + s * W3:P + (s + 1) * W3].rearrange("p (h d) -> p h d", h=H3)
                    mean = ST[:, s * H3:(s + 1) * H3]
                    then(v.tensor_reduce(mean, w, AX_X, ALU.add))
                    then(TS(mean, mean, 1.0 / HD3, None, ALU.mult))
                    TT(w, w, mean.unsqueeze(2).broadcast_to([P, H3, HD3]), ALU.subtract).then_inc(sem("w3c"), 1)
                for hf in range(2):
                    centred_times(4, hf)
                    then(TS(half(T_, hf), half(T_, hf), vcol("l3_ln1g"), None, ALU.mult))
                    TT(bview(half(HN, hf)), bview(half(T_, hf)), bb(SH3, hf), ALU.add).then_inc(sem("hn"), 1)
                st = [ST[:, i * H3:(i + 1) * H3] for i in range(4)]
                dve.wait_ge(sem("w3c"), 2)
                dve.wait_ge(sem("ptb_zero"), 1)

                def summed(s, nm, t):
                    dve.wait_ge(sem(nm + "sq"), t + 1)
                    v.tensor_reduce(st[s], SQ.rearrange("p (h d) -> p h d", h=H3), AX_X, ALU.add).then_inc(sem(nm + "sum"), 1)

                def scaled(s, nm, t):
                    dve.wait_ge(sem(nm + "rs"), t + 1)
                    if t >= 1:
                        dve.wait_ge(sem(nm + "tp"), 2 * t)
                    TT((T_ if s == 0 else RS).rearrange("p (h d) -> p h d", h=H3),
                       PS[:, 2 * s:2 * s + 2, :].rearrange("p k (h d) -> p (k h) d", d=HD3),
                       st[2 + s].unsqueeze(2).broadcast_to([P, H3, HD3]), ALU.mult).then_inc(sem(nm + "n"), 1)

                ex4 = EXB[:, 0, :].rearrange("p (u c n) -> p u c n", u=2, c=C3)
                ex3 = EXB[:, 0, :].rearrange("p (h n) -> p h n", h=H3)
                rec3 = REC[:, 0:H3]

                def shift(t):
                    dve.wait_ge(sem("scores3"), t + 1)
                    sc = PS[:, 6:8, 0:256].rearrange("p u (c n) -> p u c n", c=C3)
                    then(v.tensor_reduce(MX[:, 0:H3], sc, AX_X, ALU.max))
                    TT(ex4, sc, MX[:, 0:H3].rearrange("p (u c) -> p u c", u=2).unsqueeze(3).broadcast_to([P, 2, C3, N]),
                       ALU.subtract).then_inc(sem("shifted3"), 1)

                def normalise(t):
                    then(TT(EXB[:, 1, :].rearrange("p (h n) -> p h n", h=H3), ex3,
                            rec3.unsqueeze(2).broadcast_to([P, H3, N]), ALU.mult))

                def turn_p(t, bs):
                    for b in bs:
                        r = slice(32 * b, 32 * b + 32)
                        m = v.transpose(PTB3[r, t % 2, :, r].rearrange("p (c u) n -> p u c n", u=2),
                                        EXB[r, 1, :].rearrange("p (u c n) -> p u c n", u=2, c=C3))
                    if BT - 1 in bs:
                        m.then_inc(sem("pt3"), 1)

                def resid3(t):
                    dve.wait_ge(sem("out3"), t + 1)
                    TT(XA[:, t * P:(t + 1) * P], PS[:, 7, 256:256 + P], XB[:, t * P:(t + 1) * P], ALU.add).then_inc(sem("x3"), 1)

                def tail(t):
                    dve.wait_ge(sem("tail"), t + 1)
                    v.tensor_copy(LG[:, t * E:(t + 1) * E], PS[:, 6, 256:256 + E])
                    v.tensor_copy(XT[:, t, :], PS[:, 6, 384:512]).then_inc(sem("tail_read"), 1)
                    dve.wait_ge(sem("tail_read"), t + 1)
                    then(v.bn_stats(CN[:, 6 * t:6 * t + 6], XT[:, t, :]))
                    v.bn_aggr(MS[:, 8 + 2 * t:10 + 2 * t], CN[:, 6 * t:6 * t + 6]).then_inc(sem("mv"), 1)

                for t in range(-1, NT + 1):
                    if 0 <= t < NT:
                        shift(t)
                        dve.wait_ge(sem("exped3"), t + 1)
                        then(v.tensor_reduce(rec3, ex3, AX_X, ALU.add))
                        then(v.reciprocal(rec3, rec3))
                    if t + 1 < NT:
                        summed(0, "q3", t + 1)
                    if 0 <= t < NT:
                        if t >= 1:
                            dve.wait_ge(sem("pt3"), t)
                            dve.wait_ge(sem("av3"), 2 * t - 2) if t >= 2 else None
                        normalise(t)
                    if t + 1 < NT:
                        scaled(0, "q3", t + 1)
                    if 0 <= t < NT:
                        turn_p(t, (0, 1))
                    if t + 1 < NT:
                        summed(1, "k3", t + 1)
                    if 0 <= t < NT:
                        turn_p(t, (2, 3))
                    if t + 1 < NT:
                        scaled(1, "k3", t + 1)
                    if t >= 1:
                        resid3(t - 1)
                    if t >= 2:
                        tail(t - 2)
                tail(NT - 1)
                lg = LG[:, :].rearrange("p (t e) -> p t e", e=E)
                g3 = GT[:, :].rearrange("p (t e) -> p t e", e=E)
                dve.wait_ge(sem("mv"), NT)
                then(v.tensor_reduce(MS[:, 0:NT], lg, AX_X, ALU.max))
                TT(g3, lg, MS[:, 0:NT].unsqueeze(2).broadcast_to([P, NT, E]), ALU.subtract).then_inc(sem("g_shift"), 1)
                for i, src in enumerate((ident, iota1, TRI[:, 2 * TE:2 * TE + P])):
                    if i == 2:
                        dve.wait_ge(sem("ld_m"), 96)
                    v.tensor_copy(CB[:, i * P:(i + 1) * P], src).then_inc(sem("cb"), 1)
                dve.wait_ge(sem("g_exp"), 1)
                then(v.tensor_reduce(MS[:, 24:32], g3, AX_X, ALU.add))
                then(v.reciprocal(MS[:, 32:40], MS[:, 24:32]))
                TT(g3, g3, MS[:, 32:40].unsqueeze(2).broadcast_to([P, NT, E]), ALU.mult).then_inc(sem("gate"), 1)
                dve.wait_ge(sem("gate"), 1)
                v.tensor_copy(gx(0), gates(0)).then_inc(sem("gate_x"), 1)
                dve.wait_ge(sem("m_rs"), 1)
                STT(MS[:, 48:56], MS[:, 8:24].rearrange("p (t s) -> p t s", s=2)[:, :, 0], -1.0, MS[:, 40:48],
                    ALU.mult, ALU.mult).then_inc(sem("m_nb"), 1)
                dve.wait_ge(sem("gate_t"), 2)
                ge = GE[:, 0:P]
                then(v.tensor_copy(ge, PS[0:TE, 2, 0:P]))
                thr, cand, dig = CI[:, 0:1], CI[:, 1:2], CI[:, 2:3]
                v.memset(ONE, 1.0)
                then(v.memset(thr, 0))
                then(TT(cand, thr, CU[:, 0:1], ALU.bitwise_or))
                dve.wait_ge(sem("g16"), 1)
                for i in range(DIG):
                    then(TS(JK, G16, cand.bitcast(F32), None, ALU.is_ge, ALU.add, accum_out=CT[:, 0:1]))
                    TS(PRED[:, 0:1], CT[:, 0:1], float(CAP), None, ALU.is_ge).then_inc(sem("pred"), 1)
                    dve.wait_ge(sem("digit"), i + 1)
                    then(TS(dig, PS[:, 3, 0:1], float(1 << (28 - 4 * i)), None, ALU.mult))
                    if i + 1 < DIG:
                        STT(cand, thr, dig, CU[:, i + 1:i + 2], ALU.bitwise_or, ALU.bitwise_or)
                    then(TT(thr, thr, dig, ALU.bitwise_or))
                gt, pg, pq, sl, eq = (GE[:, i * P:(i + 1) * P] for i in (1, 2, 3, 4, 5))
                thf = thr[0:TE, :].bitcast(F32)
                TS(eq, ge, thf, None, ALU.is_equal)
                then(TS(gt, ge, thf, None, ALU.is_gt))
                v.tensor_tensor_scan(pq, ONE, eq, 0.0, ALU.mult, ALU.add).then_inc(sem("prefix"), 1)
                v.tensor_tensor_scan(pg, ONE, gt, 0.0, ALU.mult, ALU.add).then_inc(sem("prefix"), 1)
                dve.wait_ge(sem("offsets"), 1)
                then(v.tensor_copy(CT[0:TE, 4:8], PS[0:TE, 3, 0:4]))
                then(TT(CT[0:TE, 5:6], CT[0:TE, 5:6], CT[0:TE, 6:7], ALU.add))
                STT(gt, pg, CT[0:TE, 4:5], gt, ALU.add, ALU.mult)
                then(STT(eq, pq, CT[0:TE, 5:6], eq, ALU.add, ALU.mult))
                TT(sl, gt, eq, ALU.add).then_inc(sem("slots"), 1)
                dve.wait_ge(sem("slots_t"), 1)
                then(v.tensor_copy(SM[:, :], PS[:, 3, 0:TE]))

                def onehot(e):
                    for t in range(NT):
                        m = TS(OHB[:, t, e, :], CB[:, P:2 * P], SM[:, t * E + e:t * E + e + 1], None, ALU.is_equal)
                    m.then_inc(sem("onehot"), 1)

                onehot(0)
                onehot(1)
                for s in range(E + 1):
                    if s < E:
                        e = s
                        dve.wait_ge(sem("e_fc1"), e + 1)
                        if e >= 2:
                            dve.wait_ge(sem("e_fc2"), e - 1)
                        TT(HS[:, (e % 2) * FF:(e % 2 + 1) * FF].rearrange("p (c n) -> p c n", c=NC),
                           bank(3 + e % 2).rearrange("p (c n) -> p c n", c=NC),
                           B1[:, e * NC:(e + 1) * NC].unsqueeze(2).broadcast_to([P, NC, P]), ALU.add).then_inc(sem("e_b1"), 1)
                        if e + 2 < E:
                            onehot(e + 2)
                    if s >= 1:
                        e = s - 1
                        dve.wait_ge(sem("e_fc2"), e + 1)
                        TT(YF[:, e, :], PS[:, 5, 0:P], B2[:, e * P:(e + 1) * P], ALU.add).then_inc(sem("e_y"), 1)
                        dve.wait_ge(sem("e_y"), e + 1)
                        gate = GR[:, e, P + e:P + e + 1]
                        TS(YS[:, 0, e, :], YF[:, e, :], gate, None, ALU.mult).then_inc(sem("yw"), 1)
                        TS(YR[:, e, :], YF[:, e, :], gate, None, ALU.mult).then_inc(sem("yw"), 1)
                for t in range(NT):
                    dve.wait_ge(sem("scattered"), 2 * (E - 1) + 1 + t // 4)
                    TT(OUT[:, t * P:(t + 1) * P], PS[:, 6 + t // 4, (t % 4) * P:(t % 4 + 1) * P], XT[:, t, :],
                       ALU.add).then_inc(sem("out_tile"), 1)


def _pack(inp):
    f = np.float32
    a = {k: np.asarray(v) for k, v in inp.items()}
    L0 = {k[8:]: v for k, v in a.items() if k.startswith("L0_cond_")}
    L1 = {k[8:]: v for k, v in a.items() if k.startswith("L1_cond_")}
    L2 = {k[8:]: v for k, v in a.items() if k.startswith("L2_cond_")}
    L3 = {k[8:]: v for k, v in a.items() if k.startswith("L3_cond_")}
    ones = np.ones(P, f)

    def rows(w):
        return w.reshape(NG, NG, HD, -1).transpose(1, 0, 2, 3).reshape(w.shape)

    wqkv0 = L0["Wqkv"].reshape(NH * HD, 3, D)
    bqkv0 = L0["bqkv"].reshape(NH * HD, 3)
    feat = lambda b: rows(b.reshape(P, 1)).reshape(P)
    col = {
        "l0_bg": L0["bg"], "l0_bb": L0["bb"], "l0_lng": L0["ln_g"], "l0_lnb": L0["ln_b"],
        "l0_bq": bqkv0[:, 0], "l0_bk": bqkv0[:, 1], "l0_bv": feat(bqkv0[:, 2]), "l0_bp": L0["bp"],
        "l1_lng": L1["ln_g"], "l1_lnb": L1["ln_b"], "l1_b1": L1["b1"],
        "l2_g1": np.broadcast_to(L2["g1"], P), "l2_g2": np.broadcast_to(L2["g2"], P),
        "l2_gq": np.broadcast_to(L2["gq"], P), "l2_gk": np.broadcast_to(L2["gk"], P),
        "l2_bq": L2["bqkv"][0:P], "l2_bk": L2["bqkv"][P:2 * P], "l2_bv": feat(L2["bqkv"][2 * P:3 * P]),
        "l2_bproj": L2["bproj"], "l2_bfc2": L2["bfc2"],
        "l3_bada": L3["b_ada"], "l3_ln1g": L3["ln1_g"], "l3_ln1b": L3["ln1_b"],
        "l3_qg": np.tile(L3["qn_g"], 2), "l3_qb": np.tile(L3["qn_b"], 2),
        "l3_kg": np.tile(L3["kn_g"], 2), "l3_kb": np.tile(L3["kn_b"], 2),
        "l3_mg": L3["mlp_g"], "l3_mb": L3["mlp_b"],
    }
    for c in range(NC):
        col[f"l2_bfc1_{c}"] = L2["bfc1"][c * P:(c + 1) * P]
    for s in range(6):
        col[f"l2_bada_{s}"] = L2["bada"][s * P:(s + 1) * P]
    part = np.arange(P)
    for h in range(4):
        col[f"mask_{h}"] = ((part // HD) % NG == h).astype(f)
    vec = np.stack([col[n] for n in VEC], axis=1)
    eye = np.eye(P, dtype=f)
    j8 = (part[:, None] // HD == part[None, :] // HD).astype(f) / f(HD)
    bm = (part[:, None] // RANK == np.arange(BH)[None, :]).astype(f)
    consts = np.concatenate([eye, eye - f(1 / P), np.full((P, P), 1 / P, f), j8,
                             np.broadcast_to(np.arange(1, P + 1, dtype=f), (P, P)), np.ones((P, P), f), bm], axis=1)
    cond = np.concatenate([a["cond_1024"].T, np.zeros((D, P - B), f)], axis=1)
    w0 = np.concatenate([L0["Wg"].T, L0["Wb"].T, wqkv0[:, 0].T, wqkv0[:, 1].T, wqkv0[:, 2].T, rows(L0["Wp"].T)], axis=1)
    w1 = np.concatenate([L1["W1"], L1["W2"].reshape(P, 4, D, RANK).transpose(0, 1, 3, 2).reshape(P, -1)], axis=1)
    l1b2 = L1["b2"].reshape(4, D, RANK).transpose(1, 0, 2).reshape(P, -1)
    w2 = np.concatenate([L2["Wqkv"].T, rows(L2["Wproj"].T), L2["Wfc1"].T,
                         L2["Wfc2"].T.reshape(NC, P, P).transpose(1, 0, 2).reshape(P, -1), L2["Wada"].T], axis=1)
    w3 = np.concatenate([L3["W_ada"].T, L3["Wqkv"].T,
                         L3["Wout"].T.reshape(C3, P, P).transpose(1, 0, 2).reshape(P, -1), L3["Wgate"].T], axis=1)
    wm1 = L3["fc1s"].transpose(2, 0, 1).reshape(P, -1)
    wm2 = L3["fc2s"].transpose(2, 0, 1).reshape(NC, P, E, P).transpose(1, 2, 0, 3).reshape(P, -1)
    b1s = L3["b1s"].reshape(E, NC, P).transpose(2, 0, 1).reshape(P, -1)
    b2s = L3["b2s"].reshape(-1)
    shift = [28 - 4 * i for i in range(DIG)]
    cands = np.array([[c << shift[i] if i or c < 4 else 7 << 28 for i in range(DIG)] for c in range(NCAND)], np.int32)
    cands = np.repeat(cands, E, axis=0)
    te = np.arange(TE)
    same = te[:, None] % E == te[None, :] % E
    before = same & (te[:, None] // E < te[None, :] // E)
    ce = np.arange(P)
    digit = (ce[:, None] % E == ce[None, :] % E) & (ce[:, None] // E >= 1)
    pad = np.zeros((P - TE, 2 * TE), bool)
    tril = np.concatenate([np.concatenate([np.concatenate([before, same], axis=1), pad]), digit], axis=1).astype(f)
    return {"xT": a["x"].reshape(TOK, D).T, "condT": cond, "vec": vec, "w0": w0, "consts": consts, "w1": w1,
            "w2": w2, "w3": w3, "wm1": wm1, "wm2": wm2, "b1s": b1s, "b2s": b2s, "l1b2": l1b2,
            "cands": cands, "tril": tril}


def kernel(**inputs):
    import concourse.bacc as _bacc
    from concourse.bass_utils import run_bass_kernel_spmd as _run

    nc = _bacc.Bacc("TRN2", target_bir_lowering=False, num_devices=1)
    arrays, args = {}, []
    for name, a in _pack(inputs).items():
        a = np.ascontiguousarray(a)
        arrays[f"in_{name}"] = a
        args.append(nc.dram_tensor(f"in_{name}", a.shape, mybir.dt.from_np(a.dtype), kind="ExternalInput").ap())
    args.append(nc.dram_tensor("out_0", (TOK, D), F32, kind="ExternalOutput").ap())
    build(nc, *args)
    r = _run(nc, [arrays], core_ids=[0])
    return r.results[0]["out_0"].reshape(B, N, D)
```

```python
import math
from contextlib import ExitStack

import numpy as np

import concourse.bass as bass
from concourse import mybir

F32 = mybir.dt.float32
BF16 = mybir.dt.bfloat16
I32 = mybir.dt.int32
ALU = mybir.AluOpType
ACT = mybir.ActivationFunctionType
AX_X = mybir.AxisListType.X

P = 128
B, N, D = 32, 32, 128
TOK = B * N
HALF = TOK // 2
NT = TOK // P
TH = NT // 2
BT = P // N
BH = B // 2
NH, HD = 16, 8
NG = 4
VW = HD + 1
RANK = 8
FF = 512
NC = FF // P
HA = 6
FILL = 3
BETWEEN = 9
STEPS0 = BETWEEN + 1
STEPS2 = 7
H3, HD3 = 16, 64
C3 = H3 * HD3 // P
W3 = H3 * HD3
E = 8
CAP = TOK // E
TE = NT * E
EPS = 1e-5
EPS_N = 1e-12
LN_SCALE = 2.0 ** 24
DIG = 8
NCAND = P // E
XW = D + E

VEC = ["l0_bg", "l0_bb", "l0_lng", "l0_lnb", "l0_bq", "l0_bk", "l0_bv", "l0_bp",
       "l1_lng", "l1_lnb", "l1_b1",
       "l2_g1", "l2_g2", "l2_gq", "l2_gk", "l2_bq", "l2_bk", "l2_bv", "l2_bproj", "l2_bfc2",
       "l2_bfc1_0", "l2_bfc1_1", "l2_bfc1_2", "l2_bfc1_3",
       "l2_bada_0", "l2_bada_1", "l2_bada_2", "l2_bada_3", "l2_bada_4", "l2_bada_5",
       "l3_bada", "l3_ln1g", "l3_ln1b", "l3_qg", "l3_qb", "l3_kg", "l3_kb", "l3_mg", "l3_mb"]
VCOL = {n: i for i, n in enumerate(VEC)}
NV = len(VEC)


def build(nc, xT, condT, vec, w0, consts, w1, w2, w3, wm1, wm2, b1s, b2s, l1b2, cands, tril, out):
    ctx = ExitStack()
    with ctx:
        def sb(name, cols, dt=F32, parts=P):
            return ctx.enter_context(nc.sbuf_tensor(name, [parts, cols], dt))

        sems = {}

        def sem(name):
            if name not in sems:
                sems[name] = ctx.enter_context(nc.semaphore(name))
            return sems[name]

        PS = ctx.enter_context(nc.psum_tensor("PS", [P, 8, 512], F32))

        XA = sb("XA", TOK)
        XB = sb("XB", TOK)
        CD = sb("CD", P)
        V = sb("V", NV)
        W0 = sb("W0", 6 * P)
        CO = sb("CO", 5 * P + BH + NH)
        W1 = sb("W1", P + 4 * RANK * P)
        W1B = sb("W1B", 4 * RANK)
        W2 = sb("W2", 3 * P + P + FF + FF + 6 * P)
        W3S = sb("W3S", P + 3 * W3 + W3 + E)
        FC1 = W1[:, P:P + E * FF]
        FC2 = sb("FC2", E * FF)
        B1 = sb("B1", E * NC)
        B2 = sb("B2", E * P)
        CU = sb("CU", DIG, I32)
        TRI = sb("TRI", 2 * TE + P)

        ident = CO[:, 0:P]
        centre = CO[:, P:2 * P]
        mean_m = CO[:, 2 * P:3 * P]
        mean8 = CO[:, 3 * P:4 * P]
        iota1 = CO[:, 4 * P:5 * P]
        bmask = CO[:, 5 * P:5 * P + BH]
        hmask = CO[:, 5 * P + BH:5 * P + BH + NH]

        def vcol(name, a=0, b=P):
            return V[a:b, VCOL[name]:VCOL[name] + 1]

        WK = sb("WK", 4 * TOK)
        T_, SQ, RS, HN = (WK[:, i * TOK:(i + 1) * TOK] for i in range(4))
        QT = sb("QT", TOK)
        AR1 = sb("AR1", 8 * TOK)
        AR2 = sb("AR2", 8 * TOK)
        KBD = AR1[:, 0:2 * NH * P].rearrange("p (b h n) -> p b h n", b=2, h=NH)
        HID = AR1[:, 4 * TOK:8 * TOK].rearrange("p (c n) -> p c n", c=NC)
        QK3 = AR1[:, 4 * TOK:8 * TOK].rearrange("p (b s c n) -> p b s c n", b=2, s=2, c=C3)
        VBD = AR2[:, 0:NT * NH * BT * VW].rearrange("p (t h b d) -> p t h b d", t=NT, h=NH, b=BT)
        V3 = AR2[:, 5 * TOK:5 * TOK + 3 * W3].rearrange("p (b n) -> p b n", b=3)
        PTB = sb("PTB", 2 * H3 * P)
        PTB3 = PTB[:, :].rearrange("p (b h n) -> p b h n", b=2, h=H3)
        EX = sb("EX", 2 * 512)
        EXB = EX[:, :].rearrange("p (b n) -> p b n", b=2)
        PT = sb("PT", 2 * 512)
        PTt = PT[:, :].rearrange("p (b n) -> p b n", b=2)
        MX = sb("MX", 2 * NH)
        REC = sb("REC", 2 * NH)
        ON = sb("ON", P)
        OA = sb("OA", TOK)
        O3 = OA[:, :].rearrange("p (c n) -> p c n", c=C3)
        ST = sb("ST", 4 * 2 * H3)
        EPSC = sb("EPSC", 4)

        CN = sb("CN", 6 * P)
        HC = sb("HC", P)
        GG = sb("GG", B)
        GB = sb("GB", B)
        GM = sb("GM", B)
        AW = sb("AW", 4 * B * RANK)
        AW4 = AW[:, :].rearrange("p (w b r) -> p w b r", w=4, b=B)
        BTT = sb("BTT", 4 * P)
        SC = sb("SC", P)
        ADA = sb("ADA", 6 * B)
        ADA6 = ADA[:, :].rearrange("p (s b) -> p s b", s=6)
        SH3 = sb("SH3", B)
        BP = sb("BP", 4)
        WPC = sb("WPC", P)
        KM = sb("KM", 1)

        SQ3 = AR1[:, 0:TOK], AR1[:, TOK:2 * TOK]
        QK3N = AR1[:, 2 * TOK:3 * TOK], AR1[:, 3 * TOK:4 * TOK]
        XT = PT[:, :].rearrange("p (t d) -> p t d", t=NT)
        XN = HN.rearrange("p (t d) -> p t d", t=NT)
        RX = T_.rearrange("p (t d) -> p t d", t=NT)
        HS = EX[:, :]
        GT = sb("GT", TE)
        LG = sb("LG", TE)
        G16 = PTB[:, 0:TOK]
        JK = PTB[:, TOK:TOK + TOK // 2].bitcast(BF16)
        GE = QT[0:TE, 0:6 * P]
        ONE = QT[0:TE, 6 * P:7 * P]
        SM = sb("SM", TE)
        CT = sb("CT", 8)
        CI = sb("CI", 4, I32)
        MS = sb("MS", 80)
        PRED = sb("PRED", 2, BF16)
        CB = sb("CB", 3 * P, BF16)
        OHB = AR1[:, 0:4 * TOK].bitcast(BF16).rearrange("p (t e n) -> p t e n", t=NT, e=E)
        OTB = AR2[:, 0:4 * TOK].bitcast(BF16).rearrange("p (e t n) -> p e t n", e=E, t=NT)
        XS = AR1[:, 4 * TOK:4 * TOK + 3 * NT * XW // 2].bitcast(BF16).rearrange("p (w t n) -> p w t n", w=3, t=NT)
        GR = AR1[:, 6 * TOK:6 * TOK + E * XW].rearrange("p (e n) -> p e n", e=E)
        YS = AR2[:, 4 * TOK:4 * TOK + 3 * TOK // 2].bitcast(BF16).rearrange("p (w e n) -> p w e n", w=3, e=E)
        YF = RS.rearrange("p (e n) -> p e n", e=E)
        YR = SQ.rearrange("p (e n) -> p e n", e=E)
        XG = OA[:, :]

        def gates(hf):
            return GT[:, hf * TH * E:(hf + 1) * TH * E].rearrange("p (t e) -> p t e", e=E).unsqueeze(2).broadcast_to([P, TH, NCAND, E])

        def gx(hf):
            return RS[:, hf * HALF:(hf + 1) * HALF].rearrange("p (t c e) -> p t c e", c=NCAND, e=E)

        OUT = XB[:, :]

        def half(ap, hf):
            return ap[:, hf * HALF:(hf + 1) * HALF]

        def bview(ap):
            return ap.rearrange("p (b n) -> p b n", b=BH)

        def bb(ap, hf):
            return ap[:, hf * BH:(hf + 1) * BH].unsqueeze(2).broadcast_to([P, BH, N])

        def bank(i):
            return PS[:, i, :]

        def tail_banks(a, hf):
            return [(bank(0), bank(1)), (bank(2), bank(3)), (bank(6), bank(7))][hf * (1 + a)]

        def ms_bank(k, hf):
            return bank(2 + hf) if k == 0 else tail_banks(k // 3, hf)[k == 3]

        def centred_bank(k, hf):
            return bank(hf) if k == 0 else tail_banks(k // 3, hf)[1]

        def av_out(n):
            return PS[:, 6 + n % 2, 0:BT * NG * VW].rearrange("p (b g d) -> p b g d", b=BT, g=NG)

        ATT_START = (0, TH + FILL + BETWEEN)
        TAIL_START = tuple(a + TH + FILL for a in ATT_START)
        STEPS = TAIL_START[1] + TH + STEPS2
        START3 = STEPS - 5

        def tiles_at(step, lag):
            for a, start in enumerate(ATT_START):
                if 0 <= step - start - lag < NT:
                    return [NT * a + step - start - lag]
            return []

        def tails_at(step):
            r = []
            for a, steps in enumerate((STEPS0, STEPS2)):
                for hf in ((1, 0) if step < TAIL_START[a] + TH + 2 else (0, 1)):
                    j = step - TAIL_START[a] - TH * hf
                    if 0 <= j < steps:
                        r.append((a, hf, j))
            return r

        block = ctx.enter_context(nc.Block())

        @block.sync
        def _(sp):
            sp.dma_start(CD[:, :], condT).then_inc(sem("ld_first"), 16)
            sp.dma_start(V[:, :], vec).then_inc(sem("ld_first"), 16)
            sp.dma_start(CO[:, :], consts).then_inc(sem("ld_first"), 16)
            sp.dma_start(XA[:, :], xT).then_inc(sem("ld_x"), 16)
            sp.dma_start(W0[:, :], w0).then_inc(sem("ld_w0"), 16)
            sp.dma_start(W2[:, :], w2).then_inc(sem("ld_w2"), 16)
            sp.dma_start(W1[:, :], w1).then_inc(sem("ld_w1"), 16)
            sp.dma_start(W1B[:, :], l1b2).then_inc(sem("ld_w1"), 16)
            sp.dma_start(W3S[:, :], w3).then_inc(sem("ld_w3"), 16)
            sp.dma_start(FC2[:, :], wm2).then_inc(sem("ld_m"), 16)
            sp.dma_start(B1[:, :], b1s).then_inc(sem("ld_m"), 16)
            sp.dma_start(B2[:, :], b2s.partition_broadcast(P)).then_inc(sem("ld_m"), 16)
            sp.dma_start(CU[:, :], cands).then_inc(sem("ld_m"), 16)
            sp.dma_start(TRI[:, :], tril).then_inc(sem("ld_m"), 16)
            sp.wait_ge(sem("w_low"), 4)
            sp.dma_start(FC1, wm1).then_inc(sem("ld_m"), 16)
            for t in range(NT):
                sp.wait_ge(sem("out_tile"), t + 1)
                sp.dma_start(out[t * P:(t + 1) * P, :], OUT[:, t * P:(t + 1) * P]).then_inc(sem("stored"), 16)
            sp.wait_ge(sem("stored"), 16 * NT)

        @block.gpsimd
        def _(pool):
            nc.gpsimd.memset(EPSC[:, 0:1], EPS).then_inc(sem("eps_set"), 1)
            nc.gpsimd.memset(EPSC[:, 1:2], 0.5 * math.log(LN_SCALE)).then_inc(sem("eps_set"), 1)
            nc.gpsimd.memset(EPSC[:, 2:3], 0.0).then_inc(sem("eps_set"), 1)
            nc.gpsimd.memset(AR2[:, 0:NT * NH * BT * VW], 0.0).then_inc(sem("vbd_zero"), 1)
            pool.wait_ge(sem("vbd_zero"), 1)
            for b in range(BT):
                nc.gpsimd.memset(VBD[32 * b:32 * b + 32, :, :, b, HD:VW].rearrange("p t h d -> p (t h) d"), 1.0).then_inc(sem("vbd_ones"), 1)
                pool.wait_ge(sem("vbd_ones"), b + 1)
            pool.wait_ge(sem("ld_first"), 48)
            for n in range(2 * NT):
                for hf in range(2):
                    if n == NT:
                        pool.wait_ge(sem("h1"), hf + 1)
                        nc.gpsimd.tensor_tensor(bview(half(HN, hf)), bview(half(XB, hf)), bb(GB, hf), ALU.add).then_inc(sem("h1_shift"), 1)
                hf = n % NT // TH
                pool.wait_ge(sem("k_sb"), 2 * (n // NT) + hf + 1)
                if n >= 2:
                    pool.wait_ge(sem("scores"), n - 1)
                c = n % NT * P
                nc.gpsimd.tensor_tensor(KBD[:, n % 2, HA:NH, :], SQ[:, c:c + P].unsqueeze(1).broadcast_to([P, NH - HA, P]),
                                        hmask[:, HA:NH].unsqueeze(2).broadcast_to([P, NH - HA, P]), ALU.mult).then_inc(sem("kbd_p"), 1)
            nc.gpsimd.memset(PTB[:, :], 0.0).then_inc(sem("ptb_zero"), 1)
            g = nc.gpsimd

            def split(src, rest, parts, tag, n):
                if len(parts) == 3:
                    g.tensor_copy(parts[0], src).then_inc(sem(tag + "_a"), 1)
                    pool.wait_ge(sem(tag + "_a"), n)
                g.tensor_tensor(rest, src, parts[0], ALU.subtract).then_inc(sem(tag + "_b"), 1)
                pool.wait_ge(sem(tag + "_b"), n)
                g.tensor_copy(parts[-2], rest).then_inc(sem(tag + "_c"), 1)
                pool.wait_ge(sem(tag + "_c"), n)
                return g.tensor_tensor(parts[-1], rest, parts[-2], ALU.subtract)

            pool.wait_ge(sem("gate"), 1)
            g3 = GT[:, :].rearrange("p (t e) -> p t e", e=E)
            split(g3, LG[:, :].rearrange("p (t e) -> p t e", e=E), [XS[:, w, :, D:XW] for w in range(3)], "gs", 1).then_inc(sem("xs"), 2)
            pool.wait_ge(sem("xs"), 2)
            pool.wait_ge(sem("xn"), NT)
            split(XN, RX, [XS[:, w, :, 0:D] for w in range(3)], "xsp", 1).then_inc(sem("xs"), 2)
            for e in range(E):
                pool.wait_ge(sem("yw"), 2 * e + 2)
                g.tensor_tensor(YF[:, e, :], YR[:, e, :], YS[:, 0, e, :], ALU.subtract).then_inc(sem("yr"), 1)
                pool.wait_ge(sem("yr"), e + 1)
                g.tensor_copy(YS[:, 1, e, :], YF[:, e, :]).then_inc(sem("ym"), 1)
                pool.wait_ge(sem("ym"), e + 1)
                g.tensor_tensor(YS[:, 2, e, :], YF[:, e, :], YS[:, 1, e, :], ALU.subtract).then_inc(sem("ys"), 1)

        @block.tensor
        def _(pe):
            mm = pe.matmul

            def conditioning():
                pe.wait_ge(sem("ld_first"), 48)
                pe.wait_ge(sem("ld_w0"), 16)
                mm(PS[:, 4, 0:P], W0[:, 0:P], CD[:, :], start=True, stop=True)
                mm(PS[:, 4, P:2 * P], W0[:, P:2 * P], CD[:, :], start=True, stop=True).then_inc(sem("c_gb"), 1)
                mm(PS[:, 5, 0:P], centre, CD[:, :], start=True, stop=True).then_inc(sem("c_cen"), 1)

            def hidden_conditioning():
                pe.wait_ge(sem("c_sq"), 1)
                mm(PS[:, 5, P:2 * P], mean_m, CN[:, 0:P], start=True, stop=True).then_inc(sem("c_var"), 1)
                pe.wait_ge(sem("c_ln"), 1)
                pe.wait_ge(sem("ld_w1"), 32)
                mm(PS[:, 5, 2 * P:3 * P], W1[:, 0:P], CN[:, 4 * P:5 * P], start=True, stop=True).then_inc(sem("c_h"), 1)

            def later_conditioning(s):
                if s == 0:
                    pe.wait_ge(sem("c_silu"), 1)
                    pe.wait_ge(sem("ld_w2"), 16)
                    pe.wait_ge(sem("hn"), 2)
                    for i in range(6):
                        m = mm(PS[:, i // 4, (i % 4) * P:(i % 4 + 1) * P],
                               W2[:, 4 * P + 2 * FF + i * P:4 * P + 2 * FF + (i + 1) * P], SC[:, :], start=True, stop=True)
                        if i == 3:
                            m.then_inc(sem("c_ada"), 1)
                    pe.wait_ge(sem("ld_w3"), 16)
                    mm(PS[:, 1, 2 * P:3 * P], W3S[:, 0:P], SC[:, :], start=True, stop=True)
                    mm(PS[:, 1, 3 * P:3 * P + 1], W0[:, 5 * P:6 * P], vcol("l0_bv"), start=True, stop=True)
                    mm(PS[:, 1, 3 * P + 1:3 * P + 2], W2[:, 3 * P:4 * P], vcol("l2_bv"), start=True, stop=True).then_inc(sem("c_bv"), 1)
                elif s <= 4:
                    w = s - 1
                    pe.wait_ge(sem("c_gelu"), 1)
                    if w < 2:
                        pe.wait_ge(sem("vbd"), 4 * w + 4)
                    else:
                        pe.wait_ge(sem("c_low_free"), 1)
                    for r in range(RANK):
                        c = P + (w * RANK + r) * P
                        m = mm(PS[:, (2, 3, 0, 1)[w], r * B:r * B + P], W1[:, c:c + P], HC[:, :], start=True, stop=True)
                    m.then_inc(sem("w_low"), 1)
                elif s == 5:
                    pe.wait_ge(sem("low_sb"), 4)
                    mm(PS[:, 3, 0:1], centre, BP[:, 0:1], start=True, stop=True).then_inc(sem("c_bc"), 1)
                    for i, w in enumerate((1, 3)):
                        for hf in range(2):
                            m = pe.transpose(PS[:, 2, (2 * i + hf) * P:(2 * i + hf + 1) * P],
                                             AW[:, (w * 2 + hf) * P:(w * 2 + hf + 1) * P], ident)
                    m.then_inc(sem("low_t"), 1)

            def scores(n):
                c = n % NT * P
                pe.wait_ge(sem("q_sb"), n // TH + 1)
                pe.wait_ge(sem("kbd_a"), n + 1)
                pe.wait_ge(sem("kbd_p"), n + 1)
                if n >= 2:
                    pe.wait_ge(sem("shifted"), n - 1)
                for b in range(BT):
                    m = mm(PS[32 * b:32 * b + 32, 4 + n % 2, :], QT[:, c + 32 * b:c + 32 * b + 32],
                           KBD[:, n % 2, :, 32 * b:32 * b + 32], start=True, stop=True)
                m.then_inc(sem("scores"), 1)

            def weighted_values(n):
                pe.wait_ge(sem("pt"), n + 1)
                pe.wait_ge(sem("vbd"), 4 * (n // TH + 1))
                if n >= 2:
                    pe.wait_ge(sem("normed"), n - 1)
                for g in range(NG):
                    for hh in range(NG):
                        h = NG * g + hh
                        m = mm(av_out(n)[32 * hh:32 * hh + 32, :, g, :], PTt[:, n % 2, h * 32:h * 32 + 32],
                               VBD[:, n % NT, h, :, :], start=True, stop=True)
                m.then_inc(sem("av"), 1)

            def tail0(hf, j):
                p, q = tail_banks(0, hf)
                if j == 0:
                    pe.wait_ge(sem("low_tsb"), 2)
                    pe.wait_ge(sem("wpc"), 1)
                    mm(q, centre, half(XA, hf), start=True, stop=False)
                    pe.wait_ge(sem("oT"), TH * (hf + 1))
                    mm(q, WPC[:, :], half(OA, hf), start=False, stop=True).then_inc(sem("centred"), 1)
                    mm(p, W0[:, 5 * P:6 * P], half(OA, hf), start=True, stop=True).then_inc(sem("proj"), 1)
                elif j == 1:
                    pe.wait_ge(sem("h1"), hf + 1)
                    pe.wait_ge(sem("squared"), 2 + hf + 1)
                    mm(p, mean_m, half(SQ, hf), start=True, stop=True).then_inc(sem("meansq"), 1)
                elif j == 2:
                    pe.wait_ge(sem("x_done"), hf + 1)
                    a1 = AW4[:, 0, hf * BH:(hf + 1) * BH, :].rearrange("p b r -> p (b r)")
                    mm(p, a1, half(XB, hf), start=True, stop=True).then_inc(sem("y1"), 1)
                elif j == 3:
                    pe.wait_ge(sem("y1m"), hf + 1)
                    mm(q, BTT[:, hf * P:(hf + 1) * P], half(T_, hf), start=True, stop=True).then_inc(sem("y2"), 1)
                elif j == 4:
                    pe.wait_ge(sem("y2g"), hf + 1)
                    a2 = AW4[:, 2, hf * BH:(hf + 1) * BH, :].rearrange("p b r -> p (b r)")
                    mm(p, a2, half(RS, hf), start=True, stop=True).then_inc(sem("y3"), 1)
                    mm(q, ident, half(XB, hf), start=True, stop=False)
                elif j == 5:
                    pe.wait_ge(sem("y3m"), hf + 1)
                    mm(q, BTT[:, (2 + hf) * P:(3 + hf) * P], half(T_, hf), start=False, stop=True).then_inc(sem("y4"), 1)
                elif j == 6:
                    pe.wait_ge(sem("squared"), 4 + hf + 1)
                    mm(p, mean_m, half(SQ, hf), start=True, stop=True).then_inc(sem("meansq"), 1)
                elif j == 7:
                    pe.wait_ge(sem("hn"), 2 + hf + 1)
                    mm(p, W2[:, 0:P], half(HN, hf), start=True, stop=True).then_inc(sem("q_ps"), 1)
                    mm(q, W2[:, P:2 * P], half(HN, hf), start=True, stop=True).then_inc(sem("k_ps"), 1)
                elif j == 8:
                    pe.wait_ge(sem("qb"), hf + 1)
                    pe.wait_ge(sem("q_sq"), hf + 1)
                    mm(p, mean8, half(SQ, hf), start=True, stop=True).then_inc(sem("q_ms"), 1)
                    pe.wait_ge(sem("kb"), hf + 1)
                    pe.wait_ge(sem("k_sq"), hf + 1)
                    mm(q, mean8, half(XB, hf), start=True, stop=True).then_inc(sem("k_ms"), 1)
                elif j == 9:
                    pe.wait_ge(sem("q_floor"), hf + 1)
                    values(1, hf, W2, 2 * hf)

            def values(a, hf, Wt, b):
                for i in range(TH):
                    t = hf * TH + i
                    m = mm(PS[:, b, i * P:(i + 1) * P], HN[:, t * P:(t + 1) * P], Wt[:, 2 * P:3 * P], start=True, stop=True)
                m.then_inc(sem("v_ps"), 1)

            def tail2(hf, j):
                p, q = tail_banks(1, hf)
                if j == 0:
                    pe.wait_ge(sem("oT"), NT + TH * (hf + 1))
                    mm(p, W2[:, 3 * P:4 * P], half(OA, hf), start=True, stop=True).then_inc(sem("proj"), 1)
                elif j == 1:
                    pe.wait_ge(sem("squared"), 6 + hf + 1)
                    mm(q, mean_m, half(SQ, hf), start=True, stop=True).then_inc(sem("meansq"), 1)
                elif j in (2, 3):
                    pe.wait_ge(sem("hn"), 4 + hf + 1)
                    for c in ((0, 1) if j == 2 else (2, 3)):
                        if c >= 2:
                            pe.wait_ge(sem("hid"), NC * hf + c - 1)
                        mm(p if c % 2 == 0 else q, W2[:, 4 * P + c * P:4 * P + (c + 1) * P], half(HN, hf),
                           start=True, stop=True).then_inc(sem("fc1_ps"), 1)
                elif j == 4:
                    pe.wait_ge(sem("hid"), NC * hf + NC - 1)
                    for c in range(NC):
                        if c == NC - 1:
                            pe.wait_ge(sem("hid"), NC * hf + NC)
                        m = mm(p, W2[:, 4 * P + FF + c * P:4 * P + FF + (c + 1) * P], half(HID[:, c, :], hf),
                               start=(c == 0), stop=(c == NC - 1))
                    m.then_inc(sem("fc2_ps"), 1)
                elif j == 5:
                    pe.wait_ge(sem("x_done"), 2 + hf + 1)
                    mm(q, centre, half(XB, hf), start=True, stop=True).then_inc(sem("centred"), 1)
                elif j == 6:
                    pe.wait_ge(sem("squared"), 8 + hf + 1)
                    mm(p, mean_m, half(SQ, hf), start=True, stop=True).then_inc(sem("meansq"), 1)

            conditioning()
            pe.wait_ge(sem("ld_x"), 16)
            for hf in range(2):
                mm(bank(hf), centre, half(XA, hf), start=True, stop=True).then_inc(sem("centred"), 1)
            for hf in range(2):
                pe.wait_ge(sem("squared"), hf + 1)
                mm(bank(2 + hf), mean_m, half(SQ, hf), start=True, stop=True).then_inc(sem("meansq"), 1)
            hidden_conditioning()
            for hf in range(2):
                pe.wait_ge(sem("hn"), hf + 1)
                if hf == 1:
                    pe.wait_ge(sem("c_gelu"), 1)
                mm(bank(4 + hf), W0[:, 2 * P:3 * P], half(HN, hf), start=True, stop=True).then_inc(sem("q_ps"), 1)
                mm(bank(6 + hf), W0[:, 3 * P:4 * P], half(HN, hf), start=True, stop=True).then_inc(sem("k_ps"), 1)
                values(0, hf, W0[:, 2 * P:5 * P], 2 + hf)

            def early(step):
                for n in tiles_at(step, 0):
                    scores(n)
                for n in tiles_at(step, 2):
                    weighted_values(n)
                later_conditioning(step)
                for a, hf, j in tails_at(step):
                    (tail2 if a else tail0)(hf, j)

            for step in range(START3):
                early(step)
            WQ3 = W3S[:, P:P + W3]
            WK3 = W3S[:, P + W3:P + 2 * W3]
            WV3 = W3S[:, P + 2 * W3:P + 3 * W3]
            WO3 = W3S[:, P + 3 * W3:P + 4 * W3]
            pe.wait_ge(sem("w3c"), 2)

            def queries(t):
                pe.wait_ge(sem("hn"), 6 + (1 if t < TH else 2))
                if t >= 1:
                    pe.wait_ge(sem("q3n"), t)
                for i in range(2):
                    m = mm(bank(i), HN[:, t * P:(t + 1) * P], WQ3[:, i * 512:(i + 1) * 512], start=True, stop=True)
                m.then_inc(sem("q3"), 1)

            def keys(t):
                if t >= 1:
                    pe.wait_ge(sem("k3n"), t)
                for i in range(2):
                    m = mm(bank(2 + i), HN[:, t * P:(t + 1) * P], WK3[:, i * 512:(i + 1) * 512], start=True, stop=True)
                m.then_inc(sem("k3"), 1)

            def values3(t):
                if t >= 1:
                    pe.wait_ge(sem("k3t"), 2 * t)
                for i in range(2):
                    m = mm(bank(4 + i), HN[:, t * P:(t + 1) * P], WV3[:, i * 512:(i + 1) * 512], start=True, stop=True)
                m.then_inc(sem("v3"), 1)

            def turn(t, src, ready, n_ready, free, n_free, done):
                pe.wait_ge(sem(ready), n_ready)
                for k in range(2):
                    pe.wait_ge(sem(free), n_free[k])
                    for c in range(4 * k, 4 * k + 4):
                        m = pe.transpose(PS[:, 4 + k, (c % 4) * P:(c % 4 + 1) * P], src[:, c * P:(c + 1) * P], ident)
                    m.then_inc(sem(done), 1)

            def scores3(t):
                if t == 0:
                    pe.wait_ge(sem("hn"), 8)
                if t >= 2:
                    pe.wait_ge(sem("x3"), t - 1)
                if t >= 3:
                    pe.wait_ge(sem("tail_read"), t - 2)
                for c in range(C3):
                    if c % 4 == 0:
                        pe.wait_ge(sem("k3t"), 2 * t + c // 4 + 1)
                    for u in range(2):
                        for b in range(BT):
                            r = slice(64 * u, 64 * u + 64)
                            n = slice(32 * b, 32 * b + 32)
                            m = mm(PS[32 * b:32 * b + 32, 6 + u, c * 32:c * 32 + 32], QK3[r, t % 2, 0, c, n],
                                   QK3[r, t % 2, 1, c, n], start=True, stop=True)
                m.then_inc(sem("scores3"), 1)

            def av3(t, rnd):
                if rnd == 0:
                    pe.wait_ge(sem("pt3"), t + 1)
                    if t + 1 < NT:
                        pe.wait_ge(sem("shifted3"), t + 2)
                    else:
                        pe.wait_ge(sem("x3"), t)
                        pe.wait_ge(sem("tail_read"), t - 1)
                else:
                    pe.wait_ge(sem("o3"), 2 * t + 1)
                for c in range(4 * rnd, 4 * rnd + 4):
                    for u in range(2):
                        h = 2 * c + u
                        m = mm(PS[64 * u:64 * u + 64, 6 + (c % 4) // 2, 256 + (c % 2) * P:256 + (c % 2 + 1) * P],
                               V3[:, t % 3, h * HD3:(h + 1) * HD3], PTB3[:, t % 2, h, :], start=True, stop=True)
                m.then_inc(sem("av3"), 1)

            def out3(t):
                pe.wait_ge(sem("o3"), 2 * t + 2)
                for c in range(C3):
                    m = mm(PS[:, 7, 256:256 + P], WO3[:, c * P:(c + 1) * P], O3[:, c, :], start=(c == 0), stop=(c == C3 - 1))
                m.then_inc(sem("out3"), 1)

            def tail(t):
                pe.wait_ge(sem("x3"), t + 1)
                mm(PS[:, 6, 256:256 + E], XA[:, t * P:(t + 1) * P], W3S[:, P + 4 * W3:P + 4 * W3 + E], start=True, stop=True)
                pe.transpose(PS[:, 6, 384:512], XA[:, t * P:(t + 1) * P], ident).then_inc(sem("tail"), 1)

            for step in range(START3, STEPS):
                early(step)
                if step == START3:
                    queries(0)
                elif step == START3 + 1:
                    keys(0)
                elif step == START3 + 2:
                    values3(0)
                elif step == START3 + 3:
                    turn(0, QK3N[0], "q3n", 1, "v3s", (1, 1), "q3tp")
                elif step == START3 + 4:
                    turn(0, QK3N[1], "k3n", 1, "q3t", (1, 2), "k3tp")
            queries(1)
            for t in range(NT + 1):
                if t < NT:
                    scores3(t)
                if t + 1 < NT:
                    values3(t + 1)
                    keys(t + 1)
                if t >= 1:
                    av3(t - 1, 0)
                if t + 1 < NT:
                    turn(t + 1, QK3N[0], "q3n", t + 2, "v3s", (t + 2, t + 2), "q3tp")
                if t >= 1:
                    av3(t - 1, 1)
                    out3(t - 1)
                if t + 1 < NT:
                    turn(t + 1, QK3N[1], "k3n", t + 2, "q3t", (2 * t + 3, 2 * t + 4), "k3tp")
                if t >= 2:
                    tail(t - 2)
                if t + 2 < NT:
                    queries(t + 2)
            pe.wait_ge(sem("tail_read"), NT - 1)
            tail(NT - 1)
            pe.wait_ge(sem("gate"), 1)
            for t in range(NT):
                if t % TH == 0:
                    pe.wait_ge(sem("gate_x"), t // TH + 1)
                m = pe.transpose(PS[:, t // 4, (t % 4) * P:(t % 4 + 1) * P], RS[:, t * P:(t + 1) * P], ident)
            m.then_inc(sem("gate_t"), 1)
            pe.transpose(PS[0:TE, 2, 0:P], GT[:, :], ident).then_inc(sem("gate_t"), 1)
            pe.wait_ge(sem("cb"), 3)
            for i in range(DIG):
                pe.wait_ge(sem("pred"), i + 1)
                mm(PS[:, 3, 0:1], CB[:, 2 * P:3 * P], PRED[:, 0:1], start=True, stop=True).then_inc(sem("digit"), 1)
            pe.wait_ge(sem("prefix"), 2)
            ends = GE[:, 3 * P - 1:4 * P:P]
            mm(PS[0:TE, 3, 0:2], TRI[0:TE, 0:TE], ends, start=True, stop=True)
            mm(PS[0:TE, 3, 2:4], TRI[0:TE, TE:2 * TE], ends, start=True, stop=True).then_inc(sem("offsets"), 1)
            pe.wait_ge(sem("slots"), 1)
            pe.transpose(PS[:, 3, 0:TE], GE[:, 4 * P:5 * P], ident[0:TE, 0:TE]).then_inc(sem("slots_t"), 1)
            pe.wait_ge(sem("xs"), 4)
            otp = PS[:, 1, :].bitcast(BF16)
            for s in range(E + 3):
                if s < E:
                    e = s
                    pe.wait_ge(sem("onehot"), e + 1)
                    if e >= 1:
                        pe.wait_ge(sem("gr"), e)
                    for t in range(NT):
                        for w in range(3):
                            m = mm(PS[:, 0, 0:XW], OHB[:, t, e, :], XS[:, w, t, :], start=(t == 0 and w == 0),
                                   stop=(t == NT - 1 and w == 2))
                    m.then_inc(sem("gathered"), 1)
                    if e >= 1:
                        pe.wait_ge(sem("ot"), e)
                    for t in range(NT):
                        m = pe.transpose(otp[:, t * P:(t + 1) * P], OHB[:, t, e, :], CB[:, 0:P])
                    m.then_inc(sem("ot_ps"), 1)
                    pe.wait_ge(sem("gr"), e + 1)
                    if e >= 1:
                        pe.wait_ge(sem("xg"), e)
                    pe.transpose(PS[:, 2, 0:P], GR[:, e, 0:P], ident).then_inc(sem("xgt"), 1)
                if 1 <= s <= E:
                    e = s - 1
                    pe.wait_ge(sem("xg"), e + 1)
                    if e >= 2:
                        pe.wait_ge(sem("e_b1"), e - 1)
                    if e == 0:
                        pe.wait_ge(sem("ld_m"), 96)
                    for c in range(NC):
                        m = mm(PS[:, 3 + e % 2, c * P:(c + 1) * P], FC1[:, e * FF + c * P:e * FF + (c + 1) * P],
                               XG[:, e * P:(e + 1) * P], start=True, stop=True)
                    m.then_inc(sem("e_fc1"), 1)
                if 2 <= s <= E + 1:
                    e = s - 2
                    pe.wait_ge(sem("e_h"), e + 1)
                    if e >= 1:
                        pe.wait_ge(sem("e_y"), e)
                    for c in range(NC):
                        m = mm(PS[:, 5, 0:P], HS[:, (e % 2) * FF + c * P:(e % 2) * FF + (c + 1) * P],
                               FC2[:, e * FF + c * P:e * FF + (c + 1) * P], start=(c == 0), stop=(c == NC - 1))
                    m.then_inc(sem("e_fc2"), 1)
                if s >= 3:
                    e = s - 3
                    pe.wait_ge(sem("ys"), e + 1)
                    if e == 0:
                        pe.wait_ge(sem("tail_read"), NT)
                    for t in range(NT):
                        for w in range(3):
                            m = mm(PS[:, 6 + t // 4, (t % 4) * P:(t % 4 + 1) * P], OTB[:, e, t, :], YS[:, w, e, :],
                                   start=(e == 0 and w == 0 and t % 4 == 0), stop=(e == E - 1 and w == 2),
                                   skip_group_check=True)
                        if t % 4 == 3:
                            m.then_inc(sem("scattered"), 1)

        @block.scalar
        def _(act):
            A = nc.scalar.activation
            eps, half_ln, zero = (EPSC[:, i:i + 1] for i in range(3))

            def rsqrt(out_, in_, w_in, n_in, scale, bias, out_bias, tag, n):
                act.wait_ge(sem(w_in), n_in)
                A(out_, in_, ACT.Ln, bias=bias, scale=scale).then_inc(sem(tag + "_ln"), 1)
                act.wait_ge(sem(tag + "_ln"), n)
                A(out_, out_, ACT.Exp, bias=out_bias, scale=-0.5).then_inc(sem(tag), 1)

            def norm_sq(k, hf):
                act.wait_ge(sem("centred"), {0: 0, 1: 2, 4: 4}[k] + hf + 1)
                A(half(SQ, hf), centred_bank(k, hf), ACT.Square).then_inc(sem("squared"), 1)

            def norm_sq_of(x, hf, w, n_w):
                act.wait_ge(sem(w), n_w)
                A(half(SQ, hf), half(x, hf), ACT.Square).then_inc(sem("squared"), 1)

            def norm_rs(k, hf):
                n = 2 * k + hf + 1
                if k in (2, 3):
                    rsqrt(half(RS, hf), half(RS, hf), "floored", 2 * (k - 2) + hf + 1, LN_SCALE, zero, half_ln, "rstd", n)
                else:
                    rsqrt(half(RS, hf), ms_bank(k, hf), "meansq", n, 1.0, eps, zero, "rstd", n)

            def exp_rows(n):
                act.wait_ge(sem("shifted"), n + 1)
                A(EXB[:, n % 2, :], EXB[:, n % 2, :], ACT.Exp).then_inc(sem("exped"), 1)

            def masked_keys(n):
                act.wait_ge(sem("k_sb"), n // TH + 1)
                if n >= 2:
                    act.wait_ge(sem("scores"), n - 1)
                c = n % NT * P
                for h in range(HA):
                    m = A(KBD[:, n % 2, h, :], SQ[:, c:c + P], ACT.Identity, scale=hmask[:, h:h + 1])
                m.then_inc(sem("kbd_a"), 1)

            def values_out(a, hf, b_):
                act.wait_ge(sem("v_ps"), 2 * a + hf + 1)
                for b in range(BT):
                    r = slice(32 * b, 32 * b + 32)
                    A(VBD[r, hf * TH:(hf + 1) * TH, :, b, 0:HD],
                      PS[r, b_, :].rearrange("p (t h d) -> p t h d", t=TH, h=NH), ACT.Identity).then_inc(sem("vbd"), 1)

            def tail0(hf, j):
                p, q = tail_banks(0, hf)
                if j == 0:
                    act.wait_ge(sem("bias_centred"), 1)
                    act.wait_ge(sem("centred"), 2 + hf + 1)
                    A(half(SQ, hf), q, ACT.Square, bias=BP[:, 2:3]).then_inc(sem("squared"), 1)
                elif j == 1:
                    norm_rs(1, hf)
                elif j == 2:
                    nc.scalar.preload_act_table_set("gelu_and_others")
                elif j == 3:
                    act.wait_ge(sem("y2"), hf + 1)
                    A(half(RS, hf), q, ACT.Gelu).then_inc(sem("y2g"), 1)
                    nc.scalar.preload_act_table_set("natural_log_exp_and_others")
                elif j == 5:
                    act.wait_ge(sem("y4"), hf + 1)
                    A(half(SQ, hf), q, ACT.Square).then_inc(sem("squared"), 1)
                elif j == 6:
                    norm_rs(2, hf)
                elif j == 7:
                    act.wait_ge(sem("q_ps"), 2 + hf + 1)
                    A(half(SQ, hf), p, ACT.Square, bias=vcol("l2_bq")).then_inc(sem("q_sq"), 1)
                    A(half(QT, hf), p, ACT.Identity, bias=vcol("l2_bq")).then_inc(sem("qb"), 1)
                    act.wait_ge(sem("k_ps"), 2 + hf + 1)
                    A(half(XB, hf), q, ACT.Square, bias=vcol("l2_bk")).then_inc(sem("k_sq"), 1)
                    A(half(T_, hf), q, ACT.Identity, bias=vcol("l2_bk")).then_inc(sem("kb"), 1)
                elif j == 8:
                    rsqrt(half(RS, hf), half(RS, hf), "q_floor", hf + 1, LN_SCALE, zero, half_ln, "q_rs", hf + 1)
                    rsqrt(half(XB, hf), half(XB, hf), "k_floor", hf + 1, LN_SCALE, zero, half_ln, "k_rs", hf + 1)
                elif j == 9:
                    values_out(1, hf, 2 * hf)

            def tail2(hf, j):
                p, q = tail_banks(1, hf)
                if j == 0:
                    norm_sq_of(XB, hf, "h1", 2 + hf + 1)
                elif j == 1:
                    norm_rs(3, hf)
                    if hf == 0:
                        nc.scalar.preload_act_table_set("gelu_apprx_tanh_and_others")
                elif j in (2, 3):
                    for c in ((0, 1) if j == 2 else (2, 3)):
                        act.wait_ge(sem("fc1_ps"), NC * hf + c + 1)
                        A(half(HID[:, c, :], hf), p if c % 2 == 0 else q, ACT.Gelu_apprx_tanh,
                          bias=vcol(f"l2_bfc1_{c}")).then_inc(sem("hid"), 1)
                    if j == 3:
                        nc.scalar.preload_act_table_set("natural_log_exp_and_others")
                elif j == 5:
                    norm_sq(4, hf)
                elif j == 6:
                    norm_rs(4, hf)

            nc.scalar.preload_act_table_set("natural_log_exp_and_others")
            act.wait_ge(sem("ld_first"), 48)
            act.wait_ge(sem("eps_set"), 3)
            act.wait_ge(sem("c_cen"), 1)
            A(CN[:, 0:P], PS[:, 5, 0:P], ACT.Square).then_inc(sem("c_sq"), 1)
            A(CN[:, 5 * P:6 * P], CD[:, :], ACT.Exp, scale=-1.0).then_inc(sem("c_exp"), 1)
            norm_sq(0, 0)
            norm_sq(0, 1)
            rsqrt(CN[:, P:2 * P], PS[:, 5, P:2 * P], "c_var", 1, 1.0, eps, zero, "c_rs", 1)
            norm_rs(0, 0)
            norm_rs(0, 1)
            act.wait_ge(sem("c_h"), 1)
            A(HC[:, :], PS[:, 5, 2 * P:3 * P], ACT.Gelu, bias=vcol("l1_b1")).then_inc(sem("c_gelu"), 1)
            nc.scalar.preload_act_table_set("natural_log_exp_and_others")
            for hf in range(2):
                act.wait_ge(sem("k_ps"), hf + 1)
                A(half(SQ, hf), bank(6 + hf), ACT.Identity, bias=vcol("l0_bk")).then_inc(sem("k_sb"), 1)
                act.wait_ge(sem("q_ps"), hf + 1)
                A(half(QT, hf), bank(4 + hf), ACT.Identity, bias=vcol("l0_bq")).then_inc(sem("q_sb"), 1)
                if hf == 0:
                    masked_keys(0)
            act.wait_ge(sem("vbd_ones"), BT)
            masked_keys(1)

            def early(step):
                for n in tiles_at(step, -1):
                    if n == 1:
                        continue
                    if n < NT or n % TH:
                        masked_keys(n)
                for n in tiles_at(step, 0):
                    exp_rows(n)
                if step < 2:
                    values_out(0, step, 2 + step)
                if step == 5:
                    act.wait_ge(sem("low_t"), 1)
                    for i in range(2):
                        A(BTT[:, i * 256:(i + 1) * 256], PS[:, 2, i * 256:(i + 1) * 256], ACT.Identity).then_inc(sem("low_tsb"), 1)
                for a, hf, j in tails_at(step):
                    (tail2 if a else tail0)(hf, j)
                for n in tiles_at(step, -1):
                    if n >= NT and n % TH == 0:
                        masked_keys(n)

            for step in range(START3):
                early(step)
            st = [ST[:, i * H3:(i + 1) * H3] for i in range(4)]

            def square3(t, s, nm):
                act.wait_ge(sem(nm), t + 1)
                if t >= 1:
                    act.wait_ge(sem(nm + "sum"), t)
                A(SQ3[s].rearrange("p (k n) -> p k n", k=2), PS[:, 2 * s:2 * s + 2, :], ACT.Square).then_inc(sem(nm + "sq"), 1)

            def turned3(t, s, g, b_, nm, ks=(0, 1)):
                for k in ks:
                    act.wait_ge(sem(nm + "p"), 2 * t + k + 1)
                    A(QK3[:, t % 2, s, 4 * k:4 * k + 4, :].rearrange("p c n -> p (c n)"), bank(4 + k),
                      ACT.Identity, bias=vcol(b_), scale=vcol(g)).then_inc(sem(nm), 1)

            def exp3(t):
                act.wait_ge(sem("shifted3"), t + 1)
                A(EXB[:, 0, :], EXB[:, 0, :], ACT.Exp, scale=1.0 / math.sqrt(HD3)).then_inc(sem("exped3"), 1)

            def out3(t, rnd):
                act.wait_ge(sem("av3"), 2 * t + rnd + 1)
                if t >= 1:
                    act.wait_ge(sem("out3"), t)
                A(O3[:, 4 * rnd:4 * rnd + 4, :].rearrange("p (k c) n -> p k (c n)", k=2), PS[:, 6:8, 256:512],
                  ACT.Identity).then_inc(sem("o3"), 1)

            def rs3(t, s, nm):
                rsqrt(st[2 + s], st[s], nm + "sum", t + 1, 1.0 / HD3, eps, zero, nm + "rs", t + 1)

            def values3(t):
                act.wait_ge(sem("v3"), t + 1)
                if t >= 3:
                    act.wait_ge(sem("av3"), 2 * (t - 2))
                A(V3[:, t % 3, :].rearrange("p (k n) -> p k n", k=2), PS[:, 4:6, :], ACT.Identity).then_inc(sem("v3s"), 1)

            for step in range(START3, STEPS):
                early(step)
                if step == START3 + 1:
                    square3(0, 0, "q3")
                elif step == START3 + 2:
                    square3(0, 1, "k3")
                    rs3(0, 0, "q3")
                    values3(0)
                elif step == START3 + 3:
                    rs3(0, 1, "k3")
                    turned3(0, 0, "l3_qg", "l3_qb", "q3t")
                elif step == START3 + 4:
                    turned3(0, 1, "l3_kg", "l3_kb", "k3t")
            for t in range(NT + 1):
                if t + 1 < NT:
                    square3(t + 1, 0, "q3")
                    rs3(t + 1, 0, "q3")
                if t < NT:
                    exp3(t)
                if t + 1 < NT:
                    values3(t + 1)
                if t >= 1:
                    out3(t - 1, 0)
                if t + 1 < NT:
                    square3(t + 1, 1, "k3")
                    turned3(t + 1, 0, "l3_qg", "l3_qb", "q3t", (0,))
                if t >= 1:
                    out3(t - 1, 1)
                if t + 1 < NT:
                    rs3(t + 1, 1, "k3")
                    turned3(t + 1, 0, "l3_qg", "l3_qb", "q3t", (1,))
                    turned3(t + 1, 1, "l3_kg", "l3_kb", "k3t", (0,))
                    turned3(t + 1, 1, "l3_kg", "l3_kb", "k3t", (1,))
            act.wait_ge(sem("g_shift"), 1)
            A(GT[:, :], GT[:, :], ACT.Exp).then_inc(sem("g_exp"), 1)
            rsqrt(MS[:, 40:48], MS[:, 8:24].rearrange("p (t s) -> p t s", s=2)[:, :, 1], "mv", NT, 1.0, eps, zero, "m_rs", 1)
            act.wait_ge(sem("gate"), 1)
            act.wait_ge(sem("gate_x"), 1)
            A(gx(1), gates(1), ACT.Identity).then_inc(sem("gate_x"), 1)
            act.wait_ge(sem("gate_t"), 1)
            A(G16.rearrange("p (k n) -> p k n", k=2), PS[:, 0:2, :], ACT.Identity).then_inc(sem("g16"), 1)
            act.wait_ge(sem("m_nb"), 1)
            for t in range(NT):
                A(XN[:, t, :], XT[:, t, :], ACT.Identity, bias=MS[:, 48 + t:49 + t], scale=MS[:, 40 + t:41 + t]).then_inc(sem("xn"), 1)
            for s in range(E + 1):
                if s < E:
                    e = s
                    act.wait_ge(sem("gathered"), e + 1)
                    A(GR[:, e, :], PS[:, 0, 0:XW], ACT.Identity).then_inc(sem("gr"), 1)
                if s >= 1:
                    e = s - 1
                    act.wait_ge(sem("e_b1"), e + 1)
                    h = HS[:, (e % 2) * FF:(e % 2 + 1) * FF]
                    A(h, h, ACT.Gelu_apprx_tanh).then_inc(sem("e_h"), 1)
                if s < E:
                    e = s
                    act.wait_ge(sem("xgt"), e + 1)
                    A(XG[:, e * P:(e + 1) * P], PS[:, 2, 0:P], ACT.Identity, bias=vcol("l3_mb"),
                      scale=vcol("l3_mg")).then_inc(sem("xg"), 1)
                    act.wait_ge(sem("ot_ps"), e + 1)
                    A(OTB[:, e, :, :].rearrange("p t n -> p (t n)"), PS[:, 1, :].bitcast(BF16), ACT.Identity).then_inc(sem("ot"), 1)

        @block.vector
        def _(dve):
            v = nc.vector
            TT, TS, STT = v.tensor_tensor, v.tensor_scalar, v.scalar_tensor_tensor
            done = [0]

            def then(ins):
                done[0] += 1
                ins.then_inc(sem("dve_step"), 1)
                dve.wait_ge(sem("dve_step"), done[0])

            def centred_times(k, hf):
                dve.wait_ge(sem("rstd"), 2 * k + hf + 1)
                then(TT(half(T_, hf), centred_bank(k, hf), half(RS, hf), ALU.mult))

            dve.wait_ge(sem("ld_first"), 48)
            dve.wait_ge(sem("c_gb"), 1)
            then(TS(GM[:, :], PS[:, 4, 0:B], vcol("l0_bg"), None, ALU.add))
            then(TS(GB[:, :], PS[:, 4, P:P + B], vcol("l0_bb"), None, ALU.add))
            TS(GG[:, :], GM[:, :], vcol("l0_lng"), None, ALU.mult)
            then(STT(GB[:, :], GM[:, :], vcol("l0_lnb"), GB[:, :], ALU.mult, ALU.add))
            then(TT(KM[:, :], vcol("l2_gq"), vcol("l2_gk"), ALU.mult))
            then(TS(KM[:, :], KM[:, :], 1.0 / math.sqrt(HD), None, ALU.mult))
            dve.wait_ge(sem("c_exp"), 1)
            then(TS(CN[:, 5 * P:6 * P], CN[:, 5 * P:6 * P], 1.0, None, ALU.add))
            then(v.reciprocal(CN[:, 5 * P:6 * P], CN[:, 5 * P:6 * P]))
            TT(SC[:, :], CD[:, :], CN[:, 5 * P:6 * P], ALU.mult).then_inc(sem("c_silu"), 1)
            dve.wait_ge(sem("c_rs"), 1)
            then(TT(CN[:, 4 * P:5 * P], PS[:, 5, 0:P], CN[:, P:2 * P], ALU.mult))
            TS(CN[:, 4 * P:5 * P], CN[:, 4 * P:5 * P], vcol("l1_lng"), vcol("l1_lnb"), ALU.mult, ALU.add).then_inc(sem("c_ln"), 1)
            for hf in range(2):
                centred_times(0, hf)
                then(TT(bview(half(T_, hf)), bview(half(T_, hf)), bb(GG, hf), ALU.mult))
                TT(bview(half(HN, hf)), bview(half(T_, hf)), bb(GB, hf), ALU.add).then_inc(sem("hn"), 1)

            def later_conditioning(s):
                if s == 0:
                    dve.wait_ge(sem("c_ada"), 1)
                    bada = V[:, VCOL["l2_bada_0"]:VCOL["l2_bada_0"] + 6]
                    TT(ADA6[:, 0:4, :], PS[:, 0, :].rearrange("p (s b) -> p s b", s=4)[:, :, 0:B],
                       bada[:, 0:4].unsqueeze(2).broadcast_to([P, 4, B]), ALU.add)
                    dve.wait_ge(sem("c_bv"), 1)
                    then(TT(ADA6[:, 4:6, :], PS[:, 1, 0:2 * P].rearrange("p (s b) -> p s b", s=2)[:, :, 0:B],
                            bada[:, 4:6].unsqueeze(2).broadcast_to([P, 2, B]), ALU.add))
                    TS(ADA6[:, 1, :], ADA6[:, 1, :], 1.0, vcol("l2_g1"), ALU.add, ALU.mult)
                    TS(ADA6[:, 4, :], ADA6[:, 4, :], 1.0, vcol("l2_g2"), ALU.add, ALU.mult)
                    TS(SH3[:, :], PS[:, 1, 2 * P:2 * P + B], vcol("l3_bada"), vcol("l3_ln1b"), ALU.add, ALU.add)
                    TS(BP[:, 0:1], PS[:, 1, 3 * P:3 * P + 1], 1.0 / math.sqrt(D), vcol("l0_bp"), ALU.mult, ALU.add)
                    then(TS(BP[:, 1:2], PS[:, 1, 3 * P + 1:3 * P + 2], vcol("l2_bproj"), None, ALU.add))
                    v.memset(CT[:, 0:1], 0.0).then_inc(sem("c_low_free"), 1)
                elif s <= 4:
                    w = s - 1
                    dve.wait_ge(sem("w_low"), w + 1)
                    TT(AW4[:, w, :, :].rearrange("p b r -> p r b"),
                       PS[:, (2, 3, 0, 1)[w], 0:RANK * B].rearrange("p (r b) -> p r b", r=RANK),
                       W1B[:, w * RANK:(w + 1) * RANK].unsqueeze(2).broadcast_to([P, RANK, B]), ALU.add).then_inc(sem("low_sb"), 1)

                elif s == 6:
                    dve.wait_ge(sem("c_bc"), 1)
                    v.tensor_copy(BP[:, 2:3], PS[:, 3, 0:1]).then_inc(sem("bias_centred"), 1)
                    dve.wait_ge(sem("bias_centred"), 1)

            def shift(n):
                dve.wait_ge(sem("scores"), n + 1)
                sc = PS[:, 4 + n % 2, :].rearrange("p (h n) -> p h n", n=N)
                mx = MX[:, (n % 2) * NH:(n % 2 + 1) * NH]
                then(v.tensor_reduce(mx, sc, AX_X, ALU.max))
                TT(EXB[:, n % 2, :].rearrange("p (h n) -> p h n", n=N), sc, mx.unsqueeze(2).broadcast_to([P, NH, N]),
                   ALU.subtract).then_inc(sem("shifted"), 1)

            def turn(n):
                dve.wait_ge(sem("exped"), n + 1)
                if n >= 2:
                    dve.wait_ge(sem("av"), n - 1)
                v.transpose(PTt[:, n % 2, :], EXB[:, n % 2, :]).then_inc(sem("pt"), 1)

            def normalised(n):
                dve.wait_ge(sem("av"), n + 1)
                rec = REC[:, (n % 2) * NH:(n % 2 + 1) * NH].rearrange("p (b g) -> p b g", b=BT)
                then(v.reciprocal(rec, av_out(n)[:, :, :, HD]))
                STT(ON[:, :].rearrange("p (b g d) -> p b g d", b=BT, g=NG), av_out(n)[:, :, :, 0:HD],
                    1.0 if n >= NT else 1.0 / math.sqrt(D), rec.unsqueeze(3).broadcast_to([P, BT, NG, HD]),
                    ALU.mult, ALU.mult).then_inc(sem("normed"), 1)
                dve.wait_ge(sem("normed"), n + 1)
                v.transpose(OA[:, n % NT * P:(n % NT + 1) * P], ON[:, :]).then_inc(sem("oT"), 1)

            FLOOR = EPS_N * EPS_N

            def floor_norm(k, hf):
                dve.wait_ge(sem("meansq"), 2 * k + hf + 1)
                TS(half(RS, hf), ms_bank(k, hf), FLOOR / D, None, ALU.max).then_inc(sem("floored"), 1)

            def scaled_by(hf, x, scale):
                then(TT(bview(half(HN, hf)), bview(half(x, hf)), bb(ADA6[:, scale, :], hf), ALU.mult))

            def modulate(k, hf, shift_):
                dve.wait_ge(sem("rstd"), 2 * k + hf + 1)
                then(TT(half(HN, hf), half(HN, hf), half(RS, hf), ALU.mult))
                TT(bview(half(HN, hf)), bview(half(HN, hf)), bb(ADA6[:, shift_, :], hf), ALU.add).then_inc(sem("hn"), 1)

            mk = bmask.unsqueeze(2).broadcast_to([P, BH, N])

            def tail0_first(hf, j):
                p, q = tail_banks(0, hf)
                if j == 6:
                    floor_norm(2, hf)
                elif j == 8:
                    dve.wait_ge(sem("q_ms"), hf + 1)
                    TS(half(RS, hf), p, FLOOR / HD, None, ALU.max).then_inc(sem("q_floor"), 1)
                    dve.wait_ge(sem("k_ms"), hf + 1)
                    TS(half(XB, hf), q, FLOOR / HD, None, ALU.max).then_inc(sem("k_floor"), 1)

            def tail0(hf, j):
                p, q = tail_banks(0, hf)
                if j == 0:
                    dve.wait_ge(sem("proj"), hf + 1)
                    STT(half(XB, hf), p, BP[:, 0:1], half(XA, hf), ALU.add, ALU.add).then_inc(sem("h1"), 1)
                    dve.wait_ge(sem("squared"), 2 + hf + 1)
                    then(STT(bview(half(T_, hf)), bview(q), BP[:, 2:3], bb(GG, hf), ALU.add, ALU.mult))
                elif j == 1:
                    dve.wait_ge(sem("rstd"), 2 + hf + 1)
                    then(TT(half(T_, hf), half(T_, hf), half(RS, hf), ALU.mult))
                    dve.wait_ge(sem("h1_shift"), hf + 1)
                    TT(half(XB, hf), half(HN, hf), half(T_, hf), ALU.add).then_inc(sem("x_done"), 1)
                elif j == 2:
                    dve.wait_ge(sem("y1"), hf + 1)
                    TT(bview(half(T_, hf)), bview(p), mk, ALU.mult).then_inc(sem("y1m"), 1)
                elif j == 4:
                    dve.wait_ge(sem("y3"), hf + 1)
                    TT(bview(half(T_, hf)), bview(p), mk, ALU.mult).then_inc(sem("y3m"), 1)
                elif j == 5:
                    dve.wait_ge(sem("squared"), 4 + hf + 1)
                    then(v.tensor_copy(half(XA, hf), q))
                    scaled_by(hf, XA, 1)
                elif j == 6:
                    modulate(2, hf, 0)
                elif j == 8:
                    dve.wait_ge(sem("q_rs"), hf + 1)
                    STT(half(QT, hf), half(QT, hf), KM[:, :], half(RS, hf), ALU.mult, ALU.mult).then_inc(sem("q_sb"), 1)
                    dve.wait_ge(sem("k_rs"), hf + 1)
                    TT(half(SQ, hf), half(T_, hf), half(XB, hf), ALU.mult).then_inc(sem("k_sb"), 1)

            def tail2_first(hf, j):
                if j == 1:
                    floor_norm(3, hf)

            def tail2(hf, j):
                p, q = tail_banks(1, hf)
                if j == 0:
                    dve.wait_ge(sem("proj"), 2 + hf + 1)
                    then(STT(bview(half(T_, hf)), bview(p), BP[:, 1:2], bb(ADA6[:, 2, :], hf), ALU.add, ALU.mult))
                    TT(half(XB, hf), half(XA, hf), half(T_, hf), ALU.add).then_inc(sem("h1"), 1)
                    dve.wait_ge(sem("h1"), 2 + hf + 1)
                    scaled_by(hf, XB, 4)
                elif j == 1:
                    modulate(3, hf, 3)
                elif j == 4:
                    dve.wait_ge(sem("fc2_ps"), hf + 1)
                    then(STT(bview(half(T_, hf)), bview(p), vcol("l2_bfc2"), bb(ADA6[:, 5, :], hf), ALU.add, ALU.mult))
                    TT(half(XB, hf), half(XB, hf), half(T_, hf), ALU.add).then_inc(sem("x_done"), 1)
                elif j == 6:
                    centred_times(4, hf)
                    STT(bview(half(HN, hf)), bview(half(T_, hf)), vcol("l3_ln1g"), bb(SH3, hf), ALU.mult, ALU.add).then_inc(sem("hn"), 1)

            def centre_weights3(s):
                dve.wait_ge(sem("ld_w3"), 16)
                w = W3S[:, P + s * W3:P + (s + 1) * W3].rearrange("p (h d) -> p h d", h=H3)
                mean = ST[:, s * H3:(s + 1) * H3]
                then(v.tensor_reduce(mean, w, AX_X, ALU.add))
                then(TS(mean, mean, 1.0 / HD3, None, ALU.mult))
                TT(w, w, mean.unsqueeze(2).broadcast_to([P, H3, HD3]), ALU.subtract).then_inc(sem("w3c"), 1)

            dve.wait_ge(sem("ld_x"), 16)
            then(v.tensor_reduce(BP[:, 3:4], W0[:, 5 * P:6 * P], AX_X, ALU.add))
            then(TS(BP[:, 3:4], BP[:, 3:4], 1.0 / D, None, ALU.mult))
            TS(WPC[:, :], W0[:, 5 * P:6 * P], BP[:, 3:4], None, ALU.subtract).then_inc(sem("wpc"), 1)
            centre_weights3(0)

            def early(step):
                for n in tiles_at(step, 0):
                    shift(n)
                for a, hf, j in tails_at(step):
                    (tail2_first if a else tail0_first)(hf, j)
                for n in tiles_at(step, 1):
                    turn(n)
                for n in tiles_at(step, 3):
                    normalised(n)
                for a, hf, j in tails_at(step):
                    (tail2 if a else tail0)(hf, j)
                later_conditioning(step)
                if step == 1:
                    centre_weights3(1)

            for step in range(START3):
                early(step)
            st = [ST[:, i * H3:(i + 1) * H3] for i in range(4)]

            def summed(s, nm, t):
                dve.wait_ge(sem(nm + "sq"), t + 1)
                v.tensor_reduce(st[s], SQ3[s].rearrange("p (h d) -> p h d", h=H3), AX_X, ALU.add).then_inc(sem(nm + "sum"), 1)

            def scaled(s, nm, t):
                dve.wait_ge(sem(nm + "rs"), t + 1)
                if t >= 1:
                    dve.wait_ge(sem(nm + "tp"), 2 * t)
                TT(QK3N[s].rearrange("p (h d) -> p h d", h=H3),
                   PS[:, 2 * s:2 * s + 2, :].rearrange("p k (h d) -> p (k h) d", d=HD3),
                   st[2 + s].unsqueeze(2).broadcast_to([P, H3, HD3]), ALU.mult).then_inc(sem(nm + "n"), 1)

            ex4 = EXB[:, 0, :].rearrange("p (u c n) -> p u c n", u=2, c=C3)
            ex3 = EXB[:, 0, :].rearrange("p (h n) -> p h n", h=H3)
            rec3 = REC[:, 0:H3]

            def shift3(t):
                dve.wait_ge(sem("scores3"), t + 1)
                sc = PS[:, 6:8, 0:256].rearrange("p u (c n) -> p u c n", c=C3)
                then(v.tensor_reduce(MX[:, 0:H3], sc, AX_X, ALU.max))
                TT(ex4, sc, MX[:, 0:H3].rearrange("p (u c) -> p u c", u=2).unsqueeze(3).broadcast_to([P, 2, C3, N]),
                   ALU.subtract).then_inc(sem("shifted3"), 1)

            def sums3(t):
                dve.wait_ge(sem("exped3"), t + 1)
                then(v.tensor_reduce(rec3, ex3, AX_X, ALU.add))
                then(v.reciprocal(rec3, rec3))

            def normalise(t):
                if t >= 1:
                    dve.wait_ge(sem("pt3"), t)
                then(TT(EXB[:, 1, :].rearrange("p (h n) -> p h n", h=H3), ex3,
                        rec3.unsqueeze(2).broadcast_to([P, H3, N]), ALU.mult))

            def turn_p(t):
                if t >= 2:
                    dve.wait_ge(sem("av3"), 2 * t - 2)
                for b in range(BT):
                    r = slice(32 * b, 32 * b + 32)
                    m = v.transpose(PTB3[r, t % 2, :, r].rearrange("p (c u) n -> p u c n", u=2),
                                    EXB[r, 1, :].rearrange("p (u c n) -> p u c n", u=2, c=C3))
                m.then_inc(sem("pt3"), 1)

            def resid3(t):
                dve.wait_ge(sem("out3"), t + 1)
                TT(XA[:, t * P:(t + 1) * P], PS[:, 7, 256:256 + P], XB[:, t * P:(t + 1) * P], ALU.add).then_inc(sem("x3"), 1)

            def tail(t):
                dve.wait_ge(sem("tail"), t + 1)
                v.tensor_copy(LG[:, t * E:(t + 1) * E], PS[:, 6, 256:256 + E])
                v.tensor_copy(XT[:, t, :], PS[:, 6, 384:512]).then_inc(sem("tail_read"), 1)
                dve.wait_ge(sem("tail_read"), t + 1)
                then(v.bn_stats(CN[:, 6 * t:6 * t + 6], XT[:, t, :]))
                v.bn_aggr(MS[:, 8 + 2 * t:10 + 2 * t], CN[:, 6 * t:6 * t + 6]).then_inc(sem("mv"), 1)

            for step in range(START3, STEPS):
                early(step)
                if step == START3 + 2:
                    summed(0, "q3", 0)
                    scaled(0, "q3", 0)
                elif step == START3 + 3:
                    summed(1, "k3", 0)
                    scaled(1, "k3", 0)
            dve.wait_ge(sem("ptb_zero"), 1)
            for t in range(NT + 1):
                if t < NT:
                    shift3(t)
                if t + 1 < NT:
                    summed(0, "q3", t + 1)
                    scaled(0, "q3", t + 1)
                if t < NT:
                    sums3(t)
                    normalise(t)
                if t + 1 < NT:
                    summed(1, "k3", t + 1)
                    scaled(1, "k3", t + 1)
                if t < NT:
                    turn_p(t)
                if t >= 1:
                    resid3(t - 1)
                if t >= 2:
                    tail(t - 2)
            tail(NT - 1)
            lg = LG[:, :].rearrange("p (t e) -> p t e", e=E)
            g3 = GT[:, :].rearrange("p (t e) -> p t e", e=E)
            dve.wait_ge(sem("mv"), NT)
            then(v.tensor_reduce(MS[:, 0:NT], lg, AX_X, ALU.max))
            TT(g3, lg, MS[:, 0:NT].unsqueeze(2).broadcast_to([P, NT, E]), ALU.subtract).then_inc(sem("g_shift"), 1)
            for i, src in enumerate((ident, iota1, TRI[:, 2 * TE:2 * TE + P])):
                if i == 2:
                    dve.wait_ge(sem("ld_m"), 96)
                v.tensor_copy(CB[:, i * P:(i + 1) * P], src).then_inc(sem("cb"), 1)
            dve.wait_ge(sem("g_exp"), 1)
            then(v.tensor_reduce(MS[:, 24:32], g3, AX_X, ALU.add))
            then(v.reciprocal(MS[:, 32:40], MS[:, 24:32]))
            TT(g3, g3, MS[:, 32:40].unsqueeze(2).broadcast_to([P, NT, E]), ALU.mult).then_inc(sem("gate"), 1)
            dve.wait_ge(sem("gate"), 1)
            v.tensor_copy(gx(0), gates(0)).then_inc(sem("gate_x"), 1)
            dve.wait_ge(sem("m_rs"), 1)
            STT(MS[:, 48:56], MS[:, 8:24].rearrange("p (t s) -> p t s", s=2)[:, :, 0], -1.0, MS[:, 40:48],
                ALU.mult, ALU.mult).then_inc(sem("m_nb"), 1)
            dve.wait_ge(sem("gate_t"), 2)
            ge = GE[:, 0:P]
            then(v.tensor_copy(ge, PS[0:TE, 2, 0:P]))
            thr, cand, dig = CI[:, 0:1], CI[:, 1:2], CI[:, 2:3]
            v.memset(ONE, 1.0)
            then(v.memset(thr, 0))
            then(TT(cand, thr, CU[:, 0:1], ALU.bitwise_or))
            dve.wait_ge(sem("g16"), 1)
            for i in range(DIG):
                then(TS(JK, G16, cand.bitcast(F32), None, ALU.is_ge, ALU.add, accum_out=CT[:, 0:1]))
                TS(PRED[:, 0:1], CT[:, 0:1], float(CAP), None, ALU.is_ge).then_inc(sem("pred"), 1)
                dve.wait_ge(sem("digit"), i + 1)
                then(TS(dig, PS[:, 3, 0:1], float(1 << (28 - 4 * i)), None, ALU.mult))
                if i + 1 < DIG:
                    STT(cand, thr, dig, CU[:, i + 1:i + 2], ALU.bitwise_or, ALU.bitwise_or)
                then(TT(thr, thr, dig, ALU.bitwise_or))
            gt, pg, pq, sl, eq = (GE[:, i * P:(i + 1) * P] for i in (1, 2, 3, 4, 5))
            thf = thr[0:TE, :].bitcast(F32)
            TS(eq, ge, thf, None, ALU.is_equal)
            then(TS(gt, ge, thf, None, ALU.is_gt))
            v.tensor_tensor_scan(pq, ONE, eq, 0.0, ALU.mult, ALU.add).then_inc(sem("prefix"), 1)
            v.tensor_tensor_scan(pg, ONE, gt, 0.0, ALU.mult, ALU.add).then_inc(sem("prefix"), 1)
            dve.wait_ge(sem("offsets"), 1)
            then(v.tensor_copy(CT[0:TE, 4:8], PS[0:TE, 3, 0:4]))
            then(TT(CT[0:TE, 5:6], CT[0:TE, 5:6], CT[0:TE, 6:7], ALU.add))
            STT(gt, pg, CT[0:TE, 4:5], gt, ALU.add, ALU.mult)
            then(STT(eq, pq, CT[0:TE, 5:6], eq, ALU.add, ALU.mult))
            TT(sl, gt, eq, ALU.add).then_inc(sem("slots"), 1)
            dve.wait_ge(sem("slots_t"), 1)
            then(v.tensor_copy(SM[:, :], PS[:, 3, 0:TE]))

            def onehot(e):
                for t in range(NT):
                    m = TS(OHB[:, t, e, :], CB[:, P:2 * P], SM[:, t * E + e:t * E + e + 1], None, ALU.is_equal)
                m.then_inc(sem("onehot"), 1)

            onehot(0)
            onehot(1)
            for s in range(E + 1):
                if s < E:
                    e = s
                    dve.wait_ge(sem("e_fc1"), e + 1)
                    if e >= 2:
                        dve.wait_ge(sem("e_fc2"), e - 1)
                    TT(HS[:, (e % 2) * FF:(e % 2 + 1) * FF].rearrange("p (c n) -> p c n", c=NC),
                       bank(3 + e % 2).rearrange("p (c n) -> p c n", c=NC),
                       B1[:, e * NC:(e + 1) * NC].unsqueeze(2).broadcast_to([P, NC, P]), ALU.add).then_inc(sem("e_b1"), 1)
                    if e + 2 < E:
                        onehot(e + 2)
                if s >= 1:
                    e = s - 1
                    dve.wait_ge(sem("e_fc2"), e + 1)
                    TT(YF[:, e, :], PS[:, 5, 0:P], B2[:, e * P:(e + 1) * P], ALU.add).then_inc(sem("e_y"), 1)
                    dve.wait_ge(sem("e_y"), e + 1)
                    gate = GR[:, e, P + e:P + e + 1]
                    TS(YS[:, 0, e, :], YF[:, e, :], gate, None, ALU.mult).then_inc(sem("yw"), 1)
                    TS(YR[:, e, :], YF[:, e, :], gate, None, ALU.mult).then_inc(sem("yw"), 1)
            for t in range(NT):
                dve.wait_ge(sem("scattered"), 2 * (E - 1) + 1 + t // 4)
                TT(OUT[:, t * P:(t + 1) * P], PS[:, 6 + t // 4, (t % 4) * P:(t % 4 + 1) * P], XT[:, t, :],
                   ALU.add).then_inc(sem("out_tile"), 1)


def _pack(inp):
    f = np.float32
    a = {k: np.asarray(v) for k, v in inp.items()}
    L0 = {k[8:]: v for k, v in a.items() if k.startswith("L0_cond_")}
    L1 = {k[8:]: v for k, v in a.items() if k.startswith("L1_cond_")}
    L2 = {k[8:]: v for k, v in a.items() if k.startswith("L2_cond_")}
    L3 = {k[8:]: v for k, v in a.items() if k.startswith("L3_cond_")}
    ones = np.ones(P, f)

    def rows(w):
        return w.reshape(NG, NG, HD, -1).transpose(1, 0, 2, 3).reshape(w.shape)

    wqkv0 = L0["Wqkv"].reshape(NH * HD, 3, D)
    bqkv0 = L0["bqkv"].reshape(NH * HD, 3)
    feat = lambda b: rows(b.reshape(P, 1)).reshape(P)
    col = {
        "l0_bg": L0["bg"], "l0_bb": L0["bb"], "l0_lng": L0["ln_g"], "l0_lnb": L0["ln_b"],
        "l0_bq": bqkv0[:, 0], "l0_bk": bqkv0[:, 1], "l0_bv": feat(bqkv0[:, 2]), "l0_bp": L0["bp"],
        "l1_lng": L1["ln_g"], "l1_lnb": L1["ln_b"], "l1_b1": L1["b1"],
        "l2_g1": np.broadcast_to(L2["g1"], P), "l2_g2": np.broadcast_to(L2["g2"], P),
        "l2_gq": np.broadcast_to(L2["gq"], P), "l2_gk": np.broadcast_to(L2["gk"], P),
        "l2_bq": L2["bqkv"][0:P], "l2_bk": L2["bqkv"][P:2 * P], "l2_bv": feat(L2["bqkv"][2 * P:3 * P]),
        "l2_bproj": L2["bproj"], "l2_bfc2": L2["bfc2"],
        "l3_bada": L3["b_ada"], "l3_ln1g": L3["ln1_g"], "l3_ln1b": L3["ln1_b"],
        "l3_qg": np.tile(L3["qn_g"], 2), "l3_qb": np.tile(L3["qn_b"], 2),
        "l3_kg": np.tile(L3["kn_g"], 2), "l3_kb": np.tile(L3["kn_b"], 2),
        "l3_mg": L3["mlp_g"], "l3_mb": L3["mlp_b"],
    }
    for c in range(NC):
        col[f"l2_bfc1_{c}"] = L2["bfc1"][c * P:(c + 1) * P]
    for s in range(6):
        col[f"l2_bada_{s}"] = L2["bada"][s * P:(s + 1) * P]
    part = np.arange(P)
    vec = np.stack([col[n] for n in VEC], axis=1)
    eye = np.eye(P, dtype=f)
    j8 = (part[:, None] // HD == part[None, :] // HD).astype(f) / f(HD)
    hm = (part[:, None] // HD == np.arange(NH)[None, :]).astype(f)
    bm = (part[:, None] // RANK == np.arange(BH)[None, :]).astype(f)
    consts = np.concatenate([eye, eye - f(1 / P), np.full((P, P), 1 / P, f), j8,
                             np.broadcast_to(np.arange(1, P + 1, dtype=f), (P, P)), bm, hm], axis=1)
    cond = np.concatenate([a["cond_1024"].T, np.zeros((D, P - B), f)], axis=1)
    w0 = np.concatenate([L0["Wg"].T, L0["Wb"].T, wqkv0[:, 0].T, wqkv0[:, 1].T, wqkv0[:, 2].T, rows(L0["Wp"].T)], axis=1)
    w1 = np.concatenate([L1["W1"], L1["W2"].reshape(P, 4, D, RANK).transpose(0, 1, 3, 2).reshape(P, -1)], axis=1)
    l1b2 = L1["b2"].reshape(4, D, RANK).transpose(1, 0, 2).reshape(P, -1)
    w2 = np.concatenate([L2["Wqkv"].T, rows(L2["Wproj"].T), L2["Wfc1"].T,
                         L2["Wfc2"].T.reshape(NC, P, P).transpose(1, 0, 2).reshape(P, -1), L2["Wada"].T], axis=1)
    w3 = np.concatenate([L3["W_ada"].T, L3["Wqkv"].T,
                         L3["Wout"].T.reshape(C3, P, P).transpose(1, 0, 2).reshape(P, -1), L3["Wgate"].T], axis=1)
    wm1 = L3["fc1s"].transpose(2, 0, 1).reshape(P, -1)
    wm2 = L3["fc2s"].transpose(2, 0, 1).reshape(NC, P, E, P).transpose(1, 2, 0, 3).reshape(P, -1)
    b1s = L3["b1s"].reshape(E, NC, P).transpose(2, 0, 1).reshape(P, -1)
    b2s = L3["b2s"].reshape(-1)
    shift = [28 - 4 * i for i in range(DIG)]
    cands = np.array([[c << shift[i] if i or c < 4 else 7 << 28 for i in range(DIG)] for c in range(NCAND)], np.int32)
    cands = np.repeat(cands, E, axis=0)
    te = np.arange(TE)
    same = te[:, None] % E == te[None, :] % E
    before = same & (te[:, None] // E < te[None, :] // E)
    ce = np.arange(P)
    digit = (ce[:, None] % E == ce[None, :] % E) & (ce[:, None] // E >= 1)
    pad = np.zeros((P - TE, 2 * TE), bool)
    tril = np.concatenate([np.concatenate([np.concatenate([before, same], axis=1), pad]), digit], axis=1).astype(f)
    return {"xT": a["x"].reshape(TOK, D).T, "condT": cond, "vec": vec, "w0": w0, "consts": consts, "w1": w1,
            "w2": w2, "w3": w3, "wm1": wm1, "wm2": wm2, "b1s": b1s, "b2s": b2s, "l1b2": l1b2,
            "cands": cands, "tril": tril}


def kernel(**inputs):
    import concourse.bacc as _bacc
    from concourse.bass_utils import run_bass_kernel_spmd as _run

    nc = _bacc.Bacc("TRN2", target_bir_lowering=False, num_devices=1)
    arrays, args = {}, []
    for name, a in _pack(inputs).items():
        a = np.ascontiguousarray(a)
        arrays[f"in_{name}"] = a
        args.append(nc.dram_tensor(f"in_{name}", a.shape, mybir.dt.from_np(a.dtype), kind="ExternalInput").ap())
    args.append(nc.dram_tensor("out_0", (TOK, D), F32, kind="ExternalOutput").ap())
    build(nc, *args)
    r = _run(nc, [arrays], core_ids=[0])
    return r.results[0]["out_0"].reshape(B, N, D)
```
